# Optimizing a Trainium2 kernel written in Bass

```python
import numpy as np
import jax
import jax.numpy as jnp

def _softmax(x, axis=-1):
    return jax.nn.softmax(x, axis=axis)

def _gelu(x):
    return jax.nn.gelu(x, approximate=True)

def _silu(x):
    return jax.nn.silu(x)

def _sigmoid(x):
    return jax.nn.sigmoid(x)

def _layernorm(x, axis=-1, eps=1e-05):
    m = jnp.mean(x, axis=axis, keepdims=True)
    v = jnp.var(x, axis=axis, keepdims=True)
    return (x - m) / jnp.sqrt(v + eps)

def _scatter_add(tgt, idx, src, axis=0):
    return tgt.at[idx].add(src)

def _segment_sum(src, seg, n):
    return jax.ops.segment_sum(src, seg, n)
kernel_name = 'mk_flamingo_gated_d4_seqx_r8_c490f4'

def setup_inputs(seed: int=0):
    np.random.seed(seed)
    _w = jnp.asarray

    def _rec_inputs():
        import jax
        import jax.numpy as jnp
        _rk = jax.random.key(seed)
        x = 7.22e-05 + 1 * jax.random.normal(jax.random.fold_in(_rk, 1), (4, 256, 128), jnp.float32)
        _lenS = 256 - jax.random.randint(jax.random.fold_in(_rk, 7), (4,), 0, max(1, 256 // 4) + 1, jnp.int32)
        _lenS2 = 256 - jax.random.randint(jax.random.fold_in(_rk, 8), (4,), 0, max(1, 256 // 4) + 1, jnp.int32)
        _ctx_1024P = jax.random.normal(jax.random.fold_in(_rk, 11), (4, 16, 128), jnp.float32)
        _ctx_1024c = jax.random.dirichlet(jax.random.fold_in(_rk, 511), 0.3 * jnp.ones((16,), jnp.float32), (4, 256))
        _ctx_1024t = jnp.einsum('bsk,bkd->bsd', _ctx_1024c, _ctx_1024P)
        _ctx_1024t = _ctx_1024t * jax.lax.rsqrt(jnp.mean(jnp.square(_ctx_1024t)) + 1e-12) * 0.953939
        ctx_1024 = 4.13588e-05 + 0.999923 * (_ctx_1024t + 0.3 * jax.random.normal(jax.random.fold_in(_rk, 611), (4, 256, 128), jnp.float32))
        _g = jax.random.normal(jax.random.fold_in(_rk, 9001), (2, 4), jnp.float32)
        _g = jnp.sign(_g) * jnp.maximum(jnp.abs(_g), 1.0) + (_g == 0) * 1.0
        g_xattn = _g[0]
        g_ffn = _g[1]
        return (x, ctx_1024, g_xattn, g_ffn)
    x, ctx_1024, g_xattn, g_ffn = _rec_inputs()

    def _L0_xattn_setup():
        import jax, jax.numpy as jnp
        import numpy as np
        D_MODEL = 128
        NUM_HEADS = 16
        HEAD_DIM = D_MODEL // NUM_HEADS
        MAX_SEQ = 64

        def rope_tables(seq_len, dim):
            inv_freq = 1.0 / 10000.0 ** (jnp.arange(0, dim, 2, dtype=jnp.float32) / dim)
            t = jnp.arange(seq_len, dtype=jnp.float32)
            freqs = jnp.einsum('i,j->ij', t, inv_freq)
            emb = jnp.concatenate([freqs, freqs], axis=-1)
            return (jnp.cos(emb), jnp.sin(emb))

        def rotate_half(x):
            x1, x2 = jnp.split(x, 2, axis=-1)
            return jnp.concatenate([-x2, x1], axis=-1)
        key = jax.random.key(seed)
        ks = jax.random.split(key, 12)
        B, S, D = (16, 64, D_MODEL)
        s = 1.0 / np.sqrt(D)
        inp = {'query': jax.random.normal(ks[0], (B, S, D), jnp.float32), 'key': jax.random.normal(ks[1], (B, S, D), jnp.float32), 'value': jax.random.normal(ks[2], (B, S, D), jnp.float32), 'Wq': jax.random.normal(ks[3], (D, D), jnp.float32) * s, 'bq': jnp.zeros((D,), jnp.float32), 'Wk': jax.random.normal(ks[4], (D, D), jnp.float32) * s, 'bk': jnp.zeros((D,), jnp.float32), 'Wv': jax.random.normal(ks[5], (D, D), jnp.float32) * s, 'bv': jnp.zeros((D,), jnp.float32), 'Wo': jax.random.normal(ks[6], (D, D), jnp.float32) * s, 'bo': jnp.zeros((D,), jnp.float32)}
        return inp
    _L0_xattn_all = _L0_xattn_setup()
    _L0_xattn_in = {k: v for k, v in _L0_xattn_all.items() if k in ('Wq', 'bq', 'Wk', 'bk', 'Wv', 'bv', 'Wo', 'bo')}
    del _L0_xattn_all

    def _L0_ffn_setup():
        import math
        import jax, jax.numpy as jnp
        import numpy as np
        B, S, H = (4, 256, 128)
        E, K, I = (8, 2, 128)
        NSH = 2
        CF, RSF = (1.25, 1.0)
        key = jax.random.key(seed)
        ks = jax.random.split(key, 8)
        w = lambda k, sh: jax.random.normal(k, sh, dtype=jnp.float32) * 0.02
        return {'hidden_states': jax.random.normal(ks[0], (B, S, H), dtype=jnp.float32), 'gate_w': w(ks[1], (E, H)), 'we_gate': w(ks[2], (E, I, H)), 'we_up': w(ks[3], (E, I, H)), 'we_down': w(ks[4], (E, H, I)), 'ws_gate': w(ks[5], (NSH * I, H)), 'ws_up': w(ks[6], (NSH * I, H)), 'ws_down': w(ks[7], (H, NSH * I))}
    _L0_ffn_all = _L0_ffn_setup()
    _L0_ffn_in = {k: v for k, v in _L0_ffn_all.items() if k in ('gate_w', 'we_gate', 'we_up', 'we_down', 'ws_gate', 'ws_up', 'ws_down')}
    del _L0_ffn_all

    def _L1_xattn_setup():
        import jax, jax.numpy as jnp
        import numpy as np
        DIM = 128
        HEADS = 16
        DIM_HEAD = 64
        FF_MULT = 4
        CTX_DIM = 128
        INNER = HEADS * DIM_HEAD
        FF_INNER = DIM * FF_MULT
        FUSED = INNER + 2 * DIM_HEAD + 2 * FF_INNER
        SCALE = DIM_HEAD ** (-0.5)

        def layer_norm(x, gamma, eps=1e-05):
            mu = jnp.mean(x, axis=-1, keepdims=True)
            var = jnp.var(x, axis=-1, keepdims=True)
            return (x - mu) * jax.lax.rsqrt(var + eps) * gamma

        def swiglu(x):
            a, gate = jnp.split(x, 2, axis=-1)
            return jax.nn.silu(gate) * a

        def parallel_block(x, gamma, W_fused, W_attn_out, W_ff_out):
            B, N, D = x.shape
            h = layer_norm(x, gamma)
            fused = h @ W_fused
            q = fused[..., :INNER]
            k = fused[..., INNER:INNER + DIM_HEAD]
            v = fused[..., INNER + DIM_HEAD:INNER + 2 * DIM_HEAD]
            ff = fused[..., INNER + 2 * DIM_HEAD:]
            q = q.reshape(B, N, HEADS, DIM_HEAD).transpose(0, 2, 1, 3) * SCALE
            sim = jnp.einsum('bhid,bjd->bhij', q, k)
            causal = jnp.triu(jnp.ones((N, N), dtype=bool), k=1)
            neg = -jnp.finfo(sim.dtype).max
            sim = jnp.where(causal, neg, sim)
            sim = sim - jax.lax.stop_gradient(jnp.max(sim, axis=-1, keepdims=True))
            attn = jax.nn.softmax(sim, axis=-1)
            out = jnp.einsum('bhij,bjd->bhid', attn, v)
            out = out.transpose(0, 2, 1, 3).reshape(B, N, INNER)
            return out @ W_attn_out + swiglu(ff) @ W_ff_out

        def cross_attention(x, context, gamma, ctx_gamma, W_q, W_kv, W_out):
            B, N, D = x.shape
            xq = layer_norm(x, gamma)
            c = layer_norm(context, ctx_gamma)
            q = (xq @ W_q).reshape(B, N, HEADS, DIM_HEAD).transpose(0, 2, 1, 3) * SCALE
            kv = c @ W_kv
            k, v = (kv[..., :DIM_HEAD], kv[..., DIM_HEAD:])
            sim = jnp.einsum('bhid,bjd->bhij', q, k)
            attn = jax.nn.softmax(sim, axis=-1)
            out = jnp.einsum('bhij,bjd->bhid', attn, v)
            out = out.transpose(0, 2, 1, 3).reshape(B, N, INNER)
            return out @ W_out
        key = jax.random.key(seed)
        ks = jax.random.split(key, 12)
        w = lambda k, shape: jax.random.normal(k, shape, dtype=jnp.float32) * 0.02
        return {'x': jax.random.normal(ks[0], (4, 128, DIM), dtype=jnp.float32), 'context': jax.random.normal(ks[1], (4, 64, CTX_DIM), dtype=jnp.float32), 'ptb_gamma': jnp.ones((DIM,), dtype=jnp.float32), 'W_fused': w(ks[2], (DIM, FUSED)), 'W_attn_out': w(ks[3], (INNER, DIM)), 'W_ff_out': w(ks[4], (FF_INNER, DIM)), 'ca_gamma': jnp.ones((DIM,), dtype=jnp.float32), 'ca_ctx_gamma': jnp.ones((CTX_DIM,), dtype=jnp.float32), 'W_q': w(ks[5], (DIM, INNER)), 'W_kv': w(ks[6], (CTX_DIM, 2 * DIM_HEAD)), 'W_out': w(ks[7], (INNER, DIM))}
    _L1_xattn_all = _L1_xattn_setup()
    _L1_xattn_in = {k: v for k, v in _L1_xattn_all.items() if k in ('ptb_gamma', 'W_fused', 'W_attn_out', 'W_ff_out', 'ca_gamma', 'ca_ctx_gamma', 'W_q', 'W_kv', 'W_out')}
    del _L1_xattn_all

    def _L1_ffn_setup():
        import jax, jax.numpy as jnp
        import numpy as np
        import math
        D_MODEL = 128
        N_EXPERTS = 16
        D_FF = 512
        CAP_FACTOR = 1.25
        MIN_CAPACITY = 4

        def _capacity(num_tokens, num_experts):
            cap = math.floor(CAP_FACTOR * num_tokens / num_experts)
            cap += cap % 2
            return max(cap, MIN_CAPACITY)

        def _top1_router(gate_logits, capacity):
            s, e = gate_logits.shape
            probs = jax.nn.softmax(gate_logits, axis=-1)
            top1 = jnp.argmax(gate_logits, axis=-1)
            mask = jax.nn.one_hot(top1, e, dtype=jnp.int32)
            ranks = jnp.cumsum(mask, axis=0) - 1
            mask = mask * (ranks < capacity).astype(jnp.int32)
            rank1 = jnp.sum(mask * ranks, axis=-1)
            ranks_oh = jax.nn.one_hot(rank1, capacity, dtype=probs.dtype)
            weight = mask.astype(probs.dtype) * probs
            combine_weights = weight[:, :, None] * ranks_oh[:, None, :]
            sec_mask = combine_weights > 0
            return (combine_weights, sec_mask)
        key = jax.random.key(seed)
        k1, k2, k3, k4 = jax.random.split(key, 4)
        x = jax.random.normal(k1, (4, 256, D_MODEL), dtype=jnp.float32)
        gate_w = jax.random.normal(k2, (N_EXPERTS, D_MODEL), dtype=jnp.float32) * math.sqrt(0.1 / D_MODEL)
        w1 = jax.random.normal(k3, (N_EXPERTS, D_MODEL, D_FF), dtype=jnp.float32) * (1.0 / math.sqrt(D_MODEL))
        w2 = jax.random.normal(k4, (N_EXPERTS, D_FF, D_MODEL), dtype=jnp.float32) * (1.0 / math.sqrt(D_FF))
        return {'x': x, 'gate_w': gate_w, 'w1': w1, 'w2': w2}
    _L1_ffn_all = _L1_ffn_setup()
    _L1_ffn_in = {k: v for k, v in _L1_ffn_all.items() if k in ('gate_w', 'w1', 'w2')}
    del _L1_ffn_all

    def _L2_xattn_setup():
        import jax, jax.numpy as jnp
        import numpy as np
        B, S, E, H = (4, 256, 64, 128)
        key = jax.random.key(seed)
        ks = jax.random.split(key, 8)
        s = 1.0 / np.sqrt(H)
        return {'hidden_states': jax.random.normal(ks[0], (B, S, H), jnp.float32), 'external_embeddings': jax.random.normal(ks[1], (B, E, H), jnp.float32), 'Wq': jax.random.normal(ks[2], (H, H), jnp.float32) * s, 'bq': jax.random.normal(ks[3], (H,), jnp.float32) * 0.02, 'Wk': jax.random.normal(ks[4], (H, H), jnp.float32) * s, 'bk': jax.random.normal(ks[5], (H,), jnp.float32) * 0.02, 'Wv': jax.random.normal(ks[6], (H, H), jnp.float32) * s, 'bv': jax.random.normal(ks[7], (H,), jnp.float32) * 0.02}
    _L2_xattn_all = _L2_xattn_setup()
    _L2_xattn_in = {k: v for k, v in _L2_xattn_all.items() if k in ('Wq', 'bq', 'Wk', 'bk', 'Wv', 'bv')}
    del _L2_xattn_all

    def _L2_ffn_setup():
        import jax, jax.numpy as jnp
        import numpy as np
        BS, SLEN, DIM = (1, 256, 128)
        NUM_EXPERTS, TOP_K = (8, 2)
        HID = 176

        def _masked_grouped_mm(x, w, onehot):
            g = jnp.einsum('tk,gnk->tgn', x, w, preferred_element_type=jnp.float32)
            return jnp.einsum('tgn,tg->tn', g, onehot)

        def moe_forward(x, gate_w, expert_bias, w_up, w_down, shared_w_up, shared_w_down):
            bs, slen, dim = x.shape
            xf = x.reshape(-1, dim)
            scores = jax.nn.sigmoid((xf @ gate_w.T).astype(jnp.float32))
            biased = scores + expert_bias
            _, sel = jax.lax.top_k(biased, TOP_K)
            top_scores = jnp.take_along_axis(scores, sel, axis=-1)
            flat_sel = sel.reshape(-1)
            counts = jnp.bincount(flat_sel, length=NUM_EXPERTS)
            order = jnp.argsort(flat_sel, stable=True)
            scores_sorted = top_scores.reshape(-1)[order]
            token_ids = order // TOP_K
            routed_in = (xf[token_ids] * scores_sorted[:, None]).astype(x.dtype)
            seg = jnp.repeat(jnp.arange(NUM_EXPERTS), counts, total_repeat_length=flat_sel.shape[0])
            onehot = jax.nn.one_hot(seg, NUM_EXPERTS, dtype=jnp.float32)
            h = _masked_grouped_mm(routed_in.astype(jnp.bfloat16), w_up.astype(jnp.bfloat16), onehot)
            h = jnp.square(jax.nn.relu(h.astype(jnp.bfloat16)))
            routed_out = _masked_grouped_mm(h.astype(jnp.bfloat16), w_down.astype(jnp.bfloat16), onehot)
            routed_out = routed_out.astype(jnp.bfloat16).astype(x.dtype)
            hs = jnp.square(jax.nn.relu(xf @ shared_w_up.T))
            shared_out = hs @ shared_w_down.T
            combined = jnp.zeros((flat_sel.shape[0], dim), routed_out.dtype).at[order].set(routed_out)
            out = combined.reshape(-1, TOP_K, dim).sum(axis=1) + shared_out
            return out.reshape(bs, slen, dim)
        key = jax.random.key(seed)
        k = jax.random.split(key, 6)
        s = 0.02
        return {'x': jax.random.normal(k[0], (BS, SLEN, DIM), jnp.float32), 'gate_w': jax.random.normal(k[1], (NUM_EXPERTS, DIM), jnp.float32) * s, 'expert_bias': jnp.zeros((NUM_EXPERTS,), jnp.float32), 'w_up': jax.random.normal(k[2], (NUM_EXPERTS, HID, DIM), jnp.float32) * s, 'w_down': jax.random.normal(k[3], (NUM_EXPERTS, DIM, HID), jnp.float32) * s, 'shared_w_up': jax.random.normal(k[4], (HID, DIM), jnp.float32) * s, 'shared_w_down': jax.random.normal(k[5], (DIM, HID), jnp.float32) * s}
    _L2_ffn_all = _L2_ffn_setup()
    _L2_ffn_in = {k: v for k, v in _L2_ffn_all.items() if k in ('gate_w', 'expert_bias', 'w_up', 'w_down', 'shared_w_up', 'shared_w_down')}
    del _L2_ffn_all

    def _L3_xattn_setup():
        import jax, jax.numpy as jnp
        import numpy as np
        NUM_HEADS = 16
        MAX_REL = 128

        def _relative_ids(q_len, k_len, max_rel):
            rel = jnp.arange(q_len)[:, None] - jnp.arange(k_len)[None, :]
            return jnp.clip(rel, -max_rel, max_rel) + max_rel
        key = jax.random.key(seed)
        ks = jax.random.split(key, 13)
        B, S, H = (2, 256, 128)
        hd = H // NUM_HEADS
        s = 1.0 / np.sqrt(H)
        inp = {'query': jax.random.normal(ks[0], (B, S, H), jnp.float32), 'key': jax.random.normal(ks[1], (B, S, H), jnp.float32), 'value': jax.random.normal(ks[2], (B, S, H), jnp.float32), 'Wq': jax.random.normal(ks[3], (H, H), jnp.float32) * s, 'bq': jnp.zeros((H,), jnp.float32), 'Wk': jax.random.normal(ks[4], (H, H), jnp.float32) * s, 'bk': jnp.zeros((H,), jnp.float32), 'Wv': jax.random.normal(ks[5], (H, H), jnp.float32) * s, 'bv': jnp.zeros((H,), jnp.float32), 'Wo': jax.random.normal(ks[6], (H, H), jnp.float32) * s, 'bo': jnp.zeros((H,), jnp.float32), 'rel_key_table': jax.random.normal(ks[7], (2 * MAX_REL + 1, hd), jnp.float32), 'rel_value_table': jax.random.normal(ks[8], (2 * MAX_REL + 1, hd), jnp.float32)}
        return inp
    _L3_xattn_all = _L3_xattn_setup()
    _L3_xattn_in = {k: v for k, v in _L3_xattn_all.items() if k in ('Wq', 'bq', 'Wk', 'bk', 'Wv', 'bv', 'Wo', 'bo', 'rel_key_table', 'rel_value_table')}
    del _L3_xattn_all

    def _L3_ffn_setup():
        import jax, jax.numpy as jnp
        import numpy as np
        HID = 128
        NH = 16
        NKV = 4
        HD = HID // NH
        E = 8
        TOPK = 2
        FFN = 256
        EPS = 1e-05
        THETA = 10000.0

        def _rmsnorm(x, w):
            var = jnp.mean(x * x, axis=-1, keepdims=True)
            return x * jax.lax.rsqrt(var + EPS) * w

        def _rope_tables(S):
            inv_freq = 1.0 / THETA ** (jnp.arange(0, HD, 2, dtype=jnp.float32) / HD)
            freqs = jnp.arange(S, dtype=jnp.float32)[:, None] * inv_freq[None, :]
            emb = jnp.concatenate([freqs, freqs], axis=-1)
            return (jnp.cos(emb), jnp.sin(emb))

        def _apply_rope(t, cos, sin):
            t1, t2 = jnp.split(t, 2, axis=-1)
            rot = jnp.concatenate([-t2, t1], axis=-1)
            return t * cos[None, :, None, :] + rot * sin[None, :, None, :]
        key = jax.random.key(seed)
        ks = jax.random.split(key, 6)
        B, S = (1, 256)
        x = jax.random.normal(ks[0], (B, S, HID), dtype=jnp.float32)
        wqkv = jax.random.normal(ks[1], ((NH + 2 * NKV) * HD, HID), dtype=jnp.float32) * 0.02
        wo = jax.random.normal(ks[2], (HID, NH * HD), dtype=jnp.float32) * 0.02
        gate_w = jax.random.normal(ks[3], (E, HID), dtype=jnp.float32) * 0.02
        w13 = jax.random.normal(ks[4], (E, 2 * FFN, HID), dtype=jnp.float32) * 0.02
        w2 = jax.random.normal(ks[5], (E, HID, FFN), dtype=jnp.float32) * 0.02
        return {'x': x, 'ln1_w': jnp.ones((HID,), jnp.float32), 'ln2_w': jnp.ones((HID,), jnp.float32), 'wqkv': wqkv, 'wo': wo, 'gate_w': gate_w, 'w13': w13, 'w2': w2}
    _L3_ffn_all = _L3_ffn_setup()
    _L3_ffn_in = {k: v for k, v in _L3_ffn_all.items() if k in ('ln1_w', 'ln2_w', 'wqkv', 'wo', 'gate_w', 'w13', 'w2')}
    del _L3_ffn_all
    return {'x': x, 'ctx_1024': ctx_1024, 'g_xattn': g_xattn, 'g_ffn': g_ffn, 'L0_xattn_Wq': _L0_xattn_in['Wq'], 'L0_xattn_bq': _L0_xattn_in['bq'], 'L0_xattn_Wk': _L0_xattn_in['Wk'], 'L0_xattn_bk': _L0_xattn_in['bk'], 'L0_xattn_Wv': _L0_xattn_in['Wv'], 'L0_xattn_bv': _L0_xattn_in['bv'], 'L0_xattn_Wo': _L0_xattn_in['Wo'], 'L0_xattn_bo': _L0_xattn_in['bo'], 'L0_ffn_gate_w': _L0_ffn_in['gate_w'], 'L0_ffn_we_gate': _L0_ffn_in['we_gate'], 'L0_ffn_we_up': _L0_ffn_in['we_up'], 'L0_ffn_we_down': _L0_ffn_in['we_down'], 'L0_ffn_ws_gate': _L0_ffn_in['ws_gate'], 'L0_ffn_ws_up': _L0_ffn_in['ws_up'], 'L0_ffn_ws_down': _L0_ffn_in['ws_down'], 'L1_xattn_ptb_gamma': _L1_xattn_in['ptb_gamma'], 'L1_xattn_W_fused': _L1_xattn_in['W_fused'], 'L1_xattn_W_attn_out': _L1_xattn_in['W_attn_out'], 'L1_xattn_W_ff_out': _L1_xattn_in['W_ff_out'], 'L1_xattn_ca_gamma': _L1_xattn_in['ca_gamma'], 'L1_xattn_ca_ctx_gamma': _L1_xattn_in['ca_ctx_gamma'], 'L1_xattn_W_q': _L1_xattn_in['W_q'], 'L1_xattn_W_kv': _L1_xattn_in['W_kv'], 'L1_xattn_W_out': _L1_xattn_in['W_out'], 'L1_ffn_gate_w': _L1_ffn_in['gate_w'], 'L1_ffn_w1': _L1_ffn_in['w1'], 'L1_ffn_w2': _L1_ffn_in['w2'], 'L2_xattn_Wq': _L2_xattn_in['Wq'], 'L2_xattn_bq': _L2_xattn_in['bq'], 'L2_xattn_Wk': _L2_xattn_in['Wk'], 'L2_xattn_bk': _L2_xattn_in['bk'], 'L2_xattn_Wv': _L2_xattn_in['Wv'], 'L2_xattn_bv': _L2_xattn_in['bv'], 'L2_ffn_gate_w': _L2_ffn_in['gate_w'], 'L2_ffn_expert_bias': _L2_ffn_in['expert_bias'], 'L2_ffn_w_up': _L2_ffn_in['w_up'], 'L2_ffn_w_down': _L2_ffn_in['w_down'], 'L2_ffn_shared_w_up': _L2_ffn_in['shared_w_up'], 'L2_ffn_shared_w_down': _L2_ffn_in['shared_w_down'], 'L3_xattn_Wq': _L3_xattn_in['Wq'], 'L3_xattn_bq': _L3_xattn_in['bq'], 'L3_xattn_Wk': _L3_xattn_in['Wk'], 'L3_xattn_bk': _L3_xattn_in['bk'], 'L3_xattn_Wv': _L3_xattn_in['Wv'], 'L3_xattn_bv': _L3_xattn_in['bv'], 'L3_xattn_Wo': _L3_xattn_in['Wo'], 'L3_xattn_bo': _L3_xattn_in['bo'], 'L3_xattn_rel_key_table': _L3_xattn_in['rel_key_table'], 'L3_xattn_rel_value_table': _L3_xattn_in['rel_value_table'], 'L3_ffn_ln1_w': _L3_ffn_in['ln1_w'], 'L3_ffn_ln2_w': _L3_ffn_in['ln2_w'], 'L3_ffn_wqkv': _L3_ffn_in['wqkv'], 'L3_ffn_wo': _L3_ffn_in['wo'], 'L3_ffn_gate_w': _L3_ffn_in['gate_w'], 'L3_ffn_w13': _L3_ffn_in['w13'], 'L3_ffn_w2': _L3_ffn_in['w2']}

def reference(x, ctx_1024, g_xattn, g_ffn, L0_xattn_Wq, L0_xattn_bq, L0_xattn_Wk, L0_xattn_bk, L0_xattn_Wv, L0_xattn_bv, L0_xattn_Wo, L0_xattn_bo, L0_ffn_gate_w, L0_ffn_we_gate, L0_ffn_we_up, L0_ffn_we_down, L0_ffn_ws_gate, L0_ffn_ws_up, L0_ffn_ws_down, L1_xattn_ptb_gamma, L1_xattn_W_fused, L1_xattn_W_attn_out, L1_xattn_W_ff_out, L1_xattn_ca_gamma, L1_xattn_ca_ctx_gamma, L1_xattn_W_q, L1_xattn_W_kv, L1_xattn_W_out, L1_ffn_gate_w, L1_ffn_w1, L1_ffn_w2, L2_xattn_Wq, L2_xattn_bq, L2_xattn_Wk, L2_xattn_bk, L2_xattn_Wv, L2_xattn_bv, L2_ffn_gate_w, L2_ffn_expert_bias, L2_ffn_w_up, L2_ffn_w_down, L2_ffn_shared_w_up, L2_ffn_shared_w_down, L3_xattn_Wq, L3_xattn_bq, L3_xattn_Wk, L3_xattn_bk, L3_xattn_Wv, L3_xattn_bv, L3_xattn_Wo, L3_xattn_bo, L3_xattn_rel_key_table, L3_xattn_rel_value_table, L3_ffn_ln1_w, L3_ffn_ln2_w, L3_ffn_wqkv, L3_ffn_wo, L3_ffn_gate_w, L3_ffn_w13, L3_ffn_w2):
    import jax
    import jax.numpy as jnp

    def _L0_xattn_ref(query, key, value, Wq, bq, Wk, bk, Wv, bv, Wo, bo):
        import jax, jax.numpy as jnp
        import numpy as np
        D_MODEL = 128
        NUM_HEADS = 16
        HEAD_DIM = D_MODEL // NUM_HEADS
        MAX_SEQ = 64

        def rope_tables(seq_len, dim):
            inv_freq = 1.0 / 10000.0 ** (jnp.arange(0, dim, 2, dtype=jnp.float32) / dim)
            t = jnp.arange(seq_len, dtype=jnp.float32)
            freqs = jnp.einsum('i,j->ij', t, inv_freq)
            emb = jnp.concatenate([freqs, freqs], axis=-1)
            return (jnp.cos(emb), jnp.sin(emb))

        def rotate_half(x):
            x1, x2 = jnp.split(x, 2, axis=-1)
            return jnp.concatenate([-x2, x1], axis=-1)
        B, S, D = query.shape
        H, Hd = (NUM_HEADS, HEAD_DIM)
        scale = Hd ** (-0.5)

        def proj(x, W, b):
            y = jnp.einsum('bsd,ed->bse', x, W) + b
            return y.reshape(B, S, H, Hd).transpose(0, 2, 1, 3)
        q = proj(query, Wq, bq)
        k = proj(key, Wk, bk)
        v = proj(value, Wv, bv)
        cos, sin = rope_tables(S, Hd)
        cos = cos[None, None]
        sin = sin[None, None]
        q = q * cos + rotate_half(q) * sin
        k = k * cos + rotate_half(k) * sin
        attn = jnp.einsum('bhqd,bhkd->bhqk', q, k) * scale
        attn_w = jax.nn.softmax(attn, axis=-1)
        out = jnp.einsum('bhqk,bhkd->bhqd', attn_w, v)
        out = out.transpose(0, 2, 1, 3).reshape(B, S, D)
        out = jnp.einsum('bsd,ed->bse', out, Wo) + bo
        return out

    def _L0_ffn_ref(hidden_states, gate_w, we_gate, we_up, we_down, ws_gate, ws_up, ws_down):
        import math
        import jax, jax.numpy as jnp
        import numpy as np
        B, S, H = (4, 256, 128)
        E, K, I = (8, 2, 128)
        NSH = 2
        CF, RSF = (1.25, 1.0)
        orig_shape = hidden_states.shape
        x = hidden_states.reshape(-1, H)
        N = x.shape[0]
        logits = x.astype(jnp.float32) @ gate_w.astype(jnp.float32).T
        scores = jax.nn.softmax(logits, axis=-1)
        topk_w, topk_idx = jax.lax.top_k(scores, K)
        topk_w = topk_w / (topk_w.sum(-1, keepdims=True) + 1e-20) * RSF
        capacity = math.ceil(CF * N * K / E)
        flat = topk_idx.reshape(-1)
        one_hot = jax.nn.one_hot(flat, E, dtype=jnp.int32)
        pos = jnp.cumsum(one_hot, axis=0) - 1
        pos_tok = jnp.take_along_axis(pos, flat[:, None], axis=1)[:, 0]
        keep = (pos_tok < capacity).reshape(N, K)
        topk_w = topk_w * keep.astype(topk_w.dtype)
        comb = jnp.zeros((N, E), jnp.float32).at[jnp.arange(N)[:, None], topk_idx].add(topk_w)
        g = jnp.einsum('nh,eih->nei', x, we_gate)
        u = jnp.einsum('nh,eih->nei', x, we_up)
        eo = jnp.einsum('nei,ehi->neh', jax.nn.silu(g) * u, we_down)
        y = jnp.einsum('neh,ne->nh', eo, comb)
        sh = jax.nn.silu(x @ ws_gate.T) * (x @ ws_up.T) @ ws_down.T
        return (y + sh).reshape(orig_shape)

    def _L1_xattn_ref(x, context, ptb_gamma, W_fused, W_attn_out, W_ff_out, ca_gamma, ca_ctx_gamma, W_q, W_kv, W_out):
        import jax, jax.numpy as jnp
        import numpy as np
        DIM = 128
        HEADS = 16
        DIM_HEAD = 64
        FF_MULT = 4
        CTX_DIM = 128
        INNER = HEADS * DIM_HEAD
        FF_INNER = DIM * FF_MULT
        FUSED = INNER + 2 * DIM_HEAD + 2 * FF_INNER
        SCALE = DIM_HEAD ** (-0.5)

        def layer_norm(x, gamma, eps=1e-05):
            mu = jnp.mean(x, axis=-1, keepdims=True)
            var = jnp.var(x, axis=-1, keepdims=True)
            return (x - mu) * jax.lax.rsqrt(var + eps) * gamma

        def swiglu(x):
            a, gate = jnp.split(x, 2, axis=-1)
            return jax.nn.silu(gate) * a

        def parallel_block(x, gamma, W_fused, W_attn_out, W_ff_out):
            B, N, D = x.shape
            h = layer_norm(x, gamma)
            fused = h @ W_fused
            q = fused[..., :INNER]
            k = fused[..., INNER:INNER + DIM_HEAD]
            v = fused[..., INNER + DIM_HEAD:INNER + 2 * DIM_HEAD]
            ff = fused[..., INNER + 2 * DIM_HEAD:]
            q = q.reshape(B, N, HEADS, DIM_HEAD).transpose(0, 2, 1, 3) * SCALE
            sim = jnp.einsum('bhid,bjd->bhij', q, k)
            causal = jnp.triu(jnp.ones((N, N), dtype=bool), k=1)
            neg = -jnp.finfo(sim.dtype).max
            sim = jnp.where(causal, neg, sim)
            sim = sim - jax.lax.stop_gradient(jnp.max(sim, axis=-1, keepdims=True))
            attn = jax.nn.softmax(sim, axis=-1)
            out = jnp.einsum('bhij,bjd->bhid', attn, v)
            out = out.transpose(0, 2, 1, 3).reshape(B, N, INNER)
            return out @ W_attn_out + swiglu(ff) @ W_ff_out

        def cross_attention(x, context, gamma, ctx_gamma, W_q, W_kv, W_out):
            B, N, D = x.shape
            xq = layer_norm(x, gamma)
            c = layer_norm(context, ctx_gamma)
            q = (xq @ W_q).reshape(B, N, HEADS, DIM_HEAD).transpose(0, 2, 1, 3) * SCALE
            kv = c @ W_kv
            k, v = (kv[..., :DIM_HEAD], kv[..., DIM_HEAD:])
            sim = jnp.einsum('bhid,bjd->bhij', q, k)
            attn = jax.nn.softmax(sim, axis=-1)
            out = jnp.einsum('bhij,bjd->bhid', attn, v)
            out = out.transpose(0, 2, 1, 3).reshape(B, N, INNER)
            return out @ W_out
        y = x + parallel_block(x, ptb_gamma, W_fused, W_attn_out, W_ff_out)
        return cross_attention(y, context, ca_gamma, ca_ctx_gamma, W_q, W_kv, W_out)

    def _L1_ffn_ref(x, gate_w, w1, w2):
        import jax, jax.numpy as jnp
        import numpy as np
        import math
        D_MODEL = 128
        N_EXPERTS = 16
        D_FF = 512
        CAP_FACTOR = 1.25
        MIN_CAPACITY = 4

        def _capacity(num_tokens, num_experts):
            cap = math.floor(CAP_FACTOR * num_tokens / num_experts)
            cap += cap % 2
            return max(cap, MIN_CAPACITY)

        def _top1_router(gate_logits, capacity):
            s, e = gate_logits.shape
            probs = jax.nn.softmax(gate_logits, axis=-1)
            top1 = jnp.argmax(gate_logits, axis=-1)
            mask = jax.nn.one_hot(top1, e, dtype=jnp.int32)
            ranks = jnp.cumsum(mask, axis=0) - 1
            mask = mask * (ranks < capacity).astype(jnp.int32)
            rank1 = jnp.sum(mask * ranks, axis=-1)
            ranks_oh = jax.nn.one_hot(rank1, capacity, dtype=probs.dtype)
            weight = mask.astype(probs.dtype) * probs
            combine_weights = weight[:, :, None] * ranks_oh[:, None, :]
            sec_mask = combine_weights > 0
            return (combine_weights, sec_mask)
        tokens = x.reshape(-1, D_MODEL)
        s = tokens.shape[0]
        capacity = _capacity(s, N_EXPERTS)
        gate_logits = tokens.astype(jnp.float32) @ gate_w.T
        combine_weights, sec_mask = _top1_router(gate_logits, capacity)
        dispatch = jnp.einsum('sec,sd->ecd', sec_mask.astype(tokens.dtype), tokens)
        h = jax.nn.gelu(jnp.einsum('ecd,edf->ecf', dispatch, w1))
        expert_out = jnp.einsum('ecf,efd->ecd', h, w2)
        out = jnp.einsum('sec,ecd->sd', combine_weights.astype(tokens.dtype), expert_out)
        return out.reshape(x.shape)

    def _L2_xattn_ref(hidden_states, external_embeddings, Wq, bq, Wk, bk, Wv, bv):
        import jax, jax.numpy as jnp
        import numpy as np
        B, S, E, H = (4, 256, 64, 128)
        q = hidden_states @ Wq + bq
        k_tok = hidden_states @ Wk + bk
        v_tok = hidden_states @ Wv + bv
        k_ext = external_embeddings @ Wk + bk
        v_ext = external_embeddings @ Wv + bv
        s_self = jnp.einsum('bsh,bsh->bs', q, k_tok)[..., None]
        s_ext = jnp.einsum('bsh,beh->bse', q, k_ext)
        scores = jnp.concatenate([s_self, s_ext], axis=-1)
        probs = jax.nn.softmax(scores, axis=-1)
        ctx = probs[..., :1] * v_tok + jnp.einsum('bse,beh->bsh', probs[..., 1:], v_ext)
        return ctx

    def _L2_ffn_ref(x, gate_w, expert_bias, w_up, w_down, shared_w_up, shared_w_down):
        import jax, jax.numpy as jnp
        import numpy as np
        BS, SLEN, DIM = (1, 256, 128)
        NUM_EXPERTS, TOP_K = (8, 2)
        HID = 176

        def _masked_grouped_mm(x, w, onehot):
            g = jnp.einsum('tk,gnk->tgn', x, w, preferred_element_type=jnp.float32)
            return jnp.einsum('tgn,tg->tn', g, onehot)

        def moe_forward(x, gate_w, expert_bias, w_up, w_down, shared_w_up, shared_w_down):
            bs, slen, dim = x.shape
            xf = x.reshape(-1, dim)
            scores = jax.nn.sigmoid((xf @ gate_w.T).astype(jnp.float32))
            biased = scores + expert_bias
            _, sel = jax.lax.top_k(biased, TOP_K)
            top_scores = jnp.take_along_axis(scores, sel, axis=-1)
            flat_sel = sel.reshape(-1)
            counts = jnp.bincount(flat_sel, length=NUM_EXPERTS)
            order = jnp.argsort(flat_sel, stable=True)
            scores_sorted = top_scores.reshape(-1)[order]
            token_ids = order // TOP_K
            routed_in = (xf[token_ids] * scores_sorted[:, None]).astype(x.dtype)
            seg = jnp.repeat(jnp.arange(NUM_EXPERTS), counts, total_repeat_length=flat_sel.shape[0])
            onehot = jax.nn.one_hot(seg, NUM_EXPERTS, dtype=jnp.float32)
            h = _masked_grouped_mm(routed_in.astype(jnp.bfloat16), w_up.astype(jnp.bfloat16), onehot)
            h = jnp.square(jax.nn.relu(h.astype(jnp.bfloat16)))
            routed_out = _masked_grouped_mm(h.astype(jnp.bfloat16), w_down.astype(jnp.bfloat16), onehot)
            routed_out = routed_out.astype(jnp.bfloat16).astype(x.dtype)
            hs = jnp.square(jax.nn.relu(xf @ shared_w_up.T))
            shared_out = hs @ shared_w_down.T
            combined = jnp.zeros((flat_sel.shape[0], dim), routed_out.dtype).at[order].set(routed_out)
            out = combined.reshape(-1, TOP_K, dim).sum(axis=1) + shared_out
            return out.reshape(bs, slen, dim)
        return moe_forward(x, gate_w, expert_bias, w_up, w_down, shared_w_up, shared_w_down)

    def _L3_xattn_ref(query, key, value, Wq, bq, Wk, bk, Wv, bv, Wo, bo, rel_key_table, rel_value_table):
        import jax, jax.numpy as jnp
        import numpy as np
        NUM_HEADS = 16
        MAX_REL = 128

        def _relative_ids(q_len, k_len, max_rel):
            rel = jnp.arange(q_len)[:, None] - jnp.arange(k_len)[None, :]
            return jnp.clip(rel, -max_rel, max_rel) + max_rel
        B, Sq, H = query.shape
        Sk = key.shape[1]
        nh = NUM_HEADS
        hd = H // nh
        q = (query @ Wq + bq).reshape(B, Sq, nh, hd).transpose(0, 2, 1, 3)
        k = (key @ Wk + bk).reshape(B, Sk, nh, hd).transpose(0, 2, 1, 3)
        v = (value @ Wv + bv).reshape(B, Sk, nh, hd).transpose(0, 2, 1, 3)
        scores = jnp.einsum('bhqd,bhkd->bhqk', q, k)
        ids = _relative_ids(Sq, Sk, MAX_REL)
        rel_k = rel_key_table[ids]
        scores = scores + jnp.einsum('bhqd,qkd->bhqk', q, rel_k)
        scores = scores / jnp.sqrt(jnp.asarray(hd, scores.dtype))
        attn = jax.nn.softmax(scores, axis=-1)
        out = jnp.einsum('bhqk,bhkd->bhqd', attn, v)
        rel_v = rel_value_table[ids]
        out = out + jnp.einsum('bhqk,qkd->bhqd', attn, rel_v)
        out = out.transpose(0, 2, 1, 3).reshape(B, Sq, H)
        return out @ Wo + bo

    def _L3_ffn_ref(x, ln1_w, ln2_w, wqkv, wo, gate_w, w13, w2):
        import jax, jax.numpy as jnp
        import numpy as np
        HID = 128
        NH = 16
        NKV = 4
        HD = HID // NH
        E = 8
        TOPK = 2
        FFN = 256
        EPS = 1e-05
        THETA = 10000.0

        def _rmsnorm(x, w):
            var = jnp.mean(x * x, axis=-1, keepdims=True)
            return x * jax.lax.rsqrt(var + EPS) * w

        def _rope_tables(S):
            inv_freq = 1.0 / THETA ** (jnp.arange(0, HD, 2, dtype=jnp.float32) / HD)
            freqs = jnp.arange(S, dtype=jnp.float32)[:, None] * inv_freq[None, :]
            emb = jnp.concatenate([freqs, freqs], axis=-1)
            return (jnp.cos(emb), jnp.sin(emb))

        def _apply_rope(t, cos, sin):
            t1, t2 = jnp.split(t, 2, axis=-1)
            rot = jnp.concatenate([-t2, t1], axis=-1)
            return t * cos[None, :, None, :] + rot * sin[None, :, None, :]
        B, S, _ = x.shape
        h = _rmsnorm(x, ln1_w)
        qkv = jnp.einsum('bsh,oh->bso', h, wqkv)
        q = qkv[..., :NH * HD].reshape(B, S, NH, HD)
        k = qkv[..., NH * HD:(NH + NKV) * HD].reshape(B, S, NKV, HD)
        v = qkv[..., (NH + NKV) * HD:].reshape(B, S, NKV, HD)
        cos, sin = _rope_tables(S)
        q = _apply_rope(q, cos, sin)
        k = _apply_rope(k, cos, sin)
        groups = NH // NKV
        k = jnp.repeat(k, groups, axis=2)
        v = jnp.repeat(v, groups, axis=2)
        scale = HD ** (-0.5)
        scores = jnp.einsum('bqhd,bkhd->bhqk', q, k) * scale
        causal = jnp.tril(jnp.ones((S, S), dtype=bool))
        scores = jnp.where(causal[None, None], scores, jnp.finfo(scores.dtype).min)
        probs = jax.nn.softmax(scores, axis=-1)
        attn = jnp.einsum('bhqk,bkhd->bqhd', probs, v).reshape(B, S, NH * HD)
        x = x + jnp.einsum('bso,ho->bsh', attn, wo)
        h = _rmsnorm(x, ln2_w).reshape(-1, HID)
        T = h.shape[0]
        logits = jnp.einsum('th,eh->te', h, gate_w)
        rprobs = jax.nn.softmax(logits.astype(jnp.float32), axis=-1)
        topw, topi = jax.lax.top_k(rprobs, TOPK)
        topw = topw / jnp.sum(topw, axis=-1, keepdims=True)
        wfull = jnp.zeros((T, E), jnp.float32).at[jnp.arange(T)[:, None], topi].set(topw)
        wfull = wfull.astype(h.dtype)
        out = jnp.zeros((T, HID), h.dtype)
        for e in range(E):
            w1 = w13[e, :FFN]
            w3 = w13[e, FFN:]
            g = jax.nn.silu(h @ w1.T) * (h @ w3.T)
            out = out + jnp.einsum('tf,hf->th', g, w2[e]) * wfull[:, e:e + 1]
        return x + out.reshape(B, S, HID)
    x = x + jnp.tanh(g_xattn[0]) * _L0_xattn_ref(_layernorm(x, axis=-1), ctx_1024, ctx_1024, L0_xattn_Wq, L0_xattn_bq, L0_xattn_Wk, L0_xattn_bk, L0_xattn_Wv, L0_xattn_bv, L0_xattn_Wo, L0_xattn_bo)
    x = x + jnp.tanh(g_ffn[0]) * _L0_ffn_ref(_layernorm(x, axis=-1), L0_ffn_gate_w, L0_ffn_we_gate, L0_ffn_we_up, L0_ffn_we_down, L0_ffn_ws_gate, L0_ffn_ws_up, L0_ffn_ws_down)
    x = x + jnp.tanh(g_xattn[1]) * _L1_xattn_ref(_layernorm(x, axis=-1), ctx_1024, L1_xattn_ptb_gamma, L1_xattn_W_fused, L1_xattn_W_attn_out, L1_xattn_W_ff_out, L1_xattn_ca_gamma, L1_xattn_ca_ctx_gamma, L1_xattn_W_q, L1_xattn_W_kv, L1_xattn_W_out)
    x = x + jnp.tanh(g_ffn[1]) * _L1_ffn_ref(_layernorm(x, axis=-1), L1_ffn_gate_w, L1_ffn_w1, L1_ffn_w2)
    x = x + jnp.tanh(g_xattn[2]) * _L2_xattn_ref(_layernorm(x, axis=-1), ctx_1024, L2_xattn_Wq, L2_xattn_bq, L2_xattn_Wk, L2_xattn_bk, L2_xattn_Wv, L2_xattn_bv)
    x = x + jnp.tanh(g_ffn[2]) * _L2_ffn_ref(_layernorm(x, axis=-1), L2_ffn_gate_w, L2_ffn_expert_bias, L2_ffn_w_up, L2_ffn_w_down, L2_ffn_shared_w_up, L2_ffn_shared_w_down)
    x = x + jnp.tanh(g_xattn[3]) * _L3_xattn_ref(_layernorm(x, axis=-1), ctx_1024, ctx_1024, L3_xattn_Wq, L3_xattn_bq, L3_xattn_Wk, L3_xattn_bk, L3_xattn_Wv, L3_xattn_bv, L3_xattn_Wo, L3_xattn_bo, L3_xattn_rel_key_table, L3_xattn_rel_value_table)
    x = x + jnp.tanh(g_ffn[3]) * _L3_ffn_ref(_layernorm(x, axis=-1), L3_ffn_ln1_w, L3_ffn_ln2_w, L3_ffn_wqkv, L3_ffn_wo, L3_ffn_gate_w, L3_ffn_w13, L3_ffn_w2)
    return x

_drawn_inputs = setup_inputs


def setup_inputs(seed=0):
    import zlib

    import numpy as np

    out = dict(_drawn_inputs(seed))
    spreads = {'L0_xattn_bq': (0.0, 0.313),
     'L0_xattn_bk': (0.0, 0.598),
     'L0_xattn_bv': (0.0, 0.1),
     'L0_xattn_bo': (0.0, 0.1),
     'L1_xattn_ptb_gamma': (1.0, 0.6),
     'L1_xattn_ca_gamma': (1.0, 0.6),
     'L1_xattn_ca_ctx_gamma': (1.0, 0.559),
     'L2_ffn_expert_bias': (0.0, 0.8),
     'L3_xattn_bq': (0.0, 0.387),
     'L3_xattn_bk': (0.0, 2.0),
     'L3_xattn_bv': (0.0, 0.1),
     'L3_xattn_bo': (0.0, 0.1),
     'L3_ffn_ln1_w': (1.0, 0.6),
     'L3_ffn_ln2_w': (1.0, 0.6)}
    factors = {'g_ffn': 27.208,
     'L0_ffn_gate_w': 7.967,
     'L0_ffn_we_gate': 8.0,
     'L0_ffn_we_up': 7.439,
     'L0_ffn_we_down': 7.715,
     'L0_ffn_ws_gate': 4.208,
     'L0_ffn_ws_up': 5.107,
     'L0_ffn_ws_down': 5.418,
     'L1_xattn_W_fused': 8.0,
     'L1_xattn_W_attn_out': 8.0,
     'L1_xattn_W_ff_out': 8.0,
     'L1_xattn_W_q': 8.0,
     'L2_xattn_bk': 64.0,
     'L2_xattn_bv': 5.001,
     'L2_ffn_gate_w': 8.0,
     'L2_ffn_w_up': 8.0,
     'L2_ffn_w_down': 8.0,
     'L2_ffn_shared_w_up': 6.985,
     'L2_ffn_shared_w_down': 6.517,
     'L3_ffn_wqkv': 5.079,
     'L3_ffn_wo': 5.366,
     'L3_ffn_gate_w': 8.0,
     'L3_ffn_w13': 8.0,
     'L3_ffn_w2': 8.0}
    for name, (base, spread) in spreads.items():
        noise = np.random.default_rng([zlib.crc32(name.encode()), seed]).standard_normal(out[name].shape)
        drawn = base * np.exp(spread * noise) if base else spread * noise
        out[name] = jnp.asarray(drawn.astype(out[name].dtype))
    for name, factor in factors.items():
        out[name] = (out[name] * factor).astype(out[name].dtype)
    return out
```

```python
from contextlib import ExitStack

import numpy as np

import concourse.bass as bass
from concourse import mybir

F32 = mybir.dt.float32
BF16 = mybir.dt.bfloat16
U32 = mybir.dt.uint32
ALU = mybir.AluOpType
ACT = mybir.ActivationFunctionType
X = mybir.AxisListType.X

B, S, D = 4, 256, 128
N = B * S
P = 128
NT = N // P
HALF = 512
H = 16
HD = D // H
DH = 64
E0, E1, E2, E3 = 8, 16, 8, 8
CAP0, CAP1 = 320, 80
FF1 = 512
HID2 = 176
HID2B = HID2 - P
REL = 128
EPS = 1e-5
SLOTS = E1 * CAP1
UNITS = 8
NEG = -3.0e38
STAGES = 8


def half(i):
    return slice(HALF * i, HALF * (i + 1))


def tile(t):
    return slice(P * t, P * (t + 1))


class Counted:

    def __init__(self, sem, past):
        self.sem, self.past = sem, past


def until(eng, counted, n):
    eng.wait_ge(counted.sem, n + counted.past)


class Attention:

    def __init__(self, sems, totals, width, causal, iters, units, staged_by, projected_by):
        self.width, self.causal, self.iters, self.units = width, causal, iters, units
        self.per_group = 4 if width == HD else 1
        self.groups = units // self.per_group
        self.staged_by = staged_by

        def counted(what, per_iteration):
            c = Counted(sems[what], totals.get(what, 0))
            totals[what] = c.past + per_iteration * iters
            return c

        self.staged = counted("staged", staged_by)
        self.projected = counted("projected", projected_by)
        self.scored = counted("scored", units)
        self.maxed = counted("maxed", units)
        self.exped = counted("exped", units)
        self.turned = [counted(f"turned{c}", self.count(c, units)) for c in range(2)]
        self.moved = [counted(f"moved{c}", self.count(c, units)) for c in range(2)]
        self.weighed = counted("weighed", units)
        self.inverted = counted("inverted", self.groups)
        self.normed = counted("normed", self.groups)
        self.outturned = counted("outturned", self.groups)
        self.stored = counted("stored", self.groups)

    def qt(self, u):
        return u // 4 % 2

    def key_tiles(self, u):
        return 1 if self.causal and self.qt(u) == 0 else 2

    def count(self, c, u):
        return sum(1 for v in range(u) if c < self.key_tiles(v))

    def ends_group(self, u):
        return u >= 0 and (u + 1) % self.per_group == 0


def wait_count(eng, sem, per, it, n):
    if isinstance(it, int):
        if per * it + n > 0:
            until(eng, sem, per * it + n)
    elif n > 0:
        until(eng, sem, it * per + n)


def build(nc, a, out):
    ctx = ExitStack()
    with ctx:
        def sb(name, shape, dt=F32):
            return ctx.enter_context(nc.sbuf_tensor(name, shape, dt))

        def sem(name):
            return ctx.enter_context(nc.semaphore(name))

        ps = ctx.enter_context(nc.psum_tensor("ps", [P, 8, HALF], F32))

        xT = sb("xT", [P, N])
        ctxT = sb("ctxT", [P, N])
        hT = sb("hT", [P, N])
        h1T = sb("h1T", [P, N])
        sq = sb("sq", [P, N])
        xc = sb("xc", [P, N])
        ident = sb("ident", [P, P])
        identb = sb("identb", [P, P], BF16)
        meaner = sb("meaner", [P, P])
        before = sb("before", [P, P])
        beforeb = sb("beforeb", [P, P], BF16)
        ones = sb("ones", [P, P])
        onesb = sb("onesb", [P, P], BF16)
        zerob = sb("zerob", [P, HALF], BF16)
        causal = sb("causal", [P, P])
        causalb = sb("causalb", [P, P], BF16)
        cols = sb("cols", [P, 32])
        hmask = sb("hmask", [P, 4])
        rope = sb("rope", [P, 4, S])
        gates = sb("gates", [P, 8])
        iota = sb("iota", [P, SLOTS])
        iota_e = sb("iota_e", [P, E1])
        slot_of = sb("slot_of", [P, E1])
        eps = sb("eps", [P, 1])

        w0 = sb("w0", [P, 6, D])
        bv = sb("bv", [P, 3, D])
        w2x = sb("w2x", [P, 3, D])
        w3x = sb("w3x", [P, 4, D])
        gw = sb("gw", [P, E0 + E1 + E2 + E3])
        ebias = sb("ebias", [P, E2])
        mA = sb("mA", [P, 48 * D])
        WA1 = 8 * D
        w1 = sb("w1", [P, 8 * D + D + DH + 8 * D + 8 * D + D + DH + 8 * D])
        up2 = sb("up2", [P, E2, HID2], BF16)
        dn2 = sb("dn2", [P, E2, 2, D], BF16)
        arena = sb("arena", [P, 2 * E1 * FF1])
        q_all = sb("q_all", [P, N])
        k_all = sb("k_all", [P, N])
        q_st = sb("q_st", [P, 8, S])
        km = sb("km", [P, 4, S])
        v_all = sb("v_all", [P, NT, H * (HD + 1)])
        prob = sb("prob", [P, 2, 4, S])
        probT = sb("probT", [P, 2, 2, HALF])
        negmax = sb("negmax", [P, 2, 4])
        rsum = sb("rsum", [P, 4, H])
        onorm = sb("onorm", [P, 2, 4 * DH])
        big = arena[:, E1 * FF1:].rearrange("p (c t) -> p c t", c=8)
        att = xc
        lg = sb("lg", [P, NT, E1])
        lg2 = sb("lg2", [P, NT, E1])
        small = sb("small", [P, 8, NT])
        top8 = sb("top8", [P, NT, 8])
        idx8 = sb("idx8", [P, NT, 8], U32)
        idxf = sb("idxf", [P, NT, 2])
        oh = sb("oh", [P, 3, NT, E1])
        selb = sb("selb", [P, NT, E1], BF16)
        comb = sb("comb", [P, NT, 10])
        g_sb = prob[:, 0, :, :].rearrange("p j k -> p (j k)").rearrange("p (i n) -> p i n", i=2)
        a_sb = prob[:, 1, :, :].rearrange("p j k -> p (j k)").rearrange("p (i n) -> p i n", i=2)
        c_sb = probT[:, 0, :, :]
        d_sb = probT[:, 1, :, :]

        ld = {k: sem("ld_" + k) for k in ("c", "x", "w0", "m0", "w1", "e1", "w2", "f2", "w3", "m3", "r3", "out")}
        ld["e1a"] = ld["e1b"] = ld["e1"]
        narrowed = sem("narrowed")
        n_mean, n_cent, n_sq, n_var, n_std, n_rstd, n_out = (
            sem(s) for s in ("n_mean", "n_cent", "n_sq", "n_var", "n_std", "n_rstd", "n_out"))
        x_done = sem("x_done")
        made = sem("made")
        gated = sem("gated")
        chain = sem("chain")
        links = [0]

        loads = {
            "c": [(ident[:, :], a["ident"]), (meaner[:, :], a["meaner"]), (before[:, :], a["before"]),
                  (causal[:, :], a["causal"]), (cols[:, :], a["cols"]), (hmask[:, :], a["hmask"]),
                  (rope[:, :, :], a["rope"]), (gates[:, :], a["gates"].broadcast_to([P, 8])),
                  (iota[:, :], a["iota"].partition_broadcast(P)), (slot_of[:, :], a["slot_of"]),
                  (iota_e[:, :], a["iota"][:, 0:E1].partition_broadcast(P)),
                  (gw[:, :], a["gw"]), (bv[:, :, :], a["bv"].partition_broadcast(P)),
                  (ebias[:, :], a["ebias"].partition_broadcast(P))],
            "x": [(xT[:, :], a["xT"]), (ctxT[:, :], a["ctxT"])],
            "w0": [(w0[:, :, :], a["w0"])],
            "m0": [(mA[:, 0:30 * D], a["m0"])],
            "w1": [(w1[:, :], a["w1"]), (mA[:, 30 * D:42 * D], a["m1"])],
            "e1a": [(arena[:, 0:E1 * FF1], a["e1"][:, 0:E1 * FF1])],
            "e1b": [(arena[:, E1 * FF1:], a["e1"][:, E1 * FF1:])],
            "w2": [(w2x[:, :, :], a["w2x"]), (w3x[:, :, :], a["w3x"])],
            "f2": [(mA[:, 0:E2 * HID2], a["up2"].rearrange("p e n -> p (e n)")),
                   (mA[:, E2 * HID2:E2 * HID2 + E2 * 2 * D], a["dn2"].rearrange("p e c n -> p (e c n)"))],
            "m3": [(mA[:, :], a["m3"])],
            "w3": [(w0[:, :, :].rearrange("p w n -> p (w n)")[:, 0:5 * D + 32], a["w3f"])],
            "r3": [(w1[:, 0:2 * S * HD], a["relv"].rearrange("p c q d -> p (c q d)")),
                   (iota[:, 512:512 + HID2 + 2 * D], a["sh2"])]
                  + [(iota[32 * c:32 * c + HD, 0:2 * S - 1], a["relk"]) for c in range(4)],
        }
        C_BQ0, C_BQR0, C_BK0, C_BKR0, C_BO0, C_PTB, C_CA, C_CTX, C_BQ2, C_BK2, C_BQ3, C_BK3, C_BO3, C_LN1, C_LN2 = range(15)

        def col(i):
            return cols[:, i:i + 1]

        def link(eng, ins):
            links[0] += 1
            ins.then_inc(chain, 1)
            eng.wait_ge(chain, links[0])

        def norm_pe(pe, k, km_, src, wait_src):
            for i in range(2):
                if km_ is not None:
                    wait_src(pe, i)
                    nc.tensor.matmul(ps[:, i, :], meaner[:, :], src[:, half(i)], start=True, stop=True).then_inc(n_mean, 1)
            for i in range(2):
                pe.wait_ge(n_sq, 2 * k + i + 1)
                nc.tensor.matmul(ps[:, 2 + i, :], meaner[:, :], sq[:, half(i)], start=True, stop=True).then_inc(n_var, 1)

        def norm_dve(v, k, km_, src, dst, gamma):
            if k:
                v.wait_ge(n_out, 2 * k)
            for i in range(2):
                if km_ is not None:
                    v.wait_ge(n_mean, 2 * km_ + i + 1)
                    nc.vector.tensor_tensor(xc[:, half(i)], src[:, half(i)], ps[:, i, :], ALU.subtract).then_inc(n_cent, 1)
            cen = xc if km_ is not None else src
            for i in range(2):
                v.wait_ge(n_std, 2 * k + i + 1)
                nc.vector.reciprocal(sq[:, half(i)], sq[:, half(i)]).then_inc(n_rstd, 1)
                v.wait_ge(n_rstd, 2 * k + i + 1)
                if gamma is None:
                    nc.vector.tensor_tensor(dst[:, half(i)], cen[:, half(i)], sq[:, half(i)], ALU.mult).then_inc(n_out, 1)
                else:
                    nc.vector.scalar_tensor_tensor(dst[:, half(i)], cen[:, half(i)], gamma, sq[:, half(i)],
                                                   ALU.mult, ALU.mult).then_inc(n_out, 1)

        def norm_act(act, k, km_, src, wait_src):
            for i in range(2):
                if km_ is not None:
                    act.wait_ge(n_cent, 2 * km_ + i + 1)
                    nc.scalar.activation(sq[:, half(i)], xc[:, half(i)], ACT.Square).then_inc(n_sq, 1)
                else:
                    wait_src(act, i)
                    nc.scalar.activation(sq[:, half(i)], src[:, half(i)], ACT.Square).then_inc(n_sq, 1)
            for i in range(2):
                act.wait_ge(n_var, 2 * k + i + 1)
                nc.scalar.activation(sq[:, half(i)], ps[:, 2 + i, :], ACT.Sqrt, bias=eps[:, 0:1]).then_inc(n_std, 1)

        def x_ready(k):
            def wait(eng, i):
                if k == 0:
                    eng.wait_ge(ld["x"], 32)
                    eng.wait_ge(ld["c"], 16 * len(loads["c"]))
                    eng.wait_ge(made, 1)
                else:
                    eng.wait_ge(x_done, 2 * (k - 1) + i + 1)
            return wait

        def norm_ready(k):
            def wait(eng, i):
                eng.wait_ge(n_out, 2 * k + i + 1)
            return wait

        def sc_bank(u, j):
            return 2 * (u % 2) + j // 2

        def scores(pe, A, it, u):
            wait_count(pe, A.exped, A.units, it, max(0, u - 1))
            for jp in range(2):
                o = ps[:, sc_bank(u, 2 * jp), :].rearrange("p (j k) -> p j k", j=2)
                last = A.score(jp, it, u, o, A.key_tiles(u) * P)
            last.then_inc(A.scored.sem, 1)

        def turn(pe, A, it, u):
            until(pe, A.exped, it * A.units + u + 1)
            for c in range(A.key_tiles(u)):
                wait_count(pe, A.moved[c], A.count(c, A.units), it, A.count(c, u))
                for j in range(4):
                    last = nc.tensor.transpose(ps[:, 4 + c, tile(j)], prob[:, u % 2, j, tile(c)], ident[:, :])
                last.then_inc(A.turned[c].sem, 1)

        def weigh(pe, A, it, u):
            for c in range(A.key_tiles(u)):
                until(pe, A.moved[c], it * A.count(c, A.units) + A.count(c, u) + 1)
            g = u // A.per_group
            if u % A.per_group == 0:
                wait_count(pe, A.stored, A.groups, it, max(0, g - 1))
            w = A.width + 1
            for j in range(4):
                off = (u % A.per_group * 4 + A.head(j)) * w
                for c in range(A.key_tiles(u)):
                    last = nc.tensor.matmul(ps[:, 6 + g % 2, off:off + w], A.probT(it, u, c, j), A.value(it, u, c, j),
                                            start=(c == 0), stop=(c == A.key_tiles(u) - 1))
            last.then_inc(A.weighed.sem, 1)

        def out_turn(pe, A, it, g):
            until(pe, A.normed, it * A.groups + g + 1)
            nb = 1 if A.width == HD else 2
            for i in range(nb):
                last = nc.tensor.transpose(ps[:, 6 + g % 2, tile(i)], onorm[:, g % 2, tile(i)], ident[:, :])
            last.then_inc(A.outturned.sem, 1)

        def attn_pe(pe, A):
            def iteration(it):
                A.project(pe, it)
                if A.staged_by:
                    until(pe, A.staged, it * A.staged_by + A.staged_by)
                scores(pe, A, it, 0)
                for u in range(A.units):
                    if u + 1 < A.units:
                        scores(pe, A, it, u + 1)
                    turn(pe, A, it, u)
                    if u >= 1:
                        weigh(pe, A, it, u - 1)
                    if A.ends_group(u - 2):
                        out_turn(pe, A, it, (u - 2) // A.per_group)
                weigh(pe, A, it, A.units - 1)
                for u in (A.units - 2, A.units - 1):
                    if A.ends_group(u):
                        out_turn(pe, A, it, u // A.per_group)
                until(pe, A.stored, it * A.groups + A.groups)
            if A.loop:
                with pe.Fori(0, A.iters) as it:
                    iteration(it)
            else:
                for it in range(A.iters):
                    A.before_pe(pe, it)
                    iteration(it)
                    A.after_pe(pe, it)

        def attn_dve(v, A):
            def maxima(it, u):
                until(v, A.scored, it * A.units + u + 1)
                b0 = sc_bank(u, 0)
                s = ps[:, b0:b0 + 2, :].rearrange("p b (j k) -> p (b j) k", j=2)[:, :, 0:A.key_tiles(u) * P]
                nc.vector.tensor_reduce(negmax[:, u % 2, :], s, X, ALU.max, negate=True).then_inc(A.maxed.sem, 1)

            def move(it, u):
                until(v, A.turned[0], it * A.count(0, A.units) + A.count(0, u) + 1)
                wait_count(v, A.weighed, A.units, it, max(0, u - 1))
                nc.vector.tensor_copy(A.moved_to(it, u, 0), A.moved_from(0)).then_inc(A.moved[0].sem, 1)

            def normalise(it, g):
                until(v, A.weighed, it * A.units + (g + 1) * A.per_group)
                wait_count(v, A.outturned, A.groups, it, max(0, g - 1))
                nh = 4 * A.per_group
                o = ps[:, 6 + g % 2, 0:nh * (A.width + 1)].rearrange("p (h w) -> p h w", h=nh)
                nc.vector.reciprocal(rsum[:, A.rslot(g), 0:nh], o[:, :, A.width]).then_inc(A.inverted.sem, 1)
                until(v, A.inverted, it * A.groups + g + 1)
                nc.vector.tensor_tensor(
                    onorm[:, g % 2, 0:nh * A.width].rearrange("p (h w) -> p h w", h=nh), o[:, :, 0:A.width],
                    rsum[:, A.rslot(g), 0:nh].unsqueeze(2).broadcast_to([P, nh, A.width]), ALU.mult).then_inc(A.normed.sem, 1)

            def iteration(it):
                A.stage(v, it)
                for u in range(A.units):
                    maxima(it, u)
                    if u >= 1:
                        move(it, u - 1)
                    if A.ends_group(u - 2):
                        normalise(it, (u - 2) // A.per_group)
                move(it, A.units - 1)
                for u in (A.units - 2, A.units - 1):
                    if A.ends_group(u):
                        normalise(it, u // A.per_group)
            if A.loop:
                with v.Fori(0, A.iters) as it:
                    iteration(it)
            else:
                for it in range(A.iters):
                    A.before_dve(v, it)
                    iteration(it)
                    A.after_dve(v, it)

        def attn_act(act, A):
            def exps(it, u):
                until(act, A.maxed, it * A.units + u + 1)
                for c in range(2):
                    wait_count(act, A.turned[c], A.count(c, A.units), it, A.count(c, max(0, u - 1)))
                n = A.key_tiles(u) * P
                for j in range(4):
                    s = ps[:, sc_bank(u, j), :].rearrange("p (j k) -> p j k", j=2)[:, j % 2, 0:n]
                    last = nc.scalar.activation(prob[:, u % 2, j, 0:n], s, ACT.Exp, bias=negmax[:, u % 2, j:j + 1])
                last.then_inc(A.exped.sem, 1)

            def move(it, u):
                if A.key_tiles(u) < 2:
                    return
                until(act, A.turned[1], it * A.count(1, A.units) + A.count(1, u) + 1)
                wait_count(act, A.weighed, A.units, it, max(0, u - 1))
                nc.scalar.copy(A.moved_to(it, u, 1), A.moved_from(1)).then_inc(A.moved[1].sem, 1)

            def store(it, g):
                until(act, A.outturned, it * A.groups + g + 1)
                nb = 1 if A.width == HD else 2
                nc.scalar.copy(A.output(it, g), ps[:, 6 + g % 2, 0:nb * P] if nb == 1 else
                               ps[:, 6 + g % 2, 0:nb * P].rearrange("p (b t) -> p b t", b=nb)).then_inc(A.stored.sem, 1)

            def iteration(it):
                A.stage_act(act, it)
                for u in range(A.units):
                    exps(it, u)
                    if u >= 1:
                        move(it, u - 1)
                    if A.ends_group(u - 3):
                        store(it, (u - 3) // A.per_group)
                move(it, A.units - 1)
                for u in (A.units - 3, A.units - 2, A.units - 1):
                    if A.ends_group(u):
                        store(it, u // A.per_group)
            if A.loop:
                with act.Fori(0, A.iters) as it:
                    iteration(it)
            else:
                for it in range(A.iters):
                    A.before_act(act, it)
                    iteration(it)
                    A.after_act(act, it)

        def nothing(*_):
            pass

        attn_sems = {x: sem(f"attn_{x}") for x in ("staged", "projected", "scored", "maxed", "exped", "turned0", "turned1",
                                                   "moved0", "moved1", "weighed", "inverted", "normed", "outturned", "stored")}
        attn_totals = {}

        def attention(width, causal, iters, units, staged_by, projected_by, loop):
            A = Attention(attn_sems, attn_totals, width, causal, iters, units, staged_by, projected_by)
            A.loop = loop
            A.rslot = lambda g: g % 2
            A.head = lambda j: j
            A.project = A.stage = A.stage_act = nothing
            A.before_pe = A.after_pe = A.before_dve = A.after_dve = A.before_act = A.after_act = nothing
            A.probT = lambda it, u, c, j: probT[:, u % 2, c, tile(j)]
            A.moved_to = lambda it, u, c: probT[:, u % 2, c, :]
            A.moved_from = lambda c: ps[:, 4 + c, :]
            return A

        def narrow(causal, value):
            A = attention(HD, causal, B, UNITS, 5, 0, True)

            def score(jp, it, u, o, nk):
                g = u % 4
                last = nc.tensor.matmul(o[:, :, 0:nk], q_st[32 * g:32 * g + 32, 0, tile(A.qt(u))],
                                        km[32 * g:32 * g + 32, 2 * jp:2 * jp + 2, 0:nk], start=True, stop=True)
                if causal:
                    last = nc.tensor.matmul(o[:, :, nk - P:nk], identb[:, :],
                                            causalb[:, :].unsqueeze(1).broadcast_to([P, 2, P]),
                                            start=False, stop=True, skip_group_check=True)
                return last

            def stage(v, it):
                cols_ = bass.ds(it * S, S)
                nc.vector.tensor_copy(q_st[:, 0, :], q_all[:, cols_]).then_inc(A.staged.sem, 1)
                for j in range(4):
                    nc.vector.tensor_scalar(km[:, j, :], k_all[:, cols_], hmask[:, j:j + 1], None,
                                            ALU.mult).then_inc(A.staged.sem, 1)

            A.score, A.stage, A.value = score, stage, value
            A.output = lambda it, g: att[:, bass.ds(it * S + g * P, P)]
            return A

        def value_narrow(it, u, c, j):
            h = 4 * (u % 4) + j
            return v_all[:, bass.ds(it * 2 + c, 1), h * (HD + 1):(h + 1) * (HD + 1)]

        def value_grouped(it, u, c, j):
            h = u % 4
            return v_all[:, bass.ds(it * 2 + c, 1), h * (HD + 1):(h + 1) * (HD + 1)]

        A0 = narrow(False, value_narrow)

        q0, k0, v0, o0 = sem("L0_qk"), sem("L0_qk_done"), sem("L0_v"), sem("L0_o")
        v0d, t0 = sem("L0_v_done"), sem("L0_t")

        def rope_pe(pe, wt, first, other, wait_h, done, qk_from_h):
            for w in range(4):
                src = hT if w < 2 or qk_from_h else other
                for i in range(2):
                    if w == 0:
                        wait_h(pe, i)
                    nc.tensor.matmul(ps[:, 2 * w + i, :], wt[:, w, :], src[:, half(i)], start=True, stop=True).then_inc(done, 1)

        def rope_dve(v, done, rdy, biases, t):
            for i in range(2):
                for w, dst in ((0, q_all), (2, k_all)):
                    cs = 2 - w
                    v.wait_ge(done, 2 * (w + 1) + i + 1)
                    pair = (a_sb, g_sb) if w == 0 else (c_sb, d_sb)
                    for r, tmp in enumerate(pair):
                        nc.vector.scalar_tensor_tensor(
                            tmp[:, i, :].rearrange("p (b s) -> p b s", b=2),
                            ps[:, 2 * (w + r) + i, :].rearrange("p (b s) -> p b s", b=2),
                            biases[w + r], rope[:, cs + r, :].unsqueeze(1).broadcast_to([P, 2, S]),
                            ALU.add, ALU.mult).then_inc(t, 1)
                    v.wait_ge(t, 4 * i + 2 * (w // 2) + 2)
                    nc.vector.tensor_tensor(dst[:, half(i)], pair[0][:, i, :], pair[1][:, i, :], ALU.add).then_inc(rdy, 1)

        def l0_attn_pe(pe):
            norm_pe(pe, 0, 0, xT, x_ready(0))
            pe.wait_ge(ld["w0"], 16)
            rope_pe(pe, w0, 0, ctxT, norm_ready(0), q0, False)
            pe.wait_ge(k0, 4)
            for t in range(NT):
                mm = nc.tensor.matmul(ps[:, t // 4, tile(t % 4)], ctxT[:, tile(t)], w0[:, 4, :], start=True, stop=True)
            mm.then_inc(v0, 1)
            attn_pe(pe, A0)
            for i in range(2):
                until(pe, A0.stored, 8)
                nc.tensor.matmul(ps[:, i, :], w0[:, 5, :], att[:, half(i)], start=True, stop=True).then_inc(o0, 1)

        def values_dve(v, layer, done, vd, heads, width):
            nc.vector.memset(v_all[:, :, 0:heads * (width + 1)], 1.0).then_inc(vd, 1)
            v.wait_ge(vd, 1)
            v.wait_ge(done, 1)
            for t in range(NT):
                o = v_all[:, t, 0:heads * (width + 1)].rearrange("p (h w) -> p h w", h=heads)[:, :, 0:width]
                s = ps[:, t // 4, (t % 4) * P:(t % 4) * P + heads * width].rearrange("p (h w) -> p h w", h=heads)
                if layer is None:
                    nc.vector.tensor_copy(o, s).then_inc(vd, 1)
                else:
                    nc.vector.tensor_tensor(o, s, bv[:, layer, 0:heads * width].rearrange("p (h w) -> p h w", h=heads),
                                            ALU.add).then_inc(vd, 1)

        def residual(v, k, i, y, gate, bias, tmp):
            if bias is not None:
                link(v, nc.vector.tensor_scalar(tmp, y, bias, None, ALU.add))
                y = tmp
            nc.vector.scalar_tensor_tensor(xT[:, half(i)], y, gates[:, gate:gate + 1], xT[:, half(i)],
                                           ALU.mult, ALU.add).then_inc(x_done, 1)

        def l0_attn_dve(v):
            v.wait_ge(ld["c"], 16 * len(loads["c"]))
            nc.vector.memset(eps[:, :], EPS)
            nc.vector.memset(zerob[:, :], 0.0)
            nc.vector.memset(ones[:, :], 1.0)
            nc.vector.memset(onesb[:, :], 1.0)
            nc.vector.tensor_copy(identb[:, :], ident[:, :])
            nc.vector.tensor_copy(beforeb[:, :], before[:, :])
            nc.vector.tensor_copy(causalb[:, :], causal[:, :]).then_inc(made, 1)
            norm_dve(v, 0, 0, xT, hT, None)
            rope_dve(v, q0, k0, [col(C_BQ0), col(C_BQR0), col(C_BK0), col(C_BKR0)], t0)
            v.wait_ge(k0, 4)
            values_dve(v, 0, v0, v0d, H, HD)
            v.wait_ge(v0d, 1 + NT)
            attn_dve(v, A0)
            v.wait_ge(gated, 1)
            for i in range(2):
                v.wait_ge(o0, i + 1)
                residual(v, 0, i, ps[:, i, :], 0, col(C_BO0), a_sb[:, i, :])

        def l0_attn_act(act):
            act.wait_ge(ld["c"], 16 * len(loads["c"]))
            nc.scalar.activation(gates[:, :], gates[:, :], ACT.Tanh).then_inc(gated, 1)
            act.wait_ge(made, 1)
            norm_act(act, 0, 0, xT, x_ready(0))
            attn_act(act, A0)

        def by_tile(ap, e):
            return ap.rearrange("p (t e) -> p t e", e=e)

        def logits_pe(pe, k, first, e, done):
            for t in range(NT):
                pe.wait_ge(n_out, 2 * k + t // 4 + 1)
                mm = nc.tensor.matmul(ps[:, 4, t * e:(t + 1) * e], hT[:, tile(t)], gw[:, first:first + e], start=True, stop=True)
            mm.then_inc(done, 1)

        def softmax_dve(v, e, done, shifted, exped):
            v.wait_ge(done, 1)
            z = by_tile(ps[:, 4, 0:NT * e], e)
            link(v, nc.vector.tensor_reduce(small[:, 0, :], z, X, ALU.max))
            nc.vector.tensor_tensor(lg[:, :, 0:e], z, small[:, 0, :].unsqueeze(2).broadcast_to([P, NT, e]),
                                    ALU.subtract).then_inc(shifted, 1)
            v.wait_ge(exped, 1)
            link(v, nc.vector.tensor_reduce(small[:, 1, :], lg[:, :, 0:e], X, ALU.add))
            link(v, nc.vector.reciprocal(small[:, 2, :], small[:, 1, :]))
            link(v, nc.vector.tensor_tensor(lg[:, :, 0:e], lg[:, :, 0:e],
                                            small[:, 2, :].unsqueeze(2).broadcast_to([P, NT, e]), ALU.mult))

        def softmax_act(act, e, shifted, exped):
            act.wait_ge(shifted, 1)
            nc.scalar.activation(lg[:, :, 0:e], lg[:, :, 0:e], ACT.Exp).then_inc(exped, 1)

        def choose(v, src, e, ks):
            for t in range(NT):
                ins = nc.vector.max(top8[:, t, :], src[:, t, 0:e])
            link(v, ins)
            for t in range(NT):
                ins = nc.vector.max_index(idx8[:, t, :], top8[:, t, :], src[:, t, 0:e])
            link(v, ins)
            link(v, nc.vector.tensor_copy(idxf[:, :, :], idx8[:, :, 0:2]))
            for k in range(ks):
                ins = nc.vector.tensor_tensor(oh[:, k, :, 0:e], iota_e[:, 0:e].unsqueeze(1).broadcast_to([P, NT, e]),
                                              idxf[:, :, k:k + 1].broadcast_to([P, NT, e]), ALU.is_equal)
            link(v, ins)
            if ks == 2:
                link(v, nc.vector.tensor_tensor(oh[:, 2, :, 0:e], oh[:, 0, :, 0:e], oh[:, 1, :, 0:e], ALU.add))

        def ranks_pe(pe, e, sel_ready, done):
            pe.wait_ge(sel_ready, 1)
            flat = selb[:, :, 0:e]
            nc.tensor.matmul(by_tile(ps[:, 5, 0:NT * e], e), beforeb[:, :], flat, start=True, stop=False, skip_group_check=True)
            for t in range(NT - 1):
                mm = nc.tensor.matmul(by_tile(ps[:, 5, (t + 1) * e:NT * e], e), onesb[:, :],
                                      selb[:, t:t + 1, 0:e].broadcast_to([P, NT - 1 - t, e]),
                                      start=False, stop=(t == NT - 2), skip_group_check=True)
            mm.then_inc(done, 1)

        class Mlp:

            upped, silued, mixed, acted, downed = (sem(f"mlp_{x}") for x in ("upped", "silued", "mixed", "acted", "downed"))

            def __init__(self, counted, base, experts, parts, weighed):
                self.counted = counted
                self.units = [(e, i, c) for e in range(experts) for i in range(2) for c in range(parts)]
                self.weights = lambda e, c, w: mA[:, base + ((e * parts + c) * 3 + w) * D:base + ((e * parts + c) * 3 + w + 1) * D]
                self.parts, self.weighed, self.last = parts, weighed, (experts - 1, parts - 1)

        def mlp_pe(pe, M, before_first):
            def up(n):
                e, i, c = M.units[n]
                if n >= 2:
                    pe.wait_ge(M.acted, M.counted + n - 1)
                nc.tensor.matmul(ps[:, 2 + n % 2, :], M.weights(e, c, 0), hT[:, half(i)], start=True, stop=True)
                mm = nc.tensor.matmul(ps[:, 4 + n % 2, :], M.weights(e, c, 1), hT[:, half(i)], start=True, stop=True)
                if M.weighed and c == 0:
                    for t in range(4):
                        mm = nc.tensor.matmul(ps[:, 6 + n // M.parts % 2, tile(t)],
                                              comb[:, 4 * i + t, e:e + 1].broadcast_to([P, P]), ident[:, :],
                                              start=True, stop=True)
                mm.then_inc(M.upped, 1)

            def down(n):
                e, i, c = M.units[n]
                pe.wait_ge(M.acted, M.counted + n + 1)
                nc.tensor.matmul(ps[:, i, :], M.weights(e, c, 2), a_sb[:, n % 2, :], start=(e == 0 and c == 0),
                                 stop=((e, c) == M.last), skip_group_check=True).then_inc(M.downed, 1)

            before_first(pe)
            up(0)
            for n in range(len(M.units)):
                if n + 1 < len(M.units):
                    up(n + 1)
                down(n)

        def mlp_act(act, M):
            for n in range(len(M.units)):
                act.wait_ge(M.upped, M.counted + n + 1)
                if n >= 2:
                    act.wait_ge(M.mixed, M.counted + n - 1)
                nc.scalar.activation(g_sb[:, n % 2, :], ps[:, 2 + n % 2, :], ACT.Silu).then_inc(M.silued, 1)

        def mlp_dve(v, M):
            for n in range(len(M.units)):
                v.wait_ge(M.silued, M.counted + n + 1)
                if n >= 2:
                    v.wait_ge(M.downed, M.counted + n - 1)
                ins = nc.vector.tensor_tensor(a_sb[:, n % 2, :], g_sb[:, n % 2, :], ps[:, 4 + n % 2, :], ALU.mult)
                ins.then_inc(M.mixed, 1)
                if M.weighed:
                    v.wait_ge(M.mixed, M.counted + n + 1)
                    ins = nc.vector.tensor_tensor(a_sb[:, n % 2, :], a_sb[:, n % 2, :],
                                                  ps[:, 6 + n // M.parts % 2, :], ALU.mult).then_inc(M.acted, 1)
                else:
                    v.wait_ge(M.mixed, M.counted + n + 1)
                    v.sem_inc(M.acted, 1)

        r0 = [sem(f"R0_{x}") for x in ("logits", "shifted", "exped", "chosen", "ranked", "ready")]
        M0 = Mlp(0, 0, 10, 1, True)

        def l0_ffn_pe(pe):
            norm_pe(pe, 1, 1, xT, x_ready(1))
            logits_pe(pe, 1, 0, E0, r0[0])
            ranks_pe(pe, E0, r0[3], r0[4])

            def first(pe):
                pe.wait_ge(ld["m0"], 16)
                pe.wait_ge(r0[5], 1)
            mlp_pe(pe, M0, first)

        def l0_ffn_act(act):
            norm_act(act, 1, 1, xT, x_ready(1))
            softmax_act(act, E0, r0[1], r0[2])
            mlp_act(act, M0)

        def l0_ffn_dve(v):
            norm_dve(v, 1, 1, xT, hT, None)
            softmax_dve(v, E0, r0[0], r0[1], r0[2])
            choose(v, lg, E0, 2)
            nc.vector.tensor_copy(selb[:, :, 0:E0], oh[:, 2, :, 0:E0]).then_inc(r0[3], 1)
            link(v, nc.vector.tensor_tensor(small[:, 3, :], top8[:, :, 0], top8[:, :, 1], ALU.add))
            link(v, nc.vector.tensor_scalar(small[:, 3, :], small[:, 3, :], 1e-20, None, ALU.add))
            link(v, nc.vector.reciprocal(small[:, 4, :], small[:, 3, :]))
            link(v, nc.vector.tensor_tensor(lg[:, :, 0:E0], lg[:, :, 0:E0],
                                            small[:, 4, :].unsqueeze(2).broadcast_to([P, NT, E0]), ALU.mult))
            link(v, nc.vector.tensor_tensor(lg[:, :, 0:E0], lg[:, :, 0:E0], oh[:, 2, :, 0:E0], ALU.mult))
            v.wait_ge(r0[4], 1)
            link(v, nc.vector.tensor_scalar(lg2[:, :, 0:E0], by_tile(ps[:, 5, 0:NT * E0], E0), float(CAP0), None, ALU.is_lt))
            nc.vector.memset(comb[:, :, E0:E0 + 2], 1.0)
            nc.vector.tensor_tensor(comb[:, :, 0:E0], lg[:, :, 0:E0], lg2[:, :, 0:E0], ALU.mult).then_inc(r0[5], 1)
            mlp_dve(v, M0)
            for i in range(2):
                v.wait_ge(M0.downed, M0.counted + len(M0.units))
                residual(v, 1, i, ps[:, i, :], 1, None, None)

        WB = 8 * P + P + DH + 8 * P
        M1 = Mlp(20, 30 * D, 4, 1, False)
        cT = k_all

        def wide(causal, base, q_src, k_src):
            A = attention(DH, causal, B, UNITS, 5, 9, True)
            A.head = lambda j: j // 2 + 2 * (j % 2)

            def project(pe, it):
                cols_ = bass.ds(it * S, S)
                for c in range(9):
                    src = q_src if c < 8 else k_src
                    nc.tensor.matmul(ps[:, c // 2, (c % 2) * S:(c % 2 + 1) * S], w1[:, base + P * c:base + P * c + P],
                                     src[:, cols_], start=True, stop=True).then_inc(A.projected.sem, 1)

            def stage(v, it):
                for c in range(0, 4, 2):
                    until(v, A.projected, it * 9 + c + 2)
                    nc.vector.tensor_scalar(q_st[:, c:c + 2, :].rearrange("p c s -> p (c s)"), ps[:, c // 2, :],
                                            DH ** -0.5, None, ALU.mult).then_inc(A.staged.sem, 1)

            def stage_act(act, it):
                for c in range(4, 8, 2):
                    until(act, A.projected, it * 9 + c + 2)
                    nc.scalar.mul(q_st[:, c:c + 2, :].rearrange("p c s -> p (c s)"), ps[:, c // 2, :],
                                  DH ** -0.5).then_inc(A.staged.sem, 1)
                until(act, A.projected, it * 9 + 9)
                nc.scalar.copy(km[:, 0, :], ps[:, 4, 0:S]).then_inc(A.staged.sem, 1)

            def score(jp, it, u, o, nk):
                for s in range(2):
                    r = slice(DH * jp, DH * jp + DH)
                    last = nc.tensor.matmul(o[:, s, 0:nk], q_st[r, 2 * (u % 4) + s, tile(A.qt(u))], km[r, 0, 0:nk],
                                            start=True, stop=True)
                    if causal:
                        last = nc.tensor.matmul(o[:, s, nk - P:nk], identb[:, :], causalb[:, :],
                                                start=False, stop=True, skip_group_check=True)
                return last

            A.project, A.stage, A.stage_act, A.score = project, stage, stage_act, score
            A.value = lambda it, u, c, j: v_all[:, bass.ds(it * 2 + c, 1), 0:DH + 1]
            A.output = lambda it, u: big[:, 2 * (u % 4):2 * (u % 4) + 2, bass.ds(it * S + A.qt(u) * P, P)]
            return A

        A1a = wide(True, 0, hT, hT)
        A1b = wide(False, WB, hT, cT)
        v1 = [[sem(f"L1{x}_v"), sem(f"L1{x}_v_done"), sem(f"L1{x}_o")] for x in "ab"]
        y1 = sem("L1_y")

        def wide_pe(pe, A, base, v_src, s):
            for t in range(NT):
                mm = nc.tensor.matmul(ps[:, t // 4, (t % 4) * P:(t % 4) * P + DH], v_src[:, tile(t)],
                                      w1[:, base + 9 * P:base + 9 * P + DH], start=True, stop=True)
            mm.then_inc(s[0], 1)
            pe.wait_ge(s[1], 1 + NT)
            attn_pe(pe, A)
            until(pe, A.stored, A.groups * B)
            for i in range(2):
                for c in range(8):
                    w = w1[:, base + 9 * P + DH + P * c:base + 9 * P + DH + P * c + P]
                    mm = nc.tensor.matmul(ps[:, i, :], w, big[:, c, half(i)], start=(c == 0), stop=(c == 7))
                mm.then_inc(s[2], 1)

        def l1_attn_pe(pe):
            norm_pe(pe, 2, 2, xT, x_ready(2))
            norm_pe(pe, 3, 3, h1T, norm_ready(2))
            norm_pe(pe, 4, 4, ctxT, norm_ready(3))

            def first(pe):
                pe.wait_ge(ld["w1"], 32)
                pe.wait_ge(n_out, 10)
            mlp_pe(pe, M1, first)
            pe.wait_ge(y1, 2)
            wide_pe(pe, A1a, 0, hT, v1[0])
            norm_pe(pe, 5, 5, h1T, lambda e, i: e.wait_ge(y1, 3 + i))
            pe.wait_ge(n_out, 12)
            wide_pe(pe, A1b, WB, cT, v1[1])

        def l1_attn_act(act):
            norm_act(act, 2, 2, xT, None)
            norm_act(act, 3, 3, h1T, None)
            norm_act(act, 4, 4, ctxT, None)
            mlp_act(act, M1)
            attn_act(act, A1a)
            norm_act(act, 5, 5, h1T, None)
            attn_act(act, A1b)

        def l1_attn_dve(v):
            norm_dve(v, 2, 2, xT, h1T, None)
            norm_dve(v, 3, 3, h1T, hT, col(C_PTB))
            norm_dve(v, 4, 4, ctxT, cT, col(C_CTX))
            mlp_dve(v, M1)
            v.wait_ge(M1.downed, M1.counted + len(M1.units))
            for i in range(2):
                nc.vector.tensor_tensor(h1T[:, half(i)], h1T[:, half(i)], ps[:, i, :], ALU.add).then_inc(y1, 1)
            values_dve(v, None, v1[0][0], v1[0][1], 1, DH)
            attn_dve(v, A1a)
            v.wait_ge(y1, 2)
            for i in range(2):
                v.wait_ge(v1[0][2], i + 1)
                nc.vector.tensor_tensor(h1T[:, half(i)], h1T[:, half(i)], ps[:, i, :], ALU.add).then_inc(y1, 1)
            norm_dve(v, 5, 5, h1T, hT, col(C_CA))
            values_dve(v, None, v1[1][0], v1[1][1], 1, DH)
            attn_dve(v, A1b)
            for i in range(2):
                v.wait_ge(v1[1][2], i + 1)
                residual(v, 2, i, ps[:, i, :], 2, None, None)

        r1 = [sem(f"R1_{x}") for x in ("logits", "shifted", "exped", "chosen", "ranked", "ready")]
        f1 = {x: sem(f"F1_{x}") for x in ("turned", "tokens", "spread", "spread_sb", "hot", "sent", "gathered",
                                          "up", "gelu", "down", "out", "pick", "y")}
        htok = q_st[:, :, :].rearrange("p c s -> p (c s)")[:, 0:N]
        xd = w1[:, 0:SLOTS]
        hot = w1[:, SLOTS:3 * SLOTS].rearrange("p (b s) -> p b s", b=2)
        eo = mA[:, 0:E1 * D]
        slotB, weightB = xc, h1T
        pick = prob[:, :, :, :].rearrange("p a j k -> p (a j k)")[:, 0:4 * HALF].rearrange("p (b n) -> p b n", b=4)
        hg = km[:, :, :].rearrange("p j s -> p (j s)")[:, 0:640].rearrange("p (b n) -> p b n", b=2)
        slot = small[:, 6, :]
        weight = small[:, 7, :]
        chunks = [(0, 512), (512, 1024), (1024, SLOTS)]

        def l1_ffn_pe(pe):
            norm_pe(pe, 6, 6, xT, x_ready(3))
            logits_pe(pe, 6, E0, E1, r1[0])
            for t in range(NT):
                mm = nc.tensor.transpose(ps[:, t // 4, tile(t % 4)], hT[:, tile(t)], ident[:, :])
            mm.then_inc(f1["turned"], 1)
            ranks_pe(pe, E1, r1[3], r1[4])
            pe.wait_ge(r1[5], 1)
            pe.wait_ge(f1["tokens"], 2)
            for w, src in enumerate((slot, weight)):
                for t in range(NT):
                    mm = nc.tensor.matmul(ps[:, (6, 0)[w] + t // 4, tile(t % 4)], src[:, t:t + 1].broadcast_to([P, P]),
                                          ident[:, :], start=True, stop=True)
                mm.then_inc(f1["spread"], 1)
            for t in range(NT):
                pe.wait_ge(f1["hot"], t + 1)
                for c, (lo, hi) in enumerate(chunks):
                    mm = nc.tensor.matmul(ps[:, 2 + c, 0:hi - lo], htok[:, tile(t)], hot[:, t % 2, lo:hi],
                                          start=(t == 0), stop=(t == NT - 1))
                mm.then_inc(f1["sent"], 1)
            pe.wait_ge(f1["gathered"], 3)
            pe.wait_ge(f1["spread_sb"], 4)
            pe.wait_ge(ld["e1"], 32)

            def up(e):
                if e >= 2:
                    pe.wait_ge(f1["gelu"], e - 1)
                for c in range(4):
                    mm = nc.tensor.matmul(ps[:, 6 + e % 2, CAP1 * c:CAP1 * c + CAP1], arena[:, FF1 * e + P * c:FF1 * e + P * c + P],
                                          xd[:, CAP1 * e:CAP1 * e + CAP1], start=True, stop=True)
                mm.then_inc(f1["up"], 1)

            up(0)
            for e in range(E1):
                if e + 1 < E1:
                    up(e + 1)
                pe.wait_ge(f1["gelu"], e + 1)
                if e >= 2:
                    pe.wait_ge(f1["out"], e - 1)
                for c in range(4):
                    w = E1 * FF1 + FF1 * e + P * c
                    mm = nc.tensor.matmul(ps[0:CAP1, e % 2, 0:D], hg[:, e % 2, CAP1 * c:CAP1 * c + CAP1],
                                          arena[:, w:w + P], start=(c == 0), stop=(c == 3))
                mm.then_inc(f1["down"], 1)
            for e in range(E1):
                pe.wait_ge(f1["out"], e + 1)
                for i in range(2):
                    n = 2 * e + i
                    pe.wait_ge(f1["pick"], n + 1)
                    nc.tensor.matmul(ps[:, 2 + i, :], eo[0:CAP1, tile(e)], pick[0:CAP1, n % 4, :],
                                     start=(e == 0), stop=(e == E1 - 1), skip_group_check=True).then_inc(f1["y"], 1)

        def l1_ffn_act(act):
            norm_act(act, 6, 6, xT, None)
            softmax_act(act, E1, r1[1], r1[2])
            act.wait_ge(f1["turned"], 1)
            for i in range(2):
                nc.scalar.copy(htok[:, half(i)], ps[:, i, :]).then_inc(f1["tokens"], 1)
            for w, dst in enumerate((slotB, weightB)):
                act.wait_ge(f1["spread"], w + 1)
                for i in range(2):
                    nc.scalar.copy(dst[:, half(i)], ps[:, (6, 0)[w] + i, :]).then_inc(f1["spread_sb"], 1)
            for e in range(E1):
                act.wait_ge(f1["up"], e + 1)
                if e >= 2:
                    act.wait_ge(f1["down"], e - 1)
                nc.scalar.activation(hg[:, e % 2, :], ps[:, 6 + e % 2, 0:4 * CAP1], ACT.Gelu_apprx_tanh).then_inc(f1["gelu"], 1)

        def l1_ffn_dve(v):
            norm_dve(v, 6, 6, xT, hT, None)
            softmax_dve(v, E1, r1[0], r1[1], r1[2])
            link(v, nc.vector.tensor_copy(lg2[:, :, :], by_tile(ps[:, 4, 0:NT * E1], E1)))
            choose(v, lg2, E1, 1)
            nc.vector.tensor_copy(selb[:, :, :], oh[:, 0, :, :]).then_inc(r1[3], 1)
            link(v, nc.vector.tensor_tensor(lg[:, :, :], lg[:, :, :], oh[:, 0, :, :], ALU.mult))
            link(v, nc.vector.tensor_reduce(weight, lg[:, :, :], X, ALU.add))
            v.wait_ge(r1[4], 1)
            link(v, nc.vector.tensor_tensor(lg2[:, :, :], by_tile(ps[:, 5, 0:NT * E1], E1), oh[:, 0, :, :], ALU.mult))
            link(v, nc.vector.tensor_reduce(small[:, 3, :], lg2[:, :, :], X, ALU.add))
            link(v, nc.vector.tensor_scalar(small[:, 4, :], small[:, 3, :], float(CAP1), 2.0 * SLOTS, ALU.is_ge, ALU.mult))
            link(v, nc.vector.tensor_tensor(small[:, 4, :], small[:, 4, :], small[:, 3, :], ALU.add))
            nc.vector.scalar_tensor_tensor(slot, idxf[:, :, 0], float(CAP1), small[:, 4, :], ALU.mult, ALU.add).then_inc(r1[5], 1)
            v.wait_ge(r1[5], 1)
            for t in range(NT):
                if t >= 2:
                    v.wait_ge(f1["sent"], t - 1)
                nc.vector.tensor_scalar(hot[:, t % 2, :], iota[:, :], slot[:, t:t + 1], None, ALU.is_equal).then_inc(f1["hot"], 1)
            v.wait_ge(f1["sent"], NT)
            for c, (lo, hi) in enumerate(chunks):
                nc.vector.tensor_copy(xd[:, lo:hi], ps[:, 2 + c, 0:hi - lo]).then_inc(f1["gathered"], 1)
            v.wait_ge(narrowed, 2)
            for e in range(E1):
                v.wait_ge(f1["down"], e + 1)
                nc.vector.tensor_copy(eo[0:CAP1, tile(e)], ps[0:CAP1, e % 2, 0:D]).then_inc(f1["out"], 1)
            v.wait_ge(f1["spread_sb"], 4)
            for e in range(E1):
                for i in range(2):
                    n = 2 * e + i
                    if n >= 4:
                        v.wait_ge(f1["y"], n - 3)
                    nc.vector.tensor_scalar(pick[0:CAP1, n % 4, :], slotB[0:CAP1, half(i)], slot_of[0:CAP1, e:e + 1], None,
                                            ALU.is_equal).then_inc(f1["pick"], 1)
            v.wait_ge(f1["y"], 2 * E1)
            for i in range(2):
                link(v, nc.vector.tensor_tensor(weightB[:, half(i)], ps[:, 2 + i, :], weightB[:, half(i)], ALU.mult))
                residual(v, 3, i, weightB[:, half(i)], 3, None, None)

        progs = {"pe": [l0_attn_pe, l0_ffn_pe, l1_attn_pe, l1_ffn_pe],
                 "dve": [l0_attn_dve, l0_ffn_dve, l1_attn_dve, l1_ffn_dve],
                 "act": [l0_attn_act, l0_ffn_act, l1_attn_act, l1_ffn_act]}

        a2 = {x: sem(f"A2_{x}") for x in ("proj", "q", "prod", "kext", "vals", "vtok", "vext", "scored", "maxed",
                                          "exped", "turned", "moved", "weighed", "mixed", "outturned")}
        prod = prob[:, 0, :, :].rearrange("p j k -> p (j k)")
        prob2 = prob[:, 1, :, :].rearrange("p j k -> p (j k)").rearrange("p (b n) -> p b n", b=2)
        pT2 = probT[:, :, 0, 0:S]
        v_tok = arena[:, 0:N].rearrange("p (t n) -> p t n", t=NT)
        v_ext = arena[:, N:2 * N].rearrange("p (t n) -> p t n", t=NT)
        shared2 = arena[:, 2 * N:3 * N]

        def l2_attn_pe(pe):
            norm_pe(pe, 7, 7, xT, x_ready(4))
            pe.wait_ge(ld["w2"], 32)
            for w, src in enumerate((hT, hT, ctxT)):
                for i in range(2):
                    if w == 0:
                        pe.wait_ge(n_out, 15 + i)
                    nc.tensor.matmul(ps[:, 2 * w + i, :], w2x[:, min(w, 1), :], src[:, half(i)],
                                     start=True, stop=True).then_inc(a2["proj"], 1)
            for w, src in enumerate((hT, ctxT)):
                for i in range(2):
                    b = (6, 0)[w] + i
                    if w == 1 and i == 0:
                        pe.wait_ge(a2["q"], 2)
                    for t in range(4):
                        mm = nc.tensor.matmul(ps[:, b, tile(t)], src[:, tile(4 * i + t)], w2x[:, 2, :], start=True, stop=True)
                    mm.then_inc(a2["vals"], 1)
            pe.wait_ge(a2["prod"], 2)
            pe.wait_ge(a2["kext"], 2)
            pe.wait_ge(a2["vext"], 2)
            pe.wait_ge(a2["vtok"], 2)

            def scores(t):
                if t >= 2:
                    pe.wait_ge(a2["exped"], t - 1)
                nc.tensor.matmul(ps[:, t % 2, 0:S], q_all[:, tile(t)], k_all[:, S * (t // 2):S * (t // 2) + S],
                                 start=True, stop=True)
                nc.tensor.matmul(ps[:, t % 2, S:S + 1], prod[:, tile(t)], ones[:, 0:1], start=True, stop=True).then_inc(a2["scored"], 1)

            def out_turn(t):
                pe.wait_ge(a2["mixed"], t + 1)
                nc.tensor.transpose(ps[:, 6 + t // 4, tile(t % 4)], onorm[:, t % 2, 0:P], ident[:, :]).then_inc(a2["outturned"], 1)

            scores(0)
            for t in range(NT):
                if t + 1 < NT:
                    scores(t + 1)
                pe.wait_ge(a2["exped"], t + 1)
                if t >= 2:
                    pe.wait_ge(a2["moved"], t - 1)
                for c in range(2):
                    mm = nc.tensor.transpose(ps[:, 2 + t % 2, tile(c)], prob2[:, t % 2, tile(c)], ident[:, :])
                mm.then_inc(a2["turned"], 1)
                if t >= 1:
                    out_turn(t - 1)
                pe.wait_ge(a2["moved"], t + 1)
                if t >= 2:
                    pe.wait_ge(a2["mixed"], t - 1)
                for c in range(2):
                    mm = nc.tensor.matmul(ps[:, 4 + t % 2, 0:D], pT2[:, t % 2, tile(c)], v_ext[:, 2 * (t // 2) + c, :],
                                          start=(c == 0), stop=(c == 1))
                mm.then_inc(a2["weighed"], 1)
            out_turn(NT - 1)

        def l2_attn_act(act):
            norm_act(act, 7, 7, xT, None)
            for i in range(2):
                act.wait_ge(a2["proj"], 5 + i)
                nc.scalar.activation(k_all[:, half(i)], ps[:, 4 + i, :], ACT.Identity, bias=col(C_BK2)).then_inc(a2["kext"], 1)
            for t in range(NT):
                act.wait_ge(a2["maxed"], t + 1)
                if t >= 2:
                    act.wait_ge(a2["mixed"], t - 1)
                nc.scalar.activation(prob2[:, t % 2, 0:S + 1], ps[:, t % 2, 0:S + 1], ACT.Exp, bias=negmax[:, t % 2, 0:1],
                                     accum_out=rsum[:, t % 2, 0:1]).then_inc(a2["exped"], 1)

        def l2_attn_dve(v):
            norm_dve(v, 7, 7, xT, hT, None)
            for i in range(2):
                v.wait_ge(a2["proj"], 1 + i)
                nc.vector.tensor_scalar(q_all[:, half(i)], ps[:, i, :], col(C_BQ2), None, ALU.add).then_inc(a2["q"], 1)
            for i in range(2):
                v.wait_ge(a2["proj"], 3 + i)
                v.wait_ge(a2["q"], 1 + i)
                nc.vector.scalar_tensor_tensor(prod[:, half(i)], ps[:, 2 + i, :], col(C_BK2), q_all[:, half(i)],
                                               ALU.add, ALU.mult).then_inc(a2["prod"], 1)
            for w, dst in enumerate((v_tok, v_ext)):
                for i in range(2):
                    v.wait_ge(a2["vals"], 2 * w + i + 1)
                    nc.vector.tensor_tensor(dst[:, 4 * i:4 * i + 4, :], ps[:, (6, 0)[w] + i, :].rearrange("p (t n) -> p t n", t=4),
                                            bv[:, 1:2, :].broadcast_to([P, 4, D]), ALU.add).then_inc(a2[("vtok", "vext")[w]], 1)
            v.wait_ge(a2["vtok"], 2)

            def mix(t):
                v.wait_ge(a2["weighed"], t + 1)
                if t >= 2:
                    v.wait_ge(a2["outturned"], t - 1)
                o = onorm[:, t % 2, 0:P]
                link(v, nc.vector.reciprocal(rsum[:, t % 2, 1:2], rsum[:, t % 2, 0:1]))
                link(v, nc.vector.scalar_tensor_tensor(o, v_tok[:, t, :], prob2[:, t % 2, S:S + 1], ps[:, 4 + t % 2, 0:D],
                                                       ALU.mult, ALU.add))
                nc.vector.tensor_scalar(o, o, rsum[:, t % 2, 1:2], None, ALU.mult).then_inc(a2["mixed"], 1)

            for t in range(NT):
                v.wait_ge(a2["scored"], t + 1)
                nc.vector.tensor_reduce(negmax[:, t % 2, 0:1], ps[:, t % 2, 0:S + 1], X, ALU.max, negate=True).then_inc(a2["maxed"], 1)
                if t >= 1:
                    mix(t - 1)
                v.wait_ge(a2["turned"], t + 1)
                nc.vector.tensor_copy(pT2[:, t % 2, :], ps[:, 2 + t % 2, 0:S]).then_inc(a2["moved"], 1)
            mix(NT - 1)
            for i in range(2):
                v.wait_ge(a2["outturned"], 4 * (i + 1))
                residual(v, 4, i, ps[:, 6 + i, :], 4, None, None)

        r2 = [sem(f"R2_{x}") for x in ("logits", "exped", "ready")]
        f2 = {x: sem(f"F2_{x}") for x in ("up", "relu", "square", "scale", "down", "rounded", "summed",
                                          "sup", "srelu", "ssq", "y")}
        sh_up = iota[:, 512:512 + HID2]
        sh_dn = iota[:, 512 + HID2:512 + HID2 + 2 * D].rearrange("p (c n) -> p c n", c=2)
        bfv = big[:, 4:8, :].rearrange("p c t -> p (c t)").bitcast(BF16).rearrange("p (k n) -> p k n", n=HALF)
        xin = [bfv[:, b, :] for b in range(2)]
        hr = [[bfv[:, 2 + 2 * b + c, :] for c in range(2)] for b in range(2)]
        hq = [[bfv[:, 6 + 2 * b + c, :] for c in range(2)] for b in range(2)]
        yb = [bfv[:, 10 + b, :] for b in range(2)]
        sr = [big[:, 2 + c, 0:HALF] for c in range(2)]
        widths = (P, HID2B)
        n2 = 2 * E2

        def l2_ffn_pe(pe):
            norm_pe(pe, 8, 8, xT, x_ready(5))
            logits_pe(pe, 8, E0 + E1, E2, r2[0])
            pe.wait_ge(r2[2], 1)
            pe.wait_ge(narrowed, 2)
            pe.wait_ge(ld["r3"], 16 * len(loads["r3"]))
            for i in range(2):
                if i:
                    pe.wait_ge(f2["ssq"], 2 * i)
                for c in range(2):
                    m = widths[c]
                    nc.tensor.matmul(ps[0:m, 2 + c, :], sh_up[:, P * c:P * c + m], hT[:, half(i)], start=True,
                                     stop=True).then_inc(f2["sup"], 1)
                for c in range(2):
                    m = widths[c]
                    pe.wait_ge(f2["ssq"], 2 * i + c + 1)
                    nc.tensor.matmul(ps[:, i, :], sh_dn[0:m, c, :], sr[c][0:m, :], start=(c == 0), stop=False,
                                     skip_group_check=True).then_inc(f2["y"], 1)

            def spread(n):
                e, i = n // 2, n % 2
                if n >= 2:
                    pe.wait_ge(f2["scale"], n - 1)
                for t in range(4):
                    mm = nc.tensor.matmul(ps[:, 6 + n % 2, tile(t)], comb[:, 4 * i + t, e:e + 1].broadcast_to([P, P]),
                                          ident[:, :], start=True, stop=True)
                mm.then_inc(f2["up"], 1)

            def up(n):
                e = n // 2
                pe.wait_ge(f2["scale"], n + 1)
                if n >= 1:
                    pe.wait_ge(f2["relu"], 2 * n)
                for c in range(2):
                    m = widths[c]
                    mm = nc.tensor.matmul(ps[0:m, 2 + c, :], up2[:, e, P * c:P * c + m], xin[n % 2], start=True, stop=True)
                mm.then_inc(f2["sup"], 1)

            def down(n):
                e = n // 2
                pe.wait_ge(f2["square"], 2 * n + 2)
                if n >= 2:
                    pe.wait_ge(f2["rounded"], n - 1)
                for c in range(2):
                    m = widths[c]
                    mm = nc.tensor.matmul(ps[:, 4 + n % 2, :], dn2[0:m, e, c, :], hq[n % 2][c][0:m, :],
                                          start=(c == 0), stop=(c == 1))
                mm.then_inc(f2["down"], 1)

            def add(n):
                pe.wait_ge(f2["rounded"], n + 1)
                nc.tensor.matmul(ps[:, n % 2, :], identb[:, :], yb[n % 2], start=False, stop=(n >= n2 - 2),
                                 skip_group_check=True).then_inc(f2["summed"], 1)

            pe.wait_ge(f2["ssq"], 4)
            spread(0)
            for n in range(n2 + 2):
                if n + 1 < n2:
                    spread(n + 1)
                if n < n2:
                    up(n)
                if 1 <= n <= n2:
                    down(n - 1)
                if n >= 2:
                    add(n - 2)

        def l2_ffn_act(act):
            norm_act(act, 8, 8, xT, None)
            act.wait_ge(r2[0], 1)
            nc.scalar.activation(lg[:, :, 0:E2], by_tile(ps[:, 4, 0:NT * E2], E2), ACT.Exp, scale=-1.0).then_inc(r2[1], 1)
            for i in range(2):
                for c in range(2):
                    m = widths[c]
                    act.wait_ge(f2["sup"], 2 * i + c + 1)
                    if i:
                        act.wait_ge(f2["y"], c + 1)
                    nc.scalar.activation(sr[c][0:m, :], ps[0:m, 2 + c, :], ACT.Relu).then_inc(f2["srelu"], 1)
            for n in range(n2 + 1):
                if n < n2:
                    act.wait_ge(f2["sup"], 4 + n + 1)
                    if n >= 2:
                        act.wait_ge(f2["square"], 2 * (n - 1))
                    for c in range(2):
                        m = widths[c]
                        nc.scalar.activation(hr[n % 2][c][0:m, :], ps[0:m, 2 + c, :], ACT.Relu).then_inc(f2["relu"], 1)
                if n >= 1:
                    act.wait_ge(f2["down"], n)
                    if n >= 3:
                        act.wait_ge(f2["summed"], n - 2)
                    nc.scalar.copy(yb[(n - 1) % 2], ps[:, 4 + (n - 1) % 2, :]).then_inc(f2["rounded"], 1)

        def l2_ffn_dve(v):
            norm_dve(v, 8, 8, xT, hT, None)
            v.wait_ge(r2[1], 1)
            link(v, nc.vector.tensor_scalar(lg[:, :, 0:E2], lg[:, :, 0:E2], 1.0, None, ALU.add))
            link(v, nc.vector.reciprocal(lg[:, :, 0:E2], lg[:, :, 0:E2]))
            link(v, nc.vector.tensor_tensor(lg2[:, :, 0:E2], lg[:, :, 0:E2],
                                            ebias[:, :].unsqueeze(1).broadcast_to([P, NT, E2]), ALU.add))
            choose(v, lg2, E2, 2)
            nc.vector.tensor_tensor(comb[:, :, 0:E2], lg[:, :, 0:E2], oh[:, 2, :, 0:E2], ALU.mult).then_inc(r2[2], 1)
            for i in range(2):
                for c in range(2):
                    m = widths[c]
                    v.wait_ge(f2["srelu"], 2 * i + c + 1)
                    nc.vector.tensor_tensor(sr[c][0:m, :], sr[c][0:m, :], sr[c][0:m, :], ALU.mult).then_inc(f2["ssq"], 1)

            def scale(n):
                v.wait_ge(f2["up"], n + 1)
                if n >= 2:
                    v.wait_ge(f2["sup"], 4 + n - 1)
                nc.vector.tensor_tensor(xin[n % 2], hT[:, half(n % 2)], ps[:, 6 + n % 2, :], ALU.mult).then_inc(f2["scale"], 1)

            scale(0)
            for n in range(n2):
                if n + 1 < n2:
                    scale(n + 1)
                if n >= 2:
                    v.wait_ge(f2["down"], n - 1)
                for c in range(2):
                    m = widths[c]
                    v.wait_ge(f2["relu"], 2 * n + c + 1)
                    nc.vector.tensor_tensor(hq[n % 2][c][0:m, :], hr[n % 2][c][0:m, :], hr[n % 2][c][0:m, :],
                                            ALU.mult).then_inc(f2["square"], 1)
            v.wait_ge(f2["summed"], n2)
            for i in range(2):
                residual(v, 5, i, ps[:, i, :], 5, None, None)

        a3 = {x: sem(f"A3_{x}") for x in ("proj", "q", "v", "v_done", "km", "spreadq", "rk", "rk_sb", "rv", "rv_sb",
                                          "rt", "rn", "ro", "att", "o")}
        rel = arena[:, :].rearrange("p (c h q) -> p c h q", c=2, h=B * H)
        qd = q_st[:, :, :].rearrange("p c s -> p (c s)").rearrange("p (h q) -> p h q", q=32)
        relk = iota[:, 0:2 * S - 1]
        relv = w1[:, 0:2 * S * HD].rearrange("p (c q d) -> p c q d", c=2, q=S)
        km_all = mA[:, 0:4 * N].rearrange("p (j n) -> p j n", j=4)
        rv1 = w1[:, 4096:4480]
        A3x = attention(HD, False, 2, 16, 0, 0, False)
        A3x.rslot = lambda g: g

        def score3(jp, it, u, o, nk):
            b, g = u // 4, u % 4
            last = nc.tensor.matmul(o, q_all[32 * g:32 * g + 32, S * b + P * it:S * b + P * it + P],
                                    km_all[32 * g:32 * g + 32, 2 * jp:2 * jp + 2, S * b:S * b + S],
                                    start=True, stop=True)
            for s in range(2):
                for c in range(2):
                    last = nc.tensor.matmul(o[:, s, tile(c)], rel[:, c, H * b + 4 * g + 2 * jp + s, :], ident[:, :],
                                            start=False, stop=True, skip_group_check=True)
            return last

        def value3(it, u, c, j):
            h = 4 * (u % 4) + j
            return v_all[:, 2 * (u // 4) + c, h * (HD + 1):(h + 1) * (HD + 1)]

        A3x.score, A3x.value = score3, value3
        A3x.probT = lambda it, u, c, j: rel[:, c, 4 * u + j, :]
        A3x.moved_to = lambda it, u, c: rel[:, c, 4 * u:4 * u + 4, :]
        A3x.moved_from = lambda c: ps[:, 4 + c, :].rearrange("p (j q) -> p j q", j=4)
        A3x.output = lambda it, g: att[:, S * g + P * it:S * g + P * it + P]

        def rel_scores_pe(pe, it):
            pe.wait_ge(a3["spreadq"], 16 * 64 * (it + 1))
            for o in range(16):
                for c in range(2):
                    n = 32 * it + 2 * o + c
                    if n >= 8:
                        pe.wait_ge(a3["rk_sb"], n - 7)
                    for q8 in range(8):
                        q = 8 * o + q8
                        r = slice(32 * (q // 32), 32 * (q // 32) + HD)
                        m = P * c - (P * it + q) + S - 1
                        mm = nc.tensor.matmul(ps[:, n % 8, q8:HALF:8], relk[r, m:m + P], qd[r, :, q % 32],
                                              start=True, stop=True)
                    mm.then_inc(a3["rk"], 1)
            pe.wait_ge(a3["rk_sb"], 32 * (it + 1))

        def rel_scores_move(eng, copy, it, c):
            for o in range(16):
                n = 32 * it + 2 * o + c
                eng.wait_ge(a3["rk"], n + 1)
                if n:
                    eng.wait_ge(a3["rk_sb"], n)
                copy(rel[:, c, :, 8 * o:8 * o + 8], ps[:, n % 8, :].rearrange("p (h q) -> p h q", q=8)).then_inc(a3["rk_sb"], 1)

        def rel_values_pe(pe, it):
            until(pe, A3x.stored, 4 * (it + 1))
            for q in range(P):
                for c in range(2):
                    mm = nc.tensor.matmul(ps[0:B * H, q // 64, HD * (q % 64):HD * (q % 64) + HD], rel[:, c, :, q],
                                          relv[:, c, P * it + q, :], start=(c == 0), stop=(c == 1))
                if q % 64 == 63:
                    mm.then_inc(a3["rv"], 1)
            pe.wait_ge(a3["rv_sb"], 2 * (it + 1))
            for d in range(HD):
                mm = nc.tensor.transpose(ps[:, 2, 64 * d:64 * d + 64], rv_sb[0:64, d:N:HD], ident[0:64, 0:64])
            mm.then_inc(a3["rt"], 1)
            pe.wait_ge(a3["rn"], it + 1)
            for b in range(B):
                mm = nc.tensor.transpose(ps[:, 3, tile(b)], rn_sb[:, tile(b)], ident[:, :])
            mm.then_inc(a3["ro"], 1)
            pe.wait_ge(a3["att"], it + 1)

        rv_sb = h1T
        rn_sb = sq[:, 0:HALF]

        def rel_values_dve(v, it):
            for i in range(2):
                v.wait_ge(a3["rv"], 2 * it + i + 1)
                nc.vector.tensor_copy(rv_sb[0:64, half(i)], ps[0:64, i, :]).then_inc(a3["rv_sb"], 1)
            v.wait_ge(a3["rt"], it + 1)
            until(v, A3x.inverted, 4 * (it + 1))
            for b in range(B):
                ins = nc.vector.tensor_tensor(
                    rn_sb[:, tile(b)].rearrange("p (h d) -> p h d", d=HD),
                    ps[:, 2, :].rearrange("p (d b h) -> p b h d", d=HD, b=B)[:, b, :, :],
                    rsum[:, b, :].unsqueeze(2).broadcast_to([P, H, HD]), ALU.mult)
            ins.then_inc(a3["rn"], 1)
            v.wait_ge(a3["ro"], it + 1)
            until(v, A3x.stored, 4 * (it + 1))
            o = att[:, :].rearrange("p (b s) -> p b s", b=B)[:, :, tile(it)]
            nc.vector.tensor_tensor(o, o, ps[:, 3, :].rearrange("p (b s) -> p b s", b=B), ALU.add).then_inc(a3["att"], 1)

        A3x.before_pe, A3x.after_pe = rel_scores_pe, rel_values_pe
        A3x.before_dve = lambda v, it: rel_scores_move(v, nc.vector.tensor_copy, it, 0)
        A3x.before_act = lambda act, it: rel_scores_move(act, nc.scalar.copy, it, 1)
        A3x.after_dve = rel_values_dve

        def l3_attn_pe(pe):
            norm_pe(pe, 9, 9, xT, x_ready(6))
            for w, src in enumerate((hT, ctxT)):
                for i in range(2):
                    if w == 0:
                        pe.wait_ge(n_out, 19 + i)
                    nc.tensor.matmul(ps[:, 2 * w + i, :], w3x[:, w, :], src[:, half(i)], start=True, stop=True).then_inc(a3["proj"], 1)
            pe.wait_ge(a3["q"], 2)
            for t in range(NT):
                mm = nc.tensor.matmul(ps[:, t // 4, tile(t % 4)], ctxT[:, tile(t)], w3x[:, 2, :], start=True, stop=True)
            mm.then_inc(a3["v"], 1)
            pe.wait_ge(a3["v_done"], 1 + NT)
            pe.wait_ge(a3["km"], 8)
            attn_pe(pe, A3x)
            for i in range(2):
                nc.tensor.matmul(ps[:, i, :], w3x[:, 3, :], att[:, half(i)], start=True, stop=True).then_inc(a3["o"], 1)

        def l3_attn_dve(v):
            norm_dve(v, 9, 9, xT, hT, None)
            for i in range(2):
                v.wait_ge(a3["proj"], 1 + i)
                nc.vector.tensor_scalar(q_all[:, half(i)], ps[:, i, :], col(C_BQ3), HD ** -0.5, ALU.add, ALU.mult).then_inc(a3["q"], 1)
            for i in range(2):
                v.wait_ge(a3["proj"], 3 + i)
                for j in range(4):
                    nc.vector.tensor_scalar(km_all[:, j, half(i)], ps[:, 2 + i, :], col(C_BK3), hmask[:, j:j + 1],
                                            ALU.add, ALU.mult).then_inc(a3["km"], 1)
            values_dve(v, 2, a3["v"], a3["v_done"], H, HD)
            attn_dve(v, A3x)
            for i in range(2):
                v.wait_ge(a3["o"], i + 1)
                residual(v, 6, i, ps[:, i, :], 6, col(C_BO3), a_sb[:, i, :])

        def l3_attn_act(act):
            norm_act(act, 9, 9, xT, None)
            attn_act(act, A3x)

        def l3_attn_sp(sp):
            for it in range(2):
                if it == 0:
                    sp.wait_ge(a3["q"], 2)
                else:
                    sp.wait_ge(a3["rk"], 32)
                for h in range(H):
                    for c in range(4):
                        src = q_all[HD * h:HD * h + HD, :].rearrange("p (b s) -> p b s", b=B)[:, :, P * it + 32 * c:P * it + 32 * c + 32]
                        dst = qd[32 * c:32 * c + HD, h:B * H:H, :]
                        sp.dma_start(dst, src).then_inc(a3["spreadq"], 16)

        w3f = w0[:, :, :].rearrange("p w n -> p (w n)")
        A3f = narrow(True, value_grouped)
        s3 = {x: sem(f"F3_{x}") for x in ("qk", "qk_done", "t", "v", "v_done", "o", "x2")}
        r3 = [sem(f"R3_{x}") for x in ("logits", "shifted", "exped", "ready")]
        M3 = Mlp(28, 0, E3, 2, True)

        def l3_ffn_pe(pe):
            norm_pe(pe, 10, 10, xT, x_ready(7))
            norm_pe(pe, 11, None, h1T, None)
            pe.wait_ge(ld["w3"], 16)
            rope_pe(pe, w3f[:, 0:4 * D].rearrange("p (w n) -> p w n", w=4), 0, None, norm_ready(11), s3["qk"], True)
            pe.wait_ge(s3["qk_done"], 4)
            for t in range(NT):
                mm = nc.tensor.matmul(ps[:, t // 4, (t % 4) * P:(t % 4) * P + 32], hT[:, tile(t)], w3f[:, 4 * D:4 * D + 32],
                                      start=True, stop=True)
            mm.then_inc(s3["v"], 1)
            attn_pe(pe, A3f)
            for i in range(2):
                until(pe, A3f.stored, 8)
                nc.tensor.matmul(ps[:, i, :], w3f[:, 4 * D + 32:5 * D + 32], att[:, half(i)], start=True, stop=True).then_inc(s3["o"], 1)
            norm_pe(pe, 12, None, h1T, None)
            logits_pe(pe, 12, E0 + E1 + E2, E3, r3[0])

            def first(pe):
                pe.wait_ge(ld["m3"], 16)
                pe.wait_ge(r3[3], 1)
            mlp_pe(pe, M3, first)

        def l3_ffn_act(act):
            norm_act(act, 10, 10, xT, None)
            norm_act(act, 11, None, h1T, norm_ready(10))
            attn_act(act, A3f)
            norm_act(act, 12, None, h1T, lambda e, i: e.wait_ge(s3["x2"], i + 1))
            softmax_act(act, E3, r3[1], r3[2])
            mlp_act(act, M3)

        def l3_ffn_dve(v):
            norm_dve(v, 10, 10, xT, h1T, None)
            norm_dve(v, 11, None, h1T, hT, col(C_LN1))
            rope_dve(v, s3["qk"], s3["qk_done"], [0.0, 0.0, 0.0, 0.0], s3["t"])
            v.wait_ge(s3["qk_done"], 4)
            values_dve(v, None, s3["v"], s3["v_done"], 4, HD)
            v.wait_ge(s3["v_done"], 1 + NT)
            attn_dve(v, A3f)
            for i in range(2):
                v.wait_ge(s3["o"], i + 1)
                nc.vector.tensor_tensor(h1T[:, half(i)], h1T[:, half(i)], ps[:, i, :], ALU.add).then_inc(s3["x2"], 1)
            norm_dve(v, 12, None, h1T, hT, col(C_LN2))
            softmax_dve(v, E3, r3[0], r3[1], r3[2])
            choose(v, lg, E3, 2)
            link(v, nc.vector.tensor_tensor(small[:, 3, :], top8[:, :, 0], top8[:, :, 1], ALU.add))
            link(v, nc.vector.reciprocal(small[:, 4, :], small[:, 3, :]))
            link(v, nc.vector.tensor_tensor(lg[:, :, 0:E3], lg[:, :, 0:E3],
                                            small[:, 4, :].unsqueeze(2).broadcast_to([P, NT, E3]), ALU.mult))
            nc.vector.tensor_tensor(comb[:, :, 0:E3], lg[:, :, 0:E3], oh[:, 2, :, 0:E3], ALU.mult).then_inc(r3[3], 1)
            mlp_dve(v, M3)
            v.wait_ge(M3.downed, M3.counted + len(M3.units))
            for i in range(2):
                link(v, nc.vector.tensor_tensor(h1T[:, half(i)], h1T[:, half(i)], ps[:, i, :], ALU.add))
                residual(v, 7, i, h1T[:, half(i)], 7, None, None)

        progs["pe"] += [l2_attn_pe, l2_ffn_pe, l3_attn_pe, l3_ffn_pe]
        progs["dve"] += [l2_attn_dve, l2_ffn_dve, l3_attn_dve, l3_ffn_dve]
        progs["act"] += [l2_attn_act, l2_ffn_act, l3_attn_act, l3_ffn_act]

        block = ctx.enter_context(nc.Block())

        @block.sync
        def _(sp):
            def load(*groups):
                for group in groups:
                    for dst, src in loads[group]:
                        sp.dma_start(dst, src).then_inc(ld[group], 16)

            load("c", "x", "w0", "m0", "w1", "w2", "e1a")
            if STAGES > 1:
                sp.wait_ge(x_done, 4)
                load("f2", "w3")
            if STAGES > 3:
                sp.wait_ge(x_done, 6)
                load("e1b")
            if STAGES > 5:
                sp.wait_ge(x_done, 8)
                load("r3")
            if STAGES > 6:
                l3_attn_sp(sp)
            if STAGES > 7:
                until(sp, A3x.scored, 32)
                load("m3")
            for i in range(2):
                sp.wait_ge(x_done, 2 * STAGES - 1 + i)
                sp.dma_start(out[:, half(i)], xT[:, half(i)]).then_inc(ld["out"], 16)
            sp.wait_ge(ld["out"], 32)

        @block.gpsimd
        def _(pool):
            if STAGES > 1:
                pool.wait_ge(ld["f2"], 32)
                nc.gpsimd.tensor_copy(up2[:, :, :].rearrange("p e n -> p (e n)"), mA[:, 0:E2 * HID2]).then_inc(narrowed, 1)
                nc.gpsimd.tensor_copy(dn2[:, :, :, :].rearrange("p e c n -> p (e c n)"),
                                      mA[:, E2 * HID2:E2 * HID2 + E2 * 2 * D]).then_inc(narrowed, 1)

        @block.tensor
        def _(pe):
            for f in progs["pe"][0:STAGES]:
                f(pe)

        @block.vector
        def _(v):
            for f in progs["dve"][0:STAGES]:
                f(v)

        @block.scalar
        def _(act):
            for f in progs["act"][0:STAGES]:
                f(act)


_TURN = [8 * (e // 8) + (e % 8 + 4) % 8 for e in range(D)]

_REL_ROWS = [int(np.clip(-(m - (S - 1)), -REL, REL)) + REL for m in range(2 * S - 1)]
_REL_IDS = np.clip(np.arange(S)[:, None] - np.arange(S)[None, :], -REL, REL).T.reshape(2, P, S) + REL


def constants():
    i = np.arange(P)
    inv = (1.0 / 10000.0 ** (np.arange(0, HD, 2, dtype=np.float32) / HD)).astype(np.float32)
    ang = np.arange(S, dtype=np.float32)[:, None] * inv[None, :]
    cos, sin = np.cos(ang), np.sin(ang)
    e = i % HD
    c = cos[:, e % 4].T
    s = sin[:, e % 4].T * np.where(e < 4, -1.0, 1.0)[:, None]
    scale = HD ** -0.5
    return {
        "ident": np.eye(P),
        "meaner": np.full((P, P), 1.0 / P),
        "before": (i[:, None] < i[None, :]),
        "causal": np.where(i[:, None] >= i[None, :], 0.0, NEG),
        "hmask": (i[:, None] % 32 // HD == np.arange(4)[None, :]),
        "rope": np.stack([c, s, c * scale, s * scale], 1),
        "iota": np.arange(SLOTS)[None],
        "slot_of": i[:, None] + CAP1 * np.arange(E1)[None, :],
    }


def kernel(**inputs):
    import concourse.bacc as _bacc
    from concourse.bass_utils import run_bass_kernel_spmd as _run

    w = {k: np.asarray(v) for k, v in inputs.items()}
    c = {k: np.ascontiguousarray(v, dtype=np.float32) for k, v in constants().items()}
    zero = np.zeros(D, np.float32)
    c["xT"] = w["x"].reshape(N, D).T
    c["ctxT"] = w["ctx_1024"].reshape(N, D).T
    c["gates"] = np.stack([w["g_xattn"], w["g_ffn"]], 1).reshape(1, 8)
    p = w["L0_xattn_Wq"], w["L0_xattn_Wk"]
    c["w0"] = np.stack([p[0].T, p[0][_TURN].T, p[1].T, p[1][_TURN].T, w["L0_xattn_Wv"].T, w["L0_xattn_Wo"].T], 1)
    c["cols"] = np.stack([
        w["L0_xattn_bq"], w["L0_xattn_bq"][_TURN], w["L0_xattn_bk"], w["L0_xattn_bk"][_TURN], w["L0_xattn_bo"],
        w["L1_xattn_ptb_gamma"], w["L1_xattn_ca_gamma"], w["L1_xattn_ca_ctx_gamma"],
        w["L2_xattn_bq"], w["L2_xattn_bk"], w["L3_xattn_bq"], w["L3_xattn_bk"], w["L3_xattn_bo"],
        w["L3_ffn_ln1_w"], w["L3_ffn_ln2_w"]] + [zero] * 17, 1)
    c["bv"] = np.stack([w["L0_xattn_bv"], w["L2_xattn_bv"], w["L3_xattn_bv"]])[None]
    c["gw"] = np.concatenate([w["L0_ffn_gate_w"], w["L1_ffn_gate_w"], w["L2_ffn_gate_w"], w["L3_ffn_gate_w"]]).T
    c["ebias"] = w["L2_ffn_expert_bias"][None]

    def lhs(x):
        return x.transpose(2, 0, 1)

    m0 = [np.concatenate([w["L0_ffn_we_gate"], w["L0_ffn_ws_gate"].reshape(2, P, D)]),
          np.concatenate([w["L0_ffn_we_up"], w["L0_ffn_ws_up"].reshape(2, P, D)]),
          np.concatenate([w["L0_ffn_we_down"], w["L0_ffn_ws_down"].reshape(D, 2, P).transpose(1, 0, 2)])]
    c["m0"] = np.stack([lhs(m) for m in m0], 2).reshape(P, -1)
    fu, wq = w["L1_xattn_W_fused"], w["L1_xattn_W_q"]

    def attn1(q, kv, o):
        k, v = kv[:, :DH], kv[:, DH:]
        return [q, k, k, v, o.reshape(8, P, D).transpose(1, 0, 2).reshape(P, -1)]

    ff = fu[:, H * DH + 2 * DH:]
    c["w1"] = np.concatenate(
        attn1(fu[:, :H * DH], fu[:, H * DH:H * DH + 2 * DH], w["L1_xattn_W_attn_out"])
        + attn1(wq, w["L1_xattn_W_kv"], w["L1_xattn_W_out"]), 1)
    parts = [np.stack([ff[:, HALF + P * e:HALF + P * e + P], ff[:, P * e:P * e + P],
                       w["L1_xattn_W_ff_out"][P * e:P * e + P]], 1) for e in range(4)]
    c["m1"] = np.stack(parts, 1).reshape(P, -1)
    c["e1"] = np.concatenate([w["L1_ffn_w1"].transpose(1, 0, 2).reshape(P, -1),
                              w["L1_ffn_w2"].reshape(E1, 4, P, D).transpose(2, 0, 1, 3).reshape(P, -1)], 1)
    c["w2x"] = np.stack([w["L2_xattn_Wq"], w["L2_xattn_Wk"], w["L2_xattn_Wv"]], 1)
    c["up2"] = lhs(w["L2_ffn_w_up"])
    dn = np.zeros((E2, 2, P, D), np.float32)
    dn[:, 0] = w["L2_ffn_w_down"].transpose(0, 2, 1)[:, :P]
    dn[:, 1, :HID2B] = w["L2_ffn_w_down"].transpose(0, 2, 1)[:, P:]
    c["dn2"] = dn.transpose(2, 0, 1, 3)
    sd = np.zeros((2, P, D), np.float32)
    sd[0] = w["L2_ffn_shared_w_down"].T[:P]
    sd[1, :HID2B] = w["L2_ffn_shared_w_down"].T[P:]
    c["sh2"] = np.concatenate([w["L2_ffn_shared_w_up"].T, sd[0], sd[1]], 1)
    c["w3x"] = np.stack([w["L3_xattn_Wq"], w["L3_xattn_Wk"], w["L3_xattn_Wv"], w["L3_xattn_Wo"]], 1)


    c["relk"] = w["L3_xattn_rel_key_table"][_REL_ROWS].T
    c["relv"] = w["L3_xattn_rel_value_table"][_REL_IDS].transpose(1, 0, 2, 3)
    f = w["L3_ffn_wqkv"]
    q, k, v = f[:D], f[D:D + 32], f[D + 32:]
    kx = k.reshape(4, 1, HD, D).repeat(4, 1).reshape(D, D)
    c["w3f"] = np.concatenate([q.T, q[_TURN].T, kx.T, kx[_TURN].T, v.T, w["L3_ffn_wo"].T], 1)
    w13, w2 = w["L3_ffn_w13"], w["L3_ffn_w2"]
    m3 = np.stack([np.stack([w13[:, P * j:P * j + P], w13[:, 256 + P * j:256 + P * j + P], w2[:, :, P * j:P * j + P]], 1)
                   for j in range(2)], 1)
    c["m3"] = m3.transpose(4, 0, 1, 2, 3).reshape(P, -1)

    nc = _bacc.Bacc("TRN2", target_bir_lowering=False, num_devices=1)
    arrays, args = {}, {}
    for name, x in c.items():
        x = np.ascontiguousarray(x)
        arrays[f"in_{name}"] = x
        args[name] = nc.dram_tensor(f"in_{name}", x.shape, mybir.dt.from_np(x.dtype), kind="ExternalInput").ap()
    out = nc.dram_tensor("out_0", (D, N), F32, kind="ExternalOutput").ap()
    build(nc, args, out)
    r = _run(nc, [arrays], core_ids=[0])
    return np.ascontiguousarray(r.results[0]["out_0"].T).reshape(B, S, D)
```

```python
from contextlib import ExitStack

import numpy as np

import concourse.bass as bass
from concourse import mybir

F32 = mybir.dt.float32
BF16 = mybir.dt.bfloat16
U32 = mybir.dt.uint32
ALU = mybir.AluOpType
ACT = mybir.ActivationFunctionType
X = mybir.AxisListType.X

B, S, D = 4, 256, 128
N = B * S
P = 128
NT = N // P
HALF = 512
H = 16
HD = D // H
DH = 64
E0, E1, E2, E3 = 8, 16, 8, 8
CAP0, CAP1 = 320, 80
FF1 = 512
HID2 = 176
HID2B = HID2 - P
REL = 128
EPS = 1e-5
SLOTS = E1 * CAP1
UNITS = 8
NEG = -3.0e38
STAGES = 8


def half(i):
    return slice(HALF * i, HALF * (i + 1))


def tile(t):
    return slice(P * t, P * (t + 1))


class Counted:

    def __init__(self, sem, past):
        self.sem, self.past = sem, past


def until(eng, counted, n):
    eng.wait_ge(counted.sem, n + counted.past)


class Attention:

    def __init__(self, sems, totals, width, causal, iters, units, staged_by, projected_by):
        self.width, self.causal, self.iters, self.units = width, causal, iters, units
        self.per_group = 4 if width == HD else 1
        self.groups = units // self.per_group
        self.staged_by = staged_by

        def counted(what, per_iteration):
            c = Counted(sems[what], totals.get(what, 0))
            totals[what] = c.past + per_iteration * iters
            return c

        self.staged = counted("staged", staged_by)
        self.projected = counted("projected", projected_by)
        self.scored = counted("scored", units)
        self.maxed = counted("maxed", units)
        self.exped = counted("exped", units)
        self.turned = [counted(f"turned{c}", self.count(c, units)) for c in range(2)]
        self.moved = [counted(f"moved{c}", self.count(c, units)) for c in range(2)]
        self.weighed = counted("weighed", units)
        self.inverted = counted("inverted", self.groups)
        self.widened = counted("widened", self.groups)
        self.spread = counted("spread", self.groups)
        self.spread_sb = counted("spread_sb", self.groups)
        self.normed = counted("normed", self.groups)
        outs = self.groups if width == HD else 0
        self.outed = counted("outed", outs)
        self.stored = counted("stored", outs)

    def qt(self, u):
        return u // 4 % 2

    def key_tiles(self, u):
        return 1 if self.causal and self.qt(u) == 0 else 2

    def count(self, c, u):
        return sum(1 for v in range(u) if c < self.key_tiles(v))

    def ends_group(self, u):
        return u >= 0 and (u + 1) % self.per_group == 0


def wait_count(eng, sem, per, it, n):
    if isinstance(it, int):
        if per * it + n > 0:
            until(eng, sem, per * it + n)
    elif n > 0:
        until(eng, sem, it * per + n)


def build(nc, a, out, qscratch):
    ctx = ExitStack()
    with ctx:
        def sb(name, shape, dt=F32):
            return ctx.enter_context(nc.sbuf_tensor(name, shape, dt))

        def sem(name):
            return ctx.enter_context(nc.semaphore(name))

        ps = ctx.enter_context(nc.psum_tensor("ps", [P, 8, HALF], F32))

        xT = sb("xT", [P, N])
        ctxT = sb("ctxT", [P, N])
        hT = sb("hT", [P, N])
        h1T = sb("h1T", [P, N])
        sq = sb("sq", [P, N])
        xc = sb("xc", [P, N])
        ident = sb("ident", [P, P])
        identb = sb("identb", [P, P], BF16)
        meaner = sb("meaner", [P, P])
        beforeb = sb("beforeb", [P, P], BF16)
        ones = sb("ones", [P, 1])
        onesb = sb("onesb", [P, P], BF16)
        zerob = sb("zerob", [P, HALF], BF16)
        causalb = sb("causalb", [P, P], BF16)
        cols = sb("cols", [P, 32])
        hmask = sb("hmask", [P, 4])
        smask = sb("smask", [P, 3])
        rope = sb("rope", [P, 4, S])
        gates = sb("gates", [P, 8])
        iota = sb("iota", [P, SLOTS])
        iota_e = sb("iota_e", [P, E1])
        slot_of = sb("slot_of", [P, E1])
        eps = sb("eps", [P, 1])
        std = sb("std", [P, NT])
        rstd = sb("rstd", [P, NT])

        w0 = sb("w0", [P, 9, D])
        bv = sb("bv", [P, 3, D])
        w2x = sb("w2x", [P, 3, D])
        w3x = sb("w3x", [P, 8, D])
        gw = sb("gw", [P, E0 + E1 + E2 + E3])
        ebias = sb("ebias", [P, E2])
        mA = sb("mA", [P, 48 * D])
        WA1 = 8 * D
        w1 = sb("w1", [P, 8 * D + D + DH + 8 * D + 8 * D + D + DH + 8 * D])
        up2 = sb("up2", [P, E2, HID2], BF16)
        dn2 = sb("dn2", [P, E2, 2, D], BF16)
        arena = sb("arena", [P, 2 * E1 * FF1])
        q_all = sb("q_all", [P, N])
        k_all = sb("k_all", [P, N])
        q_st = sb("q_st", [P, 8, S])
        km = sb("km", [P, 4, S])
        v_all = sb("v_all", [P, NT, D])
        v_st = sb("v_st", [P, 2, D])
        prob = sb("prob", [P, 2, 4, S])
        probT = sb("probT", [P, 2, 2, HALF])
        negmax = sb("negmax", [P, 2, 4])
        rsum = sb("rsum", [P, 4, H])
        onorm = sb("onorm", [P, HALF])
        before, causal = onorm[:, 0:P], onorm[:, P:2 * P]
        sums = sb("sums", [P, 4, H])
        rspread = sq[:, :].rearrange("p (g q) -> p g q", g=2)
        big = arena[:, E1 * FF1:].rearrange("p (c t) -> p c t", c=8)
        att = xc
        lg = sb("lg", [P, NT, E1])
        lg2 = sb("lg2", [P, NT, E1])
        small = sb("small", [P, 8, NT])
        top8 = sb("top8", [P, NT, 8])
        idx8 = sb("idx8", [P, NT, 8], U32)
        idxf = sb("idxf", [P, NT, 2])
        oh = sb("oh", [P, 3, NT, E1])
        selb = sb("selb", [P, NT, E1], BF16)
        comb = sb("comb", [P, NT, 10])
        g_sb = prob[:, 0, :, :].rearrange("p j k -> p (j k)").rearrange("p (i n) -> p i n", i=2)
        a_sb = prob[:, 1, :, :].rearrange("p j k -> p (j k)").rearrange("p (i n) -> p i n", i=2)
        c_sb = probT[:, 0, :, :]
        d_sb = probT[:, 1, :, :]

        ld = {k: sem("ld_" + k) for k in ("c", "x", "w0", "m0", "w1", "e1", "w2", "f2", "w3", "m3", "r3", "out")}
        ld["e1a"] = ld["e1b"] = ld["e1"]
        narrowed = sem("narrowed")
        n_mean, n_cent, n_sq, n_var, n_std, n_rstd, n_wide, n_out = (
            sem(s) for s in ("n_mean", "n_cent", "n_sq", "n_var", "n_std", "n_rstd", "n_wide", "n_out"))
        x_done = sem("x_done")
        made = sem("made")
        gated = sem("gated")
        chain = sem("chain")
        links = [0]

        loads = {
            "c": [(ident[:, :], a["ident"]), (meaner[:, :], a["meaner"]), (before[:, :], a["before"]),
                  (causal[:, :], a["causal"]), (cols[:, :], a["cols"]), (hmask[:, :], a["hmask"]), (smask[:, :], a["smask"]),
                  (rope[:, :, :], a["rope"]), (gates[:, :], a["gates"].broadcast_to([P, 8])),
                  (iota[:, :], a["iota"].partition_broadcast(P)), (slot_of[:, :], a["slot_of"]),
                  (iota_e[:, :], a["iota"][:, 0:E1].partition_broadcast(P)),
                  (gw[:, :], a["gw"]), (bv[:, :, :], a["bv"].partition_broadcast(P)),
                  (ebias[:, :], a["ebias"].partition_broadcast(P))],
            "x": [(xT[:, :], a["xT"]), (ctxT[:, :], a["ctxT"])],
            "w0": [(w0[:, :, :], a["w0"])],
            "m0": [(mA[:, 0:30 * D], a["m0"])],
            "w1": [(w1[:, :], a["w1"]), (mA[:, 30 * D:42 * D], a["m1"])],
            "e1a": [(arena[:, 0:E1 * FF1], a["e1"][:, 0:E1 * FF1])],
            "e1b": [(arena[:, E1 * FF1:], a["e1"][:, E1 * FF1:])],
            "w2": [(w2x[:, :, :], a["w2x"]), (w3x[:, :, :], a["w3x"])],
            "f2": [(mA[:, 0:E2 * HID2], a["up2"].rearrange("p e n -> p (e n)")),
                   (mA[:, E2 * HID2:E2 * HID2 + E2 * 2 * D], a["dn2"].rearrange("p e c n -> p (e c n)"))],
            "m3": [(mA[:, :], a["m3"])],
            "w3": [(w0[:, :, :].rearrange("p w n -> p (w n)")[:, 0:8 * D + 32], a["w3f"])],
            "r3": [(w1[:, 0:2 * S * HD], a["relv"].rearrange("p c q d -> p (c q d)")),
                   (iota[:, 512:512 + HID2 + 2 * D], a["sh2"])]
                  + [(iota[:, 0:2 * S - 1], a["relk"])],
        }
        C_BQ0, C_BQR0, C_BK0, C_BKR0, C_BO0, C_PTB, C_CA, C_CTX, C_BQ2, C_BK2, C_BQ3, C_BK3, C_BO3, C_LN1, C_LN2 = range(15)

        def col(i):
            return cols[:, i:i + 1]

        def link(eng, ins):
            links[0] += 1
            ins.then_inc(chain, 1)
            eng.wait_ge(chain, links[0])

        def norm_pe(pe, k, km_, src, wait_src):
            for i in range(2):
                if km_ is not None:
                    wait_src(pe, i)
                    nc.tensor.matmul(ps[:, i, :], meaner[:, :], src[:, half(i)], start=True, stop=True).then_inc(n_mean, 1)
            for t in range(NT):
                pe.wait_ge(n_sq, 2 * k + t // 4 + 1)
                mm = nc.tensor.matmul(ps[:, 2, t:t + 1], sq[:, tile(t)], meaner[:, 0:1], start=True, stop=True)
            mm.then_inc(n_var, 1)
            pe.wait_ge(n_rstd, k + 1)
            for t in range(NT):
                mm = nc.tensor.matmul(ps[:, 2 + t // 4, tile(t % 4)], rstd[:, t:t + 1].broadcast_to([P, P]), ident[:, :],
                                      start=True, stop=True)
                if t % 4 == 3:
                    mm.then_inc(n_wide, 1)

        def norm_dve(v, k, km_, src, dst, gamma):
            if k:
                v.wait_ge(n_out, 2 * k)
            for i in range(2):
                if km_ is not None:
                    v.wait_ge(n_mean, 2 * km_ + i + 1)
                    nc.vector.tensor_tensor(xc[:, half(i)], src[:, half(i)], ps[:, i, :], ALU.subtract).then_inc(n_cent, 1)
            cen = xc if km_ is not None else src
            v.wait_ge(n_std, k + 1)
            nc.vector.reciprocal(rstd[:, :], std[:, :]).then_inc(n_rstd, 1)
            for i in range(2):
                v.wait_ge(n_wide, 2 * k + i + 1)
                if gamma is None:
                    nc.vector.tensor_tensor(dst[:, half(i)], cen[:, half(i)], ps[:, 2 + i, :], ALU.mult).then_inc(n_out, 1)
                else:
                    nc.vector.scalar_tensor_tensor(dst[:, half(i)], cen[:, half(i)], gamma, ps[:, 2 + i, :],
                                                   ALU.mult, ALU.mult).then_inc(n_out, 1)

        def norm_act(act, k, km_, src, wait_src):
            for i in range(2):
                if km_ is not None:
                    act.wait_ge(n_cent, 2 * km_ + i + 1)
                    nc.scalar.activation(sq[:, half(i)], xc[:, half(i)], ACT.Square).then_inc(n_sq, 1)
                else:
                    wait_src(act, i)
                    nc.scalar.activation(sq[:, half(i)], src[:, half(i)], ACT.Square).then_inc(n_sq, 1)
            act.wait_ge(n_var, k + 1)
            nc.scalar.activation(std[:, :], ps[:, 2, 0:NT], ACT.Sqrt, bias=eps[:, 0:1]).then_inc(n_std, 1)

        def x_ready(k):
            def wait(eng, i):
                if k == 0:
                    eng.wait_ge(ld["x"], 32)
                    eng.wait_ge(ld["c"], 16 * len(loads["c"]))
                    eng.wait_ge(made, 1)
                else:
                    eng.wait_ge(x_done, 2 * (k - 1) + i + 1)
            return wait

        def norm_ready(k):
            def wait(eng, i):
                eng.wait_ge(n_out, 2 * k + i + 1)
            return wait

        def sc_bank(u, j):
            return 2 * (u % 2) + j // 2

        def scores(pe, A, it, u):
            wait_count(pe, A.exped, A.units, it, max(0, u - 1))
            banks = [ps[:, sc_bank(u, 2 * jp), :].rearrange("p (j k) -> p j k", j=2) for jp in range(2)]
            A.score(it, u, banks, A.key_tiles(u) * P).then_inc(A.scored.sem, 1)

        def turn(pe, A, it, u):
            until(pe, A.exped, it * A.units + u + 1)
            for c in range(A.key_tiles(u)):
                wait_count(pe, A.moved[c], A.count(c, A.units), it, A.count(c, u))
                for j in range(4):
                    last = nc.tensor.transpose(ps[:, 4 + c, tile(j)], prob[:, u % 2, j, tile(c)], ident[:, :])
                last.then_inc(A.turned[c].sem, 1)

        def weigh(pe, A, it, u):
            for c in range(A.key_tiles(u)):
                until(pe, A.moved[c], it * A.count(c, A.units) + A.count(c, u) + 1)
            g = u // A.per_group
            last_c = A.key_tiles(u) - 1
            if A.width == HD:
                if u % 4 == 0:
                    until(pe, A.normed, it * A.groups + g)
                for j in range(4):
                    for c in range(last_c + 1):
                        last = nc.tensor.matmul(ps[32 * j:32 * j + HD, 6, tile(u % 4)], A.value(it, u, c, j),
                                                A.probT(it, u, c, j), start=(c == 0), stop=(c == last_c),
                                                skip_group_check=True)
            else:
                until(pe, A.normed, it * A.groups + max(0, g - 1))
                for c in range(last_c + 1):
                    for p in range(2):
                        last = nc.tensor.matmul(ps[DH * p:DH * p + DH, 6 + u % 2, 0:S], A.value(it, u, c, p),
                                                probT[:, u % 2, c, S * p:S * p + S], start=(c == 0), stop=(c == last_c),
                                                skip_group_check=True)
            last.then_inc(A.weighed.sem, 1)

        def spread(pe, A, it, g):
            until(pe, A.widened, it * A.groups + g + 1)
            if A.width == HD:
                until(pe, A.stored, it * A.groups + g)
                for i in range(4):
                    last = nc.tensor.matmul(ps[:, 7, tile(i)], A.inverse(g)[:, tile(i)], ident[:, :], start=True, stop=True)
            else:
                for i in range(2):
                    last = nc.tensor.matmul(ps[:, 6 + g % 2, S + P * i:S + P * i + P], A.inverse(g)[:, tile(i)], ident[:, :],
                                            start=True, stop=True, skip_group_check=True)
            last.then_inc(A.spread.sem, 1)

        def out_project(pe, A, it, g):
            until(pe, A.normed, it * A.groups + g + 1)
            for i in range(4):
                last = nc.tensor.matmul(ps[:, 7, 0:P], A.wo(i), onorm[:, tile(i)], start=(i == 0), stop=(i == 3))
            last.then_inc(A.outed.sem, 1)

        def batches(eng, A, prologue, iteration):
            prologue()
            with eng.Fori(0, A.iters - 1) as it:
                iteration(it, it + 1)
            iteration(A.iters - 1, None)

        def attn_pe(pe, A):
            def iteration(it, following):
                if A.staged_by:
                    until(pe, A.staged, it * A.staged_by + A.staged_by)
                scores(pe, A, it, 0)
                for u in range(A.units + 3):
                    if u + 1 < A.units:
                        scores(pe, A, it, u + 1)
                    if 1 <= u <= A.units:
                        weigh(pe, A, it, u - 1)
                    if u < A.units:
                        turn(pe, A, it, u)
                    if following is not None and u in (A.units - 1, A.units):
                        A.project(pe, following, u - (A.units - 1))
                    if 1 <= u <= A.units:
                        if A.ends_group(u - 1):
                            spread(pe, A, it, (u - 1) // A.per_group)
                    if A.width == HD and u >= 3 and A.ends_group(u - 3):
                        out_project(pe, A, it, (u - 3) // A.per_group)

            if A.loop:
                def first():
                    A.project(pe, 0, 0)
                    A.project(pe, 0, 1)
                batches(pe, A, first, iteration)
            else:
                for it in range(A.iters):
                    A.before_pe(pe, it)
                    iteration(it, None)
                    A.after_pe(pe, it)
            until(pe, A.stored if A.width == HD else A.normed, A.iters * A.groups)

        def attn_dve(v, A):
            def maxima(it, u):
                until(v, A.scored, it * A.units + u + 1)
                b0 = sc_bank(u, 0)
                s = ps[:, b0:b0 + 2, :].rearrange("p b (j k) -> p (b j) k", j=2)[:, :, 0:A.key_tiles(u) * P]
                nc.vector.tensor_reduce(negmax[:, u % 2, :], s, X, ALU.max, negate=True).then_inc(A.maxed.sem, 1)

            def move(it, u):
                wait_count(v, A.weighed, A.units, it, max(0, u - 1))
                for c in range(A.key_tiles(u)):
                    until(v, A.turned[c], it * A.count(c, A.units) + A.count(c, u) + 1)
                    nc.vector.tensor_copy(A.moved_to(it, u, c), A.moved_from(c)).then_inc(A.moved[c].sem, 1)

            def invert(it, g):
                until(v, A.exped, it * A.units + (g + 1) * A.per_group)
                nh = 4 * A.per_group
                nc.vector.reciprocal(rsum[:, g % 4, 0:nh], sums[:, g % 4, 0:nh]).then_inc(A.inverted.sem, 1)

            def normalise(it, g):
                until(v, A.spread_sb, it * A.groups + g + 1)
                if A.width == HD:
                    wait_count(v, A.outed, A.groups, it, g)
                    until(v, A.weighed, it * A.units + (g + 1) * 4)
                    ins = nc.vector.tensor_tensor(onorm[:, :], ps[:, 6, :], rspread[:, g % 2, :], ALU.mult)
                else:
                    until(v, A.weighed, it * A.units + g + 1)
                    ins = nc.vector.tensor_tensor(A.output(it, g), ps[:, 6 + g % 2, 0:S].rearrange("p (c q) -> p c q", c=2),
                                                  rspread[:, g % 2, 0:S].rearrange("p (c q) -> p c q", c=2), ALU.mult)
                ins.then_inc(A.normed.sem, 1)

            def iteration(it, following):
                for u in range(A.units + 2):
                    if u < A.units:
                        maxima(it, u)
                    if 1 <= u <= A.units:
                        move(it, u - 1)
                        if A.ends_group(u - 1):
                            invert(it, (u - 1) // A.per_group)
                    if following is not None and u == A.units:
                        A.stage(v, following)
                    if A.ends_group(u - 2):
                        normalise(it, (u - 2) // A.per_group)
                if following is not None:
                    A.stage_values(v, following)

            if A.loop:
                def first():
                    A.stage(v, 0)
                    A.stage_values(v, 0)
                batches(v, A, first, iteration)
            else:
                for it in range(A.iters):
                    A.before_dve(v, it)
                    iteration(it, None)
                    A.after_dve(v, it)

        def attn_act(act, A):
            def exps(it, u):
                until(act, A.maxed, it * A.units + u + 1)
                for c in range(2):
                    wait_count(act, A.turned[c], A.count(c, A.units), it, A.count(c, max(0, u - 1)))
                n = A.key_tiles(u) * P
                g, at = u // A.per_group, 4 * (u % A.per_group)
                for j in range(4):
                    s = ps[:, sc_bank(u, j), :].rearrange("p (j k) -> p j k", j=2)[:, j % 2, 0:n]
                    h = at + A.head(j)
                    last = nc.scalar.activation(prob[:, u % 2, j, 0:n], s, ACT.Exp, bias=negmax[:, u % 2, j:j + 1],
                                                accum_out=sums[:, g % 4, h:h + 1])
                last.then_inc(A.exped.sem, 1)

            def widen(it, g):
                until(act, A.inverted, it * A.groups + g + 1)
                wait_count(act, A.spread, A.groups, it, max(0, g - 1))
                nh, w = (H, 32) if A.width == HD else (4, DH)
                nc.scalar.copy(A.inverse(g).rearrange("p (h w) -> p h w", w=w),
                               rsum[:, g % 4, 0:nh].unsqueeze(2).broadcast_to([P, nh, w])).then_inc(A.widened.sem, 1)

            def spread_move(it, g):
                until(act, A.spread, it * A.groups + g + 1)
                wait_count(act, A.normed, A.groups, it, max(0, g - 1))
                src, n = (ps[:, 7, :], HALF) if A.width == HD else (ps[:, 6 + g % 2, S:2 * S], S)
                nc.scalar.copy(rspread[:, g % 2, 0:n], src).then_inc(A.spread_sb.sem, 1)

            def store(it, g):
                until(act, A.outed, it * A.groups + g + 1)
                nc.scalar.copy(A.output(it, g), ps[:, 7, 0:P]).then_inc(A.stored.sem, 1)

            def iteration(it, following):
                for u in range(A.units + 4):
                    if u < A.units:
                        exps(it, u)
                    if 1 <= u <= A.units:
                        if A.ends_group(u - 1):
                            widen(it, (u - 1) // A.per_group)
                    if u < A.units + 2 and A.ends_group(u - 2):
                        spread_move(it, (u - 2) // A.per_group)
                    if following is not None and u == A.units:
                        A.stage_act(act, following)
                    if A.width == HD and A.ends_group(u - 4):
                        store(it, (u - 4) // A.per_group)
            if A.loop:
                batches(act, A, lambda: A.stage_act(act, 0), iteration)
            else:
                for it in range(A.iters):
                    A.before_act(act, it)
                    iteration(it, None)
                    A.after_act(act, it)

        def nothing(*_):
            pass

        attn_sems = {x: sem(f"attn_{x}") for x in ("staged", "projected", "scored", "maxed", "exped", "turned0", "turned1",
                                                   "moved0", "moved1", "weighed", "inverted", "widened", "spread", "spread_sb",
                                                   "normed", "outed", "stored")}
        attn_totals = {"normed": 1, "stored": 1}

        def attention(width, causal, iters, units, staged_by, projected_by, loop):
            A = Attention(attn_sems, attn_totals, width, causal, iters, units, staged_by, projected_by)
            A.loop = loop
            A.inverse = lambda g: km[:, 2 * (g % 2):2 * (g % 2) + 2, :].rearrange("p a s -> p (a s)")
            A.head = lambda j: j
            A.project = A.stage = A.stage_act = A.stage_values = nothing
            A.before_pe = A.after_pe = A.before_dve = A.after_dve = A.before_act = A.after_act = nothing
            A.probT = lambda it, u, c, j: probT[:, u % 2, c, tile(j)]
            A.moved_to = lambda it, u, c: probT[:, u % 2, c, :]
            A.moved_from = lambda c: ps[:, 4 + c, :]
            return A

        def narrow(causal, value, wo):
            A = attention(HD, causal, B, UNITS, 6, 0, True)

            def score(it, u, banks, nk):
                g = u % 4
                for jp, o in enumerate(banks):
                    last = nc.tensor.matmul(o[:, :, 0:nk], q_st[32 * g:32 * g + 32, 0, tile(A.qt(u))],
                                            km[32 * g:32 * g + 32, 2 * jp:2 * jp + 2, 0:nk], start=True, stop=True)
                for o in banks:
                    if causal:
                        last = nc.tensor.matmul(o[:, :, nk - P:nk], identb[:, :],
                                                causalb[:, :].unsqueeze(1).broadcast_to([P, 2, P]),
                                                start=False, stop=True, skip_group_check=True)
                return last

            def stage_values(v, it):
                nc.vector.tensor_copy(v_st[:, :, :], v_all[:, bass.ds(it * 2, 2), :]).then_inc(A.staged.sem, 1)

            def stage_act(act, it):
                nc.scalar.copy(q_st[:, 0, :], q_all[:, bass.ds(it * S, S)]).then_inc(A.staged.sem, 1)

            def stage(v, it):
                for j in range(4):
                    nc.vector.tensor_scalar(km[:, j, :], k_all[:, bass.ds(it * S, S)], hmask[:, j:j + 1], None,
                                            ALU.mult).then_inc(A.staged.sem, 1)

            A.stage = stage
            A.score, A.stage_values, A.stage_act, A.value, A.wo = score, stage_values, stage_act, value, wo
            A.inverse = lambda g: q_st[:, 2 + 2 * (g % 2):4 + 2 * (g % 2), :].rearrange("p a s -> p (a s)")
            A.output = lambda it, g: att[:, bass.ds(it * S + g * P, P)]
            return A

        def value_narrow(it, u, c, j):
            h = 4 * (u % 4) + j
            return v_st[:, c, h * HD:(h + 1) * HD]

        def value_grouped(it, u, c, j):
            h = u % 4
            return v_st[:, c, h * HD:(h + 1) * HD]

        A0 = narrow(False, value_narrow, lambda i: w0[:, 5 + i, :])

        def clear_bank(v):
            nc.vector.memset(ps[:, 6, :], 0.0)

        q0, k0, v0 = sem("L0_qk"), sem("L0_qk_done"), sem("L0_v")
        v0d, t0 = sem("L0_v_done"), sem("L0_t")

        def rope_pe(pe, wt, first, other, wait_h, done, qk_from_h):
            for w in range(4):
                src = hT if w < 2 or qk_from_h else other
                for i in range(2):
                    if w == 0:
                        wait_h(pe, i)
                    nc.tensor.matmul(ps[:, 2 * w + i, :], wt[:, w, :], src[:, half(i)], start=True, stop=True).then_inc(done, 1)

        def rope_dve(v, done, rdy, biases, t):
            for i in range(2):
                for w, dst in ((0, q_all), (2, k_all)):
                    cs = 2 - w
                    v.wait_ge(done, 2 * (w + 1) + i + 1)
                    pair = (a_sb, g_sb) if w == 0 else (c_sb, d_sb)
                    for r, tmp in enumerate(pair):
                        nc.vector.scalar_tensor_tensor(
                            tmp[:, i, :].rearrange("p (b s) -> p b s", b=2),
                            ps[:, 2 * (w + r) + i, :].rearrange("p (b s) -> p b s", b=2),
                            biases[w + r], rope[:, cs + r, :].unsqueeze(1).broadcast_to([P, 2, S]),
                            ALU.add, ALU.mult).then_inc(t, 1)
                    v.wait_ge(t, 4 * i + 2 * (w // 2) + 2)
                    nc.vector.tensor_tensor(dst[:, half(i)], pair[0][:, i, :], pair[1][:, i, :], ALU.add).then_inc(rdy, 1)

        def l0_attn_pe(pe):
            norm_pe(pe, 0, 0, xT, x_ready(0))
            pe.wait_ge(ld["w0"], 16)
            rope_pe(pe, w0, 0, ctxT, norm_ready(0), q0, False)
            pe.wait_ge(k0, 4)
            for t in range(NT):
                mm = nc.tensor.matmul(ps[:, t // 4, tile(t % 4)], ctxT[:, tile(t)], w0[:, 4, :], start=True, stop=True)
            mm.then_inc(v0, 1)
            attn_pe(pe, A0)

        def values_dve(v, layer, done, vd, heads, width):
            v.wait_ge(done, 1)
            n = heads * width
            for i in range(2):
                o = v_all[:, 4 * i:4 * i + 4, 0:n]
                src = ps[:, i, :].rearrange("p (t n) -> p t n", t=4)[:, :, 0:n]
                if layer is None:
                    nc.vector.tensor_copy(o, src).then_inc(vd, 1)
                else:
                    nc.vector.tensor_tensor(o, src, bv[:, layer:layer + 1, 0:n].broadcast_to([P, 4, n]), ALU.add).then_inc(vd, 1)

        def residual(v, k, i, y, gate, bias, tmp):
            if bias is not None:
                link(v, nc.vector.tensor_scalar(tmp, y, bias, None, ALU.add))
                y = tmp
            nc.vector.scalar_tensor_tensor(xT[:, half(i)], y, gates[:, gate:gate + 1], xT[:, half(i)],
                                           ALU.mult, ALU.add).then_inc(x_done, 1)

        def l0_attn_dve(v):
            v.wait_ge(ld["c"], 16 * len(loads["c"]))
            v.sem_inc(attn_sems["normed"], 1)
            nc.vector.memset(eps[:, :], EPS)
            nc.vector.memset(zerob[:, :], 0.0)
            nc.vector.memset(ones[:, :], 1.0)
            nc.vector.memset(onesb[:, :], 1.0)
            nc.vector.tensor_copy(identb[:, :], ident[:, :])
            nc.vector.tensor_copy(beforeb[:, :], before[:, :])
            nc.vector.tensor_copy(causalb[:, :], causal[:, :]).then_inc(made, 1)
            norm_dve(v, 0, 0, xT, hT, None)
            rope_dve(v, q0, k0, [col(C_BQ0), col(C_BQR0), col(C_BK0), col(C_BKR0)], t0)
            v.wait_ge(k0, 4)
            values_dve(v, 0, v0, v0d, H, HD)
            v.wait_ge(v0d, 2)
            clear_bank(v)
            attn_dve(v, A0)
            v.wait_ge(gated, 1)
            for i in range(2):
                until(v, A0.stored, 2 * B)
                residual(v, 0, i, att[:, half(i)], 0, col(C_BO0), a_sb[:, i, :])

        def l0_attn_act(act):
            act.wait_ge(ld["c"], 16 * len(loads["c"]))
            act.sem_inc(attn_sems["stored"], 1)
            nc.scalar.activation(gates[:, :], gates[:, :], ACT.Tanh).then_inc(gated, 1)
            act.wait_ge(made, 1)
            norm_act(act, 0, 0, xT, x_ready(0))
            act.wait_ge(k0, 4)
            attn_act(act, A0)

        def by_tile(ap, e):
            return ap.rearrange("p (t e) -> p t e", e=e)

        def logits_pe(pe, k, first, e, done):
            for t in range(NT):
                pe.wait_ge(n_out, 2 * k + t // 4 + 1)
                mm = nc.tensor.matmul(ps[:, 4, t * e:(t + 1) * e], hT[:, tile(t)], gw[:, first:first + e], start=True, stop=True)
            mm.then_inc(done, 1)

        def softmax_dve(v, e, done, shifted, exped):
            v.wait_ge(done, 1)
            z = by_tile(ps[:, 4, 0:NT * e], e)
            link(v, nc.vector.tensor_reduce(small[:, 0, :], z, X, ALU.max))
            nc.vector.tensor_tensor(lg[:, :, 0:e], z, small[:, 0, :].unsqueeze(2).broadcast_to([P, NT, e]),
                                    ALU.subtract).then_inc(shifted, 1)
            v.wait_ge(exped, 1)
            link(v, nc.vector.tensor_reduce(small[:, 1, :], lg[:, :, 0:e], X, ALU.add))
            link(v, nc.vector.reciprocal(small[:, 2, :], small[:, 1, :]))
            link(v, nc.vector.tensor_tensor(lg[:, :, 0:e], lg[:, :, 0:e],
                                            small[:, 2, :].unsqueeze(2).broadcast_to([P, NT, e]), ALU.mult))

        def softmax_act(act, e, shifted, exped):
            act.wait_ge(shifted, 1)
            nc.scalar.activation(lg[:, :, 0:e], lg[:, :, 0:e], ACT.Exp).then_inc(exped, 1)

        def choose(v, src, e, ks):
            for t in range(NT):
                ins = nc.vector.max(top8[:, t, :], src[:, t, 0:e])
            link(v, ins)
            for t in range(NT):
                ins = nc.vector.max_index(idx8[:, t, :], top8[:, t, :], src[:, t, 0:e])
            link(v, ins)
            link(v, nc.vector.tensor_copy(idxf[:, :, :], idx8[:, :, 0:2]))
            for k in range(ks):
                ins = nc.vector.tensor_tensor(oh[:, k, :, 0:e], iota_e[:, 0:e].unsqueeze(1).broadcast_to([P, NT, e]),
                                              idxf[:, :, k:k + 1].broadcast_to([P, NT, e]), ALU.is_equal)
            link(v, ins)
            if ks == 2:
                link(v, nc.vector.tensor_tensor(oh[:, 2, :, 0:e], oh[:, 0, :, 0:e], oh[:, 1, :, 0:e], ALU.add))

        def ranks_pe(pe, e, sel_ready, done):
            pe.wait_ge(sel_ready, 1)
            flat = selb[:, :, 0:e]
            nc.tensor.matmul(by_tile(ps[:, 5, 0:NT * e], e), beforeb[:, :], flat, start=True, stop=False, skip_group_check=True)
            for t in range(NT - 1):
                mm = nc.tensor.matmul(by_tile(ps[:, 5, (t + 1) * e:NT * e], e), onesb[:, :],
                                      selb[:, t:t + 1, 0:e].broadcast_to([P, NT - 1 - t, e]),
                                      start=False, stop=(t == NT - 2), skip_group_check=True)
            mm.then_inc(done, 1)

        class Mlp:

            upped, silued, mixed, acted, downed = (sem(f"mlp_{x}") for x in ("upped", "silued", "mixed", "acted", "downed"))

            def __init__(self, counted, base, experts, parts, weighed):
                self.counted = counted
                self.units = [(e, i, c) for e in range(experts) for i in range(2) for c in range(parts)]
                self.weights = lambda e, c, w: mA[:, base + ((e * parts + c) * 3 + w) * D:base + ((e * parts + c) * 3 + w + 1) * D]
                self.parts, self.weighed, self.last = parts, weighed, (experts - 1, parts - 1)

        def mlp_pe(pe, M, before_first):
            def up(n):
                e, i, c = M.units[n]
                if n >= 2:
                    pe.wait_ge(M.acted, M.counted + n - 1)
                nc.tensor.matmul(ps[:, 2 + n % 2, :], M.weights(e, c, 0), hT[:, half(i)], start=True, stop=True)
                mm = nc.tensor.matmul(ps[:, 4 + n % 2, :], M.weights(e, c, 1), hT[:, half(i)], start=True, stop=True)
                if M.weighed and c == 0:
                    for t in range(4):
                        mm = nc.tensor.matmul(ps[:, 6 + n // M.parts % 2, tile(t)],
                                              comb[:, 4 * i + t, e:e + 1].broadcast_to([P, P]), ident[:, :],
                                              start=True, stop=True)
                mm.then_inc(M.upped, 1)

            def down(n):
                e, i, c = M.units[n]
                pe.wait_ge(M.acted, M.counted + n + 1)
                nc.tensor.matmul(ps[:, i, :], M.weights(e, c, 2), a_sb[:, n % 2, :], start=(e == 0 and c == 0),
                                 stop=((e, c) == M.last), skip_group_check=True).then_inc(M.downed, 1)

            before_first(pe)
            up(0)
            for n in range(len(M.units)):
                if n + 1 < len(M.units):
                    up(n + 1)
                down(n)

        def mlp_act(act, M):
            for n in range(len(M.units)):
                act.wait_ge(M.upped, M.counted + n + 1)
                if n >= 2:
                    act.wait_ge(M.mixed, M.counted + n - 1)
                nc.scalar.activation(g_sb[:, n % 2, :], ps[:, 2 + n % 2, :], ACT.Silu).then_inc(M.silued, 1)

        def mlp_dve(v, M):
            for n in range(len(M.units)):
                v.wait_ge(M.silued, M.counted + n + 1)
                if n >= 2:
                    v.wait_ge(M.downed, M.counted + n - 1)
                ins = nc.vector.tensor_tensor(a_sb[:, n % 2, :], g_sb[:, n % 2, :], ps[:, 4 + n % 2, :], ALU.mult)
                ins.then_inc(M.mixed, 1)
                if M.weighed:
                    v.wait_ge(M.mixed, M.counted + n + 1)
                    ins = nc.vector.tensor_tensor(a_sb[:, n % 2, :], a_sb[:, n % 2, :],
                                                  ps[:, 6 + n // M.parts % 2, :], ALU.mult).then_inc(M.acted, 1)
                else:
                    v.wait_ge(M.mixed, M.counted + n + 1)
                    v.sem_inc(M.acted, 1)

        r0 = [sem(f"R0_{x}") for x in ("logits", "shifted", "exped", "chosen", "ranked", "ready")]
        M0 = Mlp(0, 0, 10, 1, True)

        def l0_ffn_pe(pe):
            norm_pe(pe, 1, 1, xT, x_ready(1))
            logits_pe(pe, 1, 0, E0, r0[0])
            ranks_pe(pe, E0, r0[3], r0[4])

            def first(pe):
                pe.wait_ge(ld["m0"], 16)
                pe.wait_ge(r0[5], 1)
            mlp_pe(pe, M0, first)

        def l0_ffn_act(act):
            norm_act(act, 1, 1, xT, x_ready(1))
            softmax_act(act, E0, r0[1], r0[2])
            mlp_act(act, M0)

        def l0_ffn_dve(v):
            norm_dve(v, 1, 1, xT, hT, None)
            softmax_dve(v, E0, r0[0], r0[1], r0[2])
            choose(v, lg, E0, 2)
            nc.vector.tensor_copy(selb[:, :, 0:E0], oh[:, 2, :, 0:E0]).then_inc(r0[3], 1)
            link(v, nc.vector.tensor_tensor(small[:, 3, :], top8[:, :, 0], top8[:, :, 1], ALU.add))
            link(v, nc.vector.tensor_scalar(small[:, 3, :], small[:, 3, :], 1e-20, None, ALU.add))
            link(v, nc.vector.reciprocal(small[:, 4, :], small[:, 3, :]))
            link(v, nc.vector.tensor_tensor(lg[:, :, 0:E0], lg[:, :, 0:E0],
                                            small[:, 4, :].unsqueeze(2).broadcast_to([P, NT, E0]), ALU.mult))
            link(v, nc.vector.tensor_tensor(lg[:, :, 0:E0], lg[:, :, 0:E0], oh[:, 2, :, 0:E0], ALU.mult))
            v.wait_ge(r0[4], 1)
            link(v, nc.vector.tensor_scalar(lg2[:, :, 0:E0], by_tile(ps[:, 5, 0:NT * E0], E0), float(CAP0), None, ALU.is_lt))
            nc.vector.memset(comb[:, :, E0:E0 + 2], 1.0)
            nc.vector.tensor_tensor(comb[:, :, 0:E0], lg[:, :, 0:E0], lg2[:, :, 0:E0], ALU.mult).then_inc(r0[5], 1)
            mlp_dve(v, M0)
            for i in range(2):
                v.wait_ge(M0.downed, M0.counted + len(M0.units))
                residual(v, 1, i, ps[:, i, :], 1, None, None)

        WB = 8 * P + P + DH + 8 * P
        M1 = Mlp(20, 30 * D, 4, 1, False)
        cT = k_all

        def wide(causal, base, q_src, k_src):
            A = attention(DH, causal, B, UNITS, 6, 9, True)
            A.head = lambda j: j // 2 + 2 * (j % 2)

            def project(pe, it, part):
                cols_ = bass.ds(it * S, S)
                for c in (range(8), (8,))[part]:
                    src = q_src if c < 8 else k_src
                    nc.tensor.matmul(ps[:, c // 2, (c % 2) * S:(c % 2 + 1) * S], w1[:, base + P * c:base + P * c + P],
                                     src[:, cols_], start=True, stop=True).then_inc(A.projected.sem, 1)

            def stage(v, it):
                for c in range(0, 4, 2):
                    until(v, A.projected, it * 9 + c + 2)
                    nc.vector.tensor_copy(q_st[:, c:c + 2, :].rearrange("p c s -> p (c s)"),
                                          ps[:, c // 2, :]).then_inc(A.staged.sem, 1)
                until(v, A.projected, it * 9 + 9)
                nc.vector.tensor_scalar(km[:, 0, :], ps[:, 4, 0:S], DH ** -0.5, None, ALU.mult).then_inc(A.staged.sem, 1)

            def stage_values(v, it):
                nc.vector.tensor_copy(v_st[:, :, 0:DH], v_all[:, bass.ds(it * 2, 2), 0:DH]).then_inc(A.staged.sem, 1)

            def stage_act(act, it):
                for c in range(4, 8, 2):
                    until(act, A.projected, it * 9 + c + 2)
                    nc.scalar.copy(q_st[:, c:c + 2, :].rearrange("p c s -> p (c s)"),
                                   ps[:, c // 2, :]).then_inc(A.staged.sem, 1)

            def score(it, u, banks, nk):
                for s in range(2):
                    for jp, o in enumerate(banks):
                        r = slice(DH * jp, DH * jp + DH)
                        last = nc.tensor.matmul(o[:, s, 0:nk], q_st[r, 2 * (u % 4) + s, tile(A.qt(u))], km[r, 0, 0:nk],
                                                start=True, stop=True)
                    for o in banks:
                        if causal:
                            last = nc.tensor.matmul(o[:, s, nk - P:nk], identb[:, :], causalb[:, :],
                                                    start=False, stop=True, skip_group_check=True)
                return last

            A.project, A.stage, A.stage_values, A.stage_act, A.score = project, stage, stage_values, stage_act, score
            A.value = lambda it, u, c, p: v_st[:, c, 0:DH]
            A.inverse = lambda g: km[:, 1 + g % 2, :]
            A.output = lambda it, u: big[:, 2 * (u % 4):2 * (u % 4) + 2, bass.ds(it * S + A.qt(u) * P, P)]
            return A

        A1a = wide(True, 0, hT, hT)
        A1b = wide(False, WB, hT, cT)
        v1 = [[sem(f"L1{x}_v"), sem(f"L1{x}_v_done"), sem(f"L1{x}_o")] for x in "ab"]
        y1 = sem("L1_y")

        def wide_pe(pe, A, base, v_src, s):
            for t in range(NT):
                mm = nc.tensor.matmul(ps[:, t // 4, (t % 4) * P:(t % 4) * P + DH], v_src[:, tile(t)],
                                      w1[:, base + 9 * P:base + 9 * P + DH], start=True, stop=True)
            mm.then_inc(s[0], 1)
            pe.wait_ge(s[1], 2)
            attn_pe(pe, A)
            until(pe, A.normed, A.groups * B)
            for i in range(2):
                for c in range(8):
                    w = w1[:, base + 9 * P + DH + P * c:base + 9 * P + DH + P * c + P]
                    mm = nc.tensor.matmul(ps[:, i, :], w, big[:, c, half(i)], start=(c == 0), stop=(c == 7))
                mm.then_inc(s[2], 1)

        def l1_attn_pe(pe):
            norm_pe(pe, 2, 2, xT, x_ready(2))
            norm_pe(pe, 3, 3, h1T, norm_ready(2))
            norm_pe(pe, 4, 4, ctxT, norm_ready(3))

            def first(pe):
                pe.wait_ge(ld["w1"], 32)
                pe.wait_ge(n_out, 10)
            mlp_pe(pe, M1, first)
            pe.wait_ge(y1, 2)
            wide_pe(pe, A1a, 0, hT, v1[0])
            norm_pe(pe, 5, 5, h1T, lambda e, i: e.wait_ge(y1, 3 + i))
            pe.wait_ge(n_out, 12)
            wide_pe(pe, A1b, WB, cT, v1[1])

        def l1_attn_act(act):
            norm_act(act, 2, 2, xT, None)
            norm_act(act, 3, 3, h1T, None)
            norm_act(act, 4, 4, ctxT, None)
            mlp_act(act, M1)
            attn_act(act, A1a)
            norm_act(act, 5, 5, h1T, None)
            attn_act(act, A1b)

        def l1_attn_dve(v):
            norm_dve(v, 2, 2, xT, h1T, None)
            norm_dve(v, 3, 3, h1T, hT, col(C_PTB))
            norm_dve(v, 4, 4, ctxT, cT, col(C_CTX))
            mlp_dve(v, M1)
            v.wait_ge(M1.downed, M1.counted + len(M1.units))
            for i in range(2):
                nc.vector.tensor_tensor(h1T[:, half(i)], h1T[:, half(i)], ps[:, i, :], ALU.add).then_inc(y1, 1)
            values_dve(v, None, v1[0][0], v1[0][1], 1, DH)
            v.wait_ge(v1[0][1], 2)
            attn_dve(v, A1a)
            v.wait_ge(y1, 2)
            for i in range(2):
                v.wait_ge(v1[0][2], i + 1)
                nc.vector.tensor_tensor(h1T[:, half(i)], h1T[:, half(i)], ps[:, i, :], ALU.add).then_inc(y1, 1)
            norm_dve(v, 5, 5, h1T, hT, col(C_CA))
            values_dve(v, None, v1[1][0], v1[1][1], 1, DH)
            v.wait_ge(v1[1][1], 2)
            attn_dve(v, A1b)
            for i in range(2):
                v.wait_ge(v1[1][2], i + 1)
                residual(v, 2, i, ps[:, i, :], 2, None, None)

        r1 = [sem(f"R1_{x}") for x in ("logits", "shifted", "exped", "chosen", "ranked", "ready")]
        f1 = {x: sem(f"F1_{x}") for x in ("turned", "tokens", "spread", "spread_sb", "hot", "sent", "gathered",
                                          "up", "gelu", "down", "out", "pick", "y")}
        htok = q_st[:, :, :].rearrange("p c s -> p (c s)")[:, 0:N]
        xd = w1[:, 0:SLOTS]
        hot = w1[:, SLOTS:3 * SLOTS].rearrange("p (b s) -> p b s", b=2)
        eo = mA[:, 0:E1 * D]
        slotB, weightB = xc, h1T
        pick = prob[:, :, :, :].rearrange("p a j k -> p (a j k)")[:, 0:4 * HALF].rearrange("p (b n) -> p b n", b=4)
        hg = km[:, :, :].rearrange("p j s -> p (j s)")[:, 0:640].rearrange("p (b n) -> p b n", b=2)
        slot = small[:, 6, :]
        weight = small[:, 7, :]
        chunks = [(0, 512), (512, 1024), (1024, SLOTS)]

        def l1_ffn_pe(pe):
            norm_pe(pe, 6, 6, xT, x_ready(3))
            logits_pe(pe, 6, E0, E1, r1[0])
            for t in range(NT):
                mm = nc.tensor.transpose(ps[:, t // 4, tile(t % 4)], hT[:, tile(t)], ident[:, :])
            mm.then_inc(f1["turned"], 1)
            ranks_pe(pe, E1, r1[3], r1[4])
            pe.wait_ge(r1[5], 1)
            pe.wait_ge(f1["tokens"], 2)
            for w, src in enumerate((slot, weight)):
                for t in range(NT):
                    mm = nc.tensor.matmul(ps[:, (6, 0)[w] + t // 4, tile(t % 4)], src[:, t:t + 1].broadcast_to([P, P]),
                                          ident[:, :], start=True, stop=True)
                mm.then_inc(f1["spread"], 1)
            for t in range(NT):
                pe.wait_ge(f1["hot"], t + 1)
                for c, (lo, hi) in enumerate(chunks):
                    mm = nc.tensor.matmul(ps[:, 2 + c, 0:hi - lo], htok[:, tile(t)], hot[:, t % 2, lo:hi],
                                          start=(t == 0), stop=(t == NT - 1))
                mm.then_inc(f1["sent"], 1)
            pe.wait_ge(f1["gathered"], 3)
            pe.wait_ge(f1["spread_sb"], 4)
            pe.wait_ge(ld["e1"], 32)

            def up(e):
                if e >= 2:
                    pe.wait_ge(f1["gelu"], e - 1)
                for c in range(4):
                    mm = nc.tensor.matmul(ps[:, 6 + e % 2, CAP1 * c:CAP1 * c + CAP1], arena[:, FF1 * e + P * c:FF1 * e + P * c + P],
                                          xd[:, CAP1 * e:CAP1 * e + CAP1], start=True, stop=True)
                mm.then_inc(f1["up"], 1)

            up(0)
            for e in range(E1):
                if e + 1 < E1:
                    up(e + 1)
                pe.wait_ge(f1["gelu"], e + 1)
                if e >= 2:
                    pe.wait_ge(f1["out"], e - 1)
                for c in range(4):
                    w = E1 * FF1 + FF1 * e + P * c
                    mm = nc.tensor.matmul(ps[0:CAP1, e % 2, 0:D], hg[:, e % 2, CAP1 * c:CAP1 * c + CAP1],
                                          arena[:, w:w + P], start=(c == 0), stop=(c == 3))
                mm.then_inc(f1["down"], 1)
            for e in range(E1):
                pe.wait_ge(f1["out"], e + 1)
                for i in range(2):
                    n = 2 * e + i
                    pe.wait_ge(f1["pick"], n + 1)
                    nc.tensor.matmul(ps[:, 2 + i, :], eo[0:CAP1, tile(e)], pick[0:CAP1, n % 4, :],
                                     start=(e == 0), stop=(e == E1 - 1), skip_group_check=True).then_inc(f1["y"], 1)

        def l1_ffn_act(act):
            norm_act(act, 6, 6, xT, None)
            softmax_act(act, E1, r1[1], r1[2])
            act.wait_ge(f1["turned"], 1)
            for i in range(2):
                nc.scalar.copy(htok[:, half(i)], ps[:, i, :]).then_inc(f1["tokens"], 1)
            for w, dst in enumerate((slotB, weightB)):
                act.wait_ge(f1["spread"], w + 1)
                for i in range(2):
                    nc.scalar.copy(dst[:, half(i)], ps[:, (6, 0)[w] + i, :]).then_inc(f1["spread_sb"], 1)
            for e in range(E1):
                act.wait_ge(f1["up"], e + 1)
                if e >= 2:
                    act.wait_ge(f1["down"], e - 1)
                nc.scalar.activation(hg[:, e % 2, :], ps[:, 6 + e % 2, 0:4 * CAP1], ACT.Gelu_apprx_tanh).then_inc(f1["gelu"], 1)

        def l1_ffn_dve(v):
            norm_dve(v, 6, 6, xT, hT, None)
            softmax_dve(v, E1, r1[0], r1[1], r1[2])
            link(v, nc.vector.tensor_copy(lg2[:, :, :], by_tile(ps[:, 4, 0:NT * E1], E1)))
            choose(v, lg2, E1, 1)
            nc.vector.tensor_copy(selb[:, :, :], oh[:, 0, :, :]).then_inc(r1[3], 1)
            link(v, nc.vector.tensor_tensor(lg[:, :, :], lg[:, :, :], oh[:, 0, :, :], ALU.mult))
            link(v, nc.vector.tensor_reduce(weight, lg[:, :, :], X, ALU.add))
            v.wait_ge(r1[4], 1)
            link(v, nc.vector.tensor_tensor(lg2[:, :, :], by_tile(ps[:, 5, 0:NT * E1], E1), oh[:, 0, :, :], ALU.mult))
            link(v, nc.vector.tensor_reduce(small[:, 3, :], lg2[:, :, :], X, ALU.add))
            link(v, nc.vector.tensor_scalar(small[:, 4, :], small[:, 3, :], float(CAP1), 2.0 * SLOTS, ALU.is_ge, ALU.mult))
            link(v, nc.vector.tensor_tensor(small[:, 4, :], small[:, 4, :], small[:, 3, :], ALU.add))
            nc.vector.scalar_tensor_tensor(slot, idxf[:, :, 0], float(CAP1), small[:, 4, :], ALU.mult, ALU.add).then_inc(r1[5], 1)
            v.wait_ge(r1[5], 1)
            for t in range(NT):
                if t >= 2:
                    v.wait_ge(f1["sent"], t - 1)
                nc.vector.tensor_scalar(hot[:, t % 2, :], iota[:, :], slot[:, t:t + 1], None, ALU.is_equal).then_inc(f1["hot"], 1)
            v.wait_ge(f1["sent"], NT)
            for c, (lo, hi) in enumerate(chunks):
                nc.vector.tensor_copy(xd[:, lo:hi], ps[:, 2 + c, 0:hi - lo]).then_inc(f1["gathered"], 1)
            v.wait_ge(narrowed, 2)
            for e in range(E1):
                v.wait_ge(f1["down"], e + 1)
                nc.vector.tensor_copy(eo[0:CAP1, tile(e)], ps[0:CAP1, e % 2, 0:D]).then_inc(f1["out"], 1)
            v.wait_ge(f1["spread_sb"], 4)
            for e in range(E1):
                for i in range(2):
                    n = 2 * e + i
                    if n >= 4:
                        v.wait_ge(f1["y"], n - 3)
                    nc.vector.tensor_scalar(pick[0:CAP1, n % 4, :], slotB[0:CAP1, half(i)], slot_of[0:CAP1, e:e + 1], None,
                                            ALU.is_equal).then_inc(f1["pick"], 1)
            v.wait_ge(f1["y"], 2 * E1)
            for i in range(2):
                link(v, nc.vector.tensor_tensor(weightB[:, half(i)], ps[:, 2 + i, :], weightB[:, half(i)], ALU.mult))
                residual(v, 3, i, weightB[:, half(i)], 3, None, None)

        progs = {"pe": [l0_attn_pe, l0_ffn_pe, l1_attn_pe, l1_ffn_pe],
                 "dve": [l0_attn_dve, l0_ffn_dve, l1_attn_dve, l1_ffn_dve],
                 "act": [l0_attn_act, l0_ffn_act, l1_attn_act, l1_ffn_act]}

        a2 = {x: sem(f"A2_{x}") for x in ("proj", "q", "prod", "kext", "vals", "vtok", "vext", "scored", "maxed",
                                          "exped", "turned", "moved", "weighed", "mixed", "outturned")}
        prod = prob[:, 0, :, :].rearrange("p j k -> p (j k)")
        prob2 = prob[:, 1, :, :].rearrange("p j k -> p (j k)").rearrange("p (b n) -> p b n", b=2)
        pT2 = probT[:, :, 0, 0:S]
        v_tok = arena[:, 0:N].rearrange("p (t n) -> p t n", t=NT)
        v_ext = arena[:, N:2 * N].rearrange("p (t n) -> p t n", t=NT)
        shared2 = arena[:, 2 * N:3 * N]

        def l2_attn_pe(pe):
            norm_pe(pe, 7, 7, xT, x_ready(4))
            pe.wait_ge(ld["w2"], 32)
            for w, src in enumerate((hT, hT, ctxT)):
                for i in range(2):
                    if w == 0:
                        pe.wait_ge(n_out, 15 + i)
                    nc.tensor.matmul(ps[:, 2 * w + i, :], w2x[:, min(w, 1), :], src[:, half(i)],
                                     start=True, stop=True).then_inc(a2["proj"], 1)
            for w, src in enumerate((hT, ctxT)):
                for i in range(2):
                    b = (6, 0)[w] + i
                    if w == 1 and i == 0:
                        pe.wait_ge(a2["q"], 2)
                    for t in range(4):
                        mm = nc.tensor.matmul(ps[:, b, tile(t)], src[:, tile(4 * i + t)], w2x[:, 2, :], start=True, stop=True)
                    mm.then_inc(a2["vals"], 1)
            pe.wait_ge(a2["prod"], 2)
            pe.wait_ge(a2["kext"], 2)
            pe.wait_ge(a2["vext"], 2)
            pe.wait_ge(a2["vtok"], 2)

            def scores(t):
                if t >= 2:
                    pe.wait_ge(a2["exped"], t - 1)
                nc.tensor.matmul(ps[:, t % 2, 0:S], q_all[:, tile(t)], k_all[:, S * (t // 2):S * (t // 2) + S],
                                 start=True, stop=True)
                nc.tensor.matmul(ps[:, t % 2, S:S + 1], prod[:, tile(t)], ones[:, 0:1], start=True, stop=True).then_inc(a2["scored"], 1)

            def out_turn(t):
                pe.wait_ge(a2["mixed"], t + 1)
                nc.tensor.transpose(ps[:, 6 + t // 4, tile(t % 4)], onorm[:, tile(t % 2)], ident[:, :]).then_inc(a2["outturned"], 1)

            scores(0)
            for t in range(NT):
                if t + 1 < NT:
                    scores(t + 1)
                pe.wait_ge(a2["exped"], t + 1)
                if t >= 2:
                    pe.wait_ge(a2["moved"], t - 1)
                for c in range(2):
                    mm = nc.tensor.transpose(ps[:, 2 + t % 2, tile(c)], prob2[:, t % 2, tile(c)], ident[:, :])
                mm.then_inc(a2["turned"], 1)
                if t >= 1:
                    out_turn(t - 1)
                pe.wait_ge(a2["moved"], t + 1)
                if t >= 2:
                    pe.wait_ge(a2["mixed"], t - 1)
                for c in range(2):
                    mm = nc.tensor.matmul(ps[:, 4 + t % 2, 0:D], pT2[:, t % 2, tile(c)], v_ext[:, 2 * (t // 2) + c, :],
                                          start=(c == 0), stop=(c == 1))
                mm.then_inc(a2["weighed"], 1)
            out_turn(NT - 1)

        def l2_attn_act(act):
            norm_act(act, 7, 7, xT, None)
            for i in range(2):
                act.wait_ge(a2["proj"], 5 + i)
                nc.scalar.activation(k_all[:, half(i)], ps[:, 4 + i, :], ACT.Identity, bias=col(C_BK2)).then_inc(a2["kext"], 1)
            for t in range(NT):
                act.wait_ge(a2["maxed"], t + 1)
                if t >= 2:
                    act.wait_ge(a2["mixed"], t - 1)
                nc.scalar.activation(prob2[:, t % 2, 0:S + 1], ps[:, t % 2, 0:S + 1], ACT.Exp, bias=negmax[:, t % 2, 0:1],
                                     accum_out=rsum[:, t % 2, 0:1]).then_inc(a2["exped"], 1)

        def l2_attn_dve(v):
            norm_dve(v, 7, 7, xT, hT, None)
            for i in range(2):
                v.wait_ge(a2["proj"], 1 + i)
                nc.vector.tensor_scalar(q_all[:, half(i)], ps[:, i, :], col(C_BQ2), None, ALU.add).then_inc(a2["q"], 1)
            for i in range(2):
                v.wait_ge(a2["proj"], 3 + i)
                v.wait_ge(a2["q"], 1 + i)
                nc.vector.scalar_tensor_tensor(prod[:, half(i)], ps[:, 2 + i, :], col(C_BK2), q_all[:, half(i)],
                                               ALU.add, ALU.mult).then_inc(a2["prod"], 1)
            for w, dst in enumerate((v_tok, v_ext)):
                for i in range(2):
                    v.wait_ge(a2["vals"], 2 * w + i + 1)
                    nc.vector.tensor_tensor(dst[:, 4 * i:4 * i + 4, :], ps[:, (6, 0)[w] + i, :].rearrange("p (t n) -> p t n", t=4),
                                            bv[:, 1:2, :].broadcast_to([P, 4, D]), ALU.add).then_inc(a2[("vtok", "vext")[w]], 1)
            v.wait_ge(a2["vtok"], 2)

            def mix(t):
                v.wait_ge(a2["weighed"], t + 1)
                if t >= 2:
                    v.wait_ge(a2["outturned"], t - 1)
                o = onorm[:, tile(t % 2)]
                link(v, nc.vector.reciprocal(rsum[:, t % 2, 1:2], rsum[:, t % 2, 0:1]))
                link(v, nc.vector.scalar_tensor_tensor(o, v_tok[:, t, :], prob2[:, t % 2, S:S + 1], ps[:, 4 + t % 2, 0:D],
                                                       ALU.mult, ALU.add))
                nc.vector.tensor_scalar(o, o, rsum[:, t % 2, 1:2], None, ALU.mult).then_inc(a2["mixed"], 1)

            for t in range(NT):
                v.wait_ge(a2["scored"], t + 1)
                nc.vector.tensor_reduce(negmax[:, t % 2, 0:1], ps[:, t % 2, 0:S + 1], X, ALU.max, negate=True).then_inc(a2["maxed"], 1)
                if t >= 1:
                    mix(t - 1)
                v.wait_ge(a2["turned"], t + 1)
                nc.vector.tensor_copy(pT2[:, t % 2, :], ps[:, 2 + t % 2, 0:S]).then_inc(a2["moved"], 1)
            mix(NT - 1)
            for i in range(2):
                v.wait_ge(a2["outturned"], 4 * (i + 1))
                residual(v, 4, i, ps[:, 6 + i, :], 4, None, None)

        r2 = [sem(f"R2_{x}") for x in ("logits", "exped", "ready")]
        f2 = {x: sem(f"F2_{x}") for x in ("up", "relu", "square", "scale", "down", "rounded", "summed",
                                          "sup", "srelu", "ssq", "y")}
        sh_up = iota[:, 512:512 + HID2]
        sh_dn = iota[:, 512 + HID2:512 + HID2 + 2 * D].rearrange("p (c n) -> p c n", c=2)
        bfv = big[:, 4:8, :].rearrange("p c t -> p (c t)").bitcast(BF16).rearrange("p (k n) -> p k n", n=HALF)
        xin = [bfv[:, b, :] for b in range(2)]
        hr = [[bfv[:, 2 + 2 * b + c, :] for c in range(2)] for b in range(2)]
        hq = [[bfv[:, 6 + 2 * b + c, :] for c in range(2)] for b in range(2)]
        yb = [bfv[:, 10 + b, :] for b in range(2)]
        sr = [big[:, 2 + c, 0:HALF] for c in range(2)]
        widths = (P, HID2B)
        n2 = 2 * E2

        def l2_ffn_pe(pe):
            norm_pe(pe, 8, 8, xT, x_ready(5))
            logits_pe(pe, 8, E0 + E1, E2, r2[0])
            pe.wait_ge(r2[2], 1)
            pe.wait_ge(narrowed, 2)
            pe.wait_ge(ld["r3"], 16 * len(loads["r3"]))
            for i in range(2):
                if i:
                    pe.wait_ge(f2["ssq"], 2 * i)
                for c in range(2):
                    m = widths[c]
                    nc.tensor.matmul(ps[0:m, 2 + c, :], sh_up[:, P * c:P * c + m], hT[:, half(i)], start=True,
                                     stop=True).then_inc(f2["sup"], 1)
                for c in range(2):
                    m = widths[c]
                    pe.wait_ge(f2["ssq"], 2 * i + c + 1)
                    nc.tensor.matmul(ps[:, i, :], sh_dn[0:m, c, :], sr[c][0:m, :], start=(c == 0), stop=False,
                                     skip_group_check=True).then_inc(f2["y"], 1)

            def spread(n):
                e, i = n // 2, n % 2
                if n >= 2:
                    pe.wait_ge(f2["scale"], n - 1)
                for t in range(4):
                    mm = nc.tensor.matmul(ps[:, 6 + n % 2, tile(t)], comb[:, 4 * i + t, e:e + 1].broadcast_to([P, P]),
                                          ident[:, :], start=True, stop=True)
                mm.then_inc(f2["up"], 1)

            def up(n):
                e = n // 2
                pe.wait_ge(f2["scale"], n + 1)
                if n >= 1:
                    pe.wait_ge(f2["relu"], 2 * n)
                for c in range(2):
                    m = widths[c]
                    mm = nc.tensor.matmul(ps[0:m, 2 + c, :], up2[:, e, P * c:P * c + m], xin[n % 2], start=True, stop=True)
                mm.then_inc(f2["sup"], 1)

            def down(n):
                e = n // 2
                pe.wait_ge(f2["square"], 2 * n + 2)
                if n >= 2:
                    pe.wait_ge(f2["rounded"], n - 1)
                for c in range(2):
                    m = widths[c]
                    mm = nc.tensor.matmul(ps[:, 4 + n % 2, :], dn2[0:m, e, c, :], hq[n % 2][c][0:m, :],
                                          start=(c == 0), stop=(c == 1))
                mm.then_inc(f2["down"], 1)

            def add(n):
                pe.wait_ge(f2["rounded"], n + 1)
                nc.tensor.matmul(ps[:, n % 2, :], identb[:, :], yb[n % 2], start=False, stop=(n >= n2 - 2),
                                 skip_group_check=True).then_inc(f2["summed"], 1)

            pe.wait_ge(f2["ssq"], 4)
            spread(0)
            for n in range(n2 + 2):
                if n + 1 < n2:
                    spread(n + 1)
                if n < n2:
                    up(n)
                if 1 <= n <= n2:
                    down(n - 1)
                if n >= 2:
                    add(n - 2)

        def l2_ffn_act(act):
            norm_act(act, 8, 8, xT, None)
            act.wait_ge(r2[0], 1)
            nc.scalar.activation(lg[:, :, 0:E2], by_tile(ps[:, 4, 0:NT * E2], E2), ACT.Exp, scale=-1.0).then_inc(r2[1], 1)
            for i in range(2):
                for c in range(2):
                    m = widths[c]
                    act.wait_ge(f2["sup"], 2 * i + c + 1)
                    if i:
                        act.wait_ge(f2["y"], c + 1)
                    nc.scalar.activation(sr[c][0:m, :], ps[0:m, 2 + c, :], ACT.Relu).then_inc(f2["srelu"], 1)
            for n in range(n2 + 1):
                if n < n2:
                    act.wait_ge(f2["sup"], 4 + n + 1)
                    if n >= 2:
                        act.wait_ge(f2["square"], 2 * (n - 1))
                    for c in range(2):
                        m = widths[c]
                        nc.scalar.activation(hr[n % 2][c][0:m, :], ps[0:m, 2 + c, :], ACT.Relu).then_inc(f2["relu"], 1)
                if n >= 1:
                    act.wait_ge(f2["down"], n)
                    if n >= 3:
                        act.wait_ge(f2["summed"], n - 2)
                    nc.scalar.copy(yb[(n - 1) % 2], ps[:, 4 + (n - 1) % 2, :]).then_inc(f2["rounded"], 1)

        def l2_ffn_dve(v):
            norm_dve(v, 8, 8, xT, hT, None)
            v.wait_ge(r2[1], 1)
            link(v, nc.vector.tensor_scalar(lg[:, :, 0:E2], lg[:, :, 0:E2], 1.0, None, ALU.add))
            link(v, nc.vector.reciprocal(lg[:, :, 0:E2], lg[:, :, 0:E2]))
            link(v, nc.vector.tensor_tensor(lg2[:, :, 0:E2], lg[:, :, 0:E2],
                                            ebias[:, :].unsqueeze(1).broadcast_to([P, NT, E2]), ALU.add))
            choose(v, lg2, E2, 2)
            nc.vector.tensor_tensor(comb[:, :, 0:E2], lg[:, :, 0:E2], oh[:, 2, :, 0:E2], ALU.mult).then_inc(r2[2], 1)
            for i in range(2):
                for c in range(2):
                    m = widths[c]
                    v.wait_ge(f2["srelu"], 2 * i + c + 1)
                    nc.vector.tensor_tensor(sr[c][0:m, :], sr[c][0:m, :], sr[c][0:m, :], ALU.mult).then_inc(f2["ssq"], 1)

            def scale(n):
                v.wait_ge(f2["up"], n + 1)
                if n >= 2:
                    v.wait_ge(f2["sup"], 4 + n - 1)
                nc.vector.tensor_tensor(xin[n % 2], hT[:, half(n % 2)], ps[:, 6 + n % 2, :], ALU.mult).then_inc(f2["scale"], 1)

            scale(0)
            for n in range(n2):
                if n + 1 < n2:
                    scale(n + 1)
                if n >= 2:
                    v.wait_ge(f2["down"], n - 1)
                for c in range(2):
                    m = widths[c]
                    v.wait_ge(f2["relu"], 2 * n + c + 1)
                    nc.vector.tensor_tensor(hq[n % 2][c][0:m, :], hr[n % 2][c][0:m, :], hr[n % 2][c][0:m, :],
                                            ALU.mult).then_inc(f2["square"], 1)
            v.wait_ge(f2["summed"], n2)
            for i in range(2):
                residual(v, 5, i, ps[:, i, :], 5, None, None)

        a3 = {x: sem(f"A3_{x}") for x in ("proj", "q", "v", "v_done", "km", "spreadq", "rk", "rk_sb0", "rk_sb1", "split", "kept", "rv", "rv_sb",
                                          "rt", "rn", "ro", "rf", "att", "o", "cleared")}
        rel = arena[:, :].rearrange("p (c h q) -> p c h q", c=2, h=B * H)
        QPART = (0, 1, 2, 0, 1, 0)
        SLOT_ROWS = HD * len(QPART)
        QH = P // 2
        qd = q_st[:, :, :].rearrange("p c s -> p (c s)").bitcast(BF16).rearrange("p (h b q) -> p h b q", h=H, b=B)
        qparts = mA[:, 4 * N:4 * N + 3 * N // 2].bitcast(BF16).rearrange("p (w k g b q) -> p w k g b q", w=2, k=3, g=2, b=B)
        relk32 = iota[:, 0:2 * S - 1]
        relk = iota[:, 1024:1024 + S].bitcast(BF16)[:, 0:2 * S - 1]
        relv = w1[:, 0:2 * S * HD].rearrange("p (c q d) -> p c q d", c=2, q=S)
        km_all = mA[:, 0:4 * N].rearrange("p (j n) -> p j n", j=4)
        A3x = attention(HD, False, 2, 16, 0, 0, False)

        def score3(it, u, banks, nk):
            b, g = u // 4, u % 4
            for jp, o in enumerate(banks):
                nc.tensor.matmul(o, q_all[32 * g:32 * g + 32, S * b + P * it:S * b + P * it + P],
                                 km_all[32 * g:32 * g + 32, 2 * jp:2 * jp + 2, S * b:S * b + S], start=True, stop=True)
            for jp, o in enumerate(banks):
                for s in range(2):
                    for c in range(2):
                        last = nc.tensor.matmul(o[:, s, tile(c)], rel[:, c, H * b + 4 * g + 2 * jp + s, :], ident[:, :],
                                                start=False, stop=True, skip_group_check=True)
            return last

        def value3(it, u, c, j):
            h = 4 * (u % 4) + j
            return v_all[:, 2 * (u // 4) + c, h * HD:(h + 1) * HD]

        A3x.score, A3x.value, A3x.wo = score3, value3, lambda i: w3x[:, 4 + i, :]
        A3x.probT = lambda it, u, c, j: rel[:, c, 4 * u + j, :]
        A3x.moved_to = lambda it, u, c: rel[:, c, 4 * u:4 * u + 4, :]
        A3x.moved_from = lambda c: ps[:, 4 + c, :].rearrange("p (j q) -> p j q", j=4)
        A3x.output = lambda it, g: att[:, S * g + P * it:S * g + P * it + P]

        def rel_scores_pe(pe, it):
            pe.wait_ge(a3["spreadq"], 16 * 12 * (it + 1))
            pe.wait_ge(a3["split"], 5)
            for o in range(16):
                for c in range(2):
                    n = 32 * it + 2 * o + c
                    if n >= 8:
                        pe.wait_ge(a3[f"rk_sb{c}"], (n - 8) // 2 + 1)
                    for q8 in range(8):
                        q = 8 * o + q8
                        r = slice(64 * (q // QH), 64 * (q // QH) + SLOT_ROWS)
                        m = P * c - (P * it + q) + S - 1
                        mm = nc.tensor.matmul(ps[:, n % 8, q8:HALF:8], relk[r, m:m + P],
                                              qd[r, :, :, q % QH].rearrange("p h b -> p b h"), start=True, stop=True)
                    mm.then_inc(a3["rk"], 1)
            pe.wait_ge(a3["rk_sb0"], 16 * (it + 1))
            pe.wait_ge(a3["rk_sb1"], 16 * (it + 1))
            pe.wait_ge(a3["cleared"], it + 1)

        def rel_scores_move(eng, copy, it, c):
            for o in range(16):
                n = 32 * it + 2 * o + c
                eng.wait_ge(a3["rk"], n + 1)
                copy(rel[:, c, :, 8 * o:8 * o + 8],
                     ps[:, n % 8, :].rearrange("p (h q) -> p h q", q=8)).then_inc(a3[f"rk_sb{c}"], 1)

        def split_queries(v, w):
            for g in range(2):
                src = q_all[:, :].rearrange("p (b w g q) -> p w g b q", b=B, w=2, g=2)[:, w, g, :, :]
                rest = a_sb[:, g, 0:S].rearrange("p (b q) -> p b q", b=B)
                link(v, nc.vector.tensor_copy(qparts[:, w, 0, g, :, :], src))
                link(v, nc.vector.tensor_tensor(rest, src, qparts[:, w, 0, g, :, :], ALU.subtract))
                link(v, nc.vector.tensor_copy(qparts[:, w, 1, g, :, :], rest))
                nc.vector.tensor_tensor(qparts[:, w, 2, g, :, :], rest, qparts[:, w, 1, g, :, :],
                                        ALU.subtract).then_inc(a3["split"], 1)

        def split_distances(v):
            n = 2 * S - 1
            k0, k1, k2 = (c_sb[:, 0, 256 * i:256 * i + 256].bitcast(BF16)[:, 0:n] if i < 2 else
                          c_sb[:, 1, 0:256].bitcast(BF16)[:, 0:n] for i in range(3))
            rest = d_sb[:, 0, 0:n]
            link(v, nc.vector.tensor_copy(k0, relk32))
            link(v, nc.vector.tensor_tensor(rest, relk32, k0, ALU.subtract))
            link(v, nc.vector.tensor_copy(k1, rest))
            link(v, nc.vector.tensor_tensor(k2, rest, k1, ALU.subtract))
            link(v, nc.vector.tensor_scalar(k0, k0, smask[:, 0:1], None, ALU.mult))
            link(v, nc.vector.scalar_tensor_tensor(k1, k1, smask[:, 1:2], k0, ALU.mult, ALU.add))
            nc.vector.scalar_tensor_tensor(relk, k2, smask[:, 2:3], k1, ALU.mult, ALU.add).then_inc(a3["split"], 1)

        def rel_values_pe(pe, it):
            until(pe, A3x.stored, 4 * (it + 1))
            for q in range(QH):
                for g in range(2):
                    for c in range(2):
                        mm = nc.tensor.matmul(ps[QH * g:QH * g + B * H, 0, HD * q:HD * q + HD], rel[:, c, :, QH * g + q],
                                              relv[:, c, P * it + QH * g + q, :], start=(c == 0), stop=(c == 1),
                                              skip_group_check=True)
            mm.then_inc(a3["rv"], 1)
            pe.wait_ge(a3["rv_sb"], it + 1)
            for d in range(HD):
                for g in range(2):
                    r = slice(QH * g, QH * g + QH)
                    mm = nc.tensor.matmul(ps[r, 2, 64 * d:64 * d + 64], rv_sb[r, d:HALF:HD], ident[r, r], start=True,
                                          stop=True, skip_group_check=True)
            mm.then_inc(a3["rt"], 1)
            pe.wait_ge(a3["rn"], it + 1)
            for b in range(B):
                mm = nc.tensor.transpose(ps[:, 3, tile(b)], rn_sb[:, tile(b)], ident[:, :])
            mm.then_inc(a3["ro"], 1)
            pe.wait_ge(a3["rf"], it + 1)
            nc.tensor.matmul(ps[:, 4, :], w3x[:, 3, :], rn_sb[:, :], start=True, stop=True).then_inc(a3["o"], 1)
            pe.wait_ge(a3["att"], it + 1)

        rv_sb = h1T
        rn_sb = sq[:, 0:HALF]

        def rel_values_dve(v, it):
            v.wait_ge(a3["rv"], it + 1)
            nc.vector.tensor_copy(rv_sb[:, 0:HALF], ps[:, 0, :]).then_inc(a3["rv_sb"], 1)
            v.wait_ge(a3["rt"], it + 1)
            until(v, A3x.inverted, 4 * (it + 1))
            for b in range(B):
                ins = nc.vector.tensor_tensor(
                    rn_sb[:, tile(b)].rearrange("p (h d) -> p h d", d=HD),
                    ps[:, 2, :].rearrange("p (d b h) -> p b h d", d=HD, b=B)[:, b, :, :],
                    rsum[:, b, :].unsqueeze(2).broadcast_to([P, H, HD]), ALU.mult)
            ins.then_inc(a3["rn"], 1)
            v.wait_ge(a3["ro"], it + 1)
            nc.vector.tensor_copy(rn_sb[:, :], ps[:, 3, :]).then_inc(a3["rf"], 1)
            v.wait_ge(a3["o"], it + 1)
            until(v, A3x.stored, 4 * (it + 1))
            o = att[:, :].rearrange("p (b s) -> p b s", b=B)[:, :, tile(it)]
            nc.vector.tensor_tensor(o, o, ps[:, 4, :].rearrange("p (b s) -> p b s", b=B), ALU.add).then_inc(a3["att"], 1)

        A3x.before_pe, A3x.after_pe = rel_scores_pe, rel_values_pe

        def before_dve3(v, it):
            rel_scores_move(v, nc.vector.tensor_copy, it, 0)
            v.wait_ge(a3["rk_sb0"], 16 * (it + 1))
            nc.vector.memset(ps[:, 6, :], 0.0).then_inc(a3["cleared"], 1)

        A3x.before_dve = before_dve3
        A3x.before_act = lambda act, it: rel_scores_move(act, nc.scalar.copy, it, 1)
        A3x.after_dve = rel_values_dve

        def l3_attn_pe(pe):
            norm_pe(pe, 9, 9, xT, x_ready(6))
            for w, src in enumerate((hT, ctxT)):
                for i in range(2):
                    if w == 0:
                        pe.wait_ge(n_out, 19 + i)
                    nc.tensor.matmul(ps[:, 2 * w + i, :], w3x[:, w, :], src[:, half(i)], start=True, stop=True).then_inc(a3["proj"], 1)
            pe.wait_ge(a3["q"], 2)
            for t in range(NT):
                mm = nc.tensor.matmul(ps[:, t // 4, tile(t % 4)], ctxT[:, tile(t)], w3x[:, 2, :], start=True, stop=True)
            mm.then_inc(a3["v"], 1)
            pe.wait_ge(a3["v_done"], 2)
            pe.wait_ge(a3["km"], 8)
            attn_pe(pe, A3x)

        def l3_attn_dve(v):
            norm_dve(v, 9, 9, xT, hT, None)
            for i in range(2):
                v.wait_ge(a3["proj"], 1 + i)
                nc.vector.tensor_scalar(q_all[:, half(i)], ps[:, i, :], col(C_BQ3), HD ** -0.5, ALU.add, ALU.mult).then_inc(a3["q"], 1)
            v.wait_ge(a3["q"], 2)
            for w in range(2):
                split_queries(v, w)
            split_distances(v)
            for i in range(2):
                v.wait_ge(a3["proj"], 3 + i)
                for j in range(4):
                    nc.vector.tensor_scalar(km_all[:, j, half(i)], ps[:, 2 + i, :], col(C_BK3), hmask[:, j:j + 1],
                                            ALU.add, ALU.mult).then_inc(a3["km"], 1)
            values_dve(v, 2, a3["v"], a3["v_done"], H, HD)
            attn_dve(v, A3x)
            v.wait_ge(a3["att"], 2)
            for i in range(2):
                residual(v, 6, i, att[:, half(i)], 6, col(C_BO3), a_sb[:, i, :])

        def l3_attn_act(act):
            norm_act(act, 9, 9, xT, None)
            attn_act(act, A3x)

        def l3_attn_sp(sp):
            for it in range(2):
                sp.wait_ge(a3["split"], 2 * (it + 1))
                sp.dma_start(qscratch[it].rearrange("k g f n -> f k g n"),
                             qparts[:, it, :, :, :, :].rearrange("p k g b q -> p k g (b q)")).then_inc(a3["kept"], 16)
                sp.wait_ge(a3["kept"], 16 * (it + 1))
                if it:
                    sp.wait_ge(a3["rk"], 32)
                for g in range(2):
                    for i, k in enumerate(QPART):
                        r = 64 * g + HD * i
                        sp.dma_start(qd[r:r + HD, :, :, :].rearrange("d h b q -> d h (b q)"),
                                     qscratch[it, k, g].rearrange("(h d) n -> d h n", d=HD)).then_inc(a3["spreadq"], 16)

        w3f = w0[:, :, :].rearrange("p w n -> p (w n)")
        A3f = narrow(True, value_grouped, lambda i: w3f[:, 4 * D + 32 + i * D:5 * D + 32 + i * D])
        s3 = {x: sem(f"F3_{x}") for x in ("qk", "qk_done", "t", "v", "v_done", "x2")}
        r3 = [sem(f"R3_{x}") for x in ("logits", "shifted", "exped", "ready")]
        M3 = Mlp(28, 0, E3, 2, True)

        def l3_ffn_pe(pe):
            norm_pe(pe, 10, 10, xT, x_ready(7))
            norm_pe(pe, 11, None, h1T, None)
            pe.wait_ge(ld["w3"], 16)
            rope_pe(pe, w3f[:, 0:4 * D].rearrange("p (w n) -> p w n", w=4), 0, None, norm_ready(11), s3["qk"], True)
            pe.wait_ge(s3["qk_done"], 4)
            for t in range(NT):
                mm = nc.tensor.matmul(ps[:, t // 4, (t % 4) * P:(t % 4) * P + 32], hT[:, tile(t)], w3f[:, 4 * D:4 * D + 32],
                                      start=True, stop=True)
            mm.then_inc(s3["v"], 1)
            attn_pe(pe, A3f)
            norm_pe(pe, 12, None, h1T, None)
            logits_pe(pe, 12, E0 + E1 + E2, E3, r3[0])

            def first(pe):
                pe.wait_ge(ld["m3"], 16)
                pe.wait_ge(r3[3], 1)
            mlp_pe(pe, M3, first)

        def l3_ffn_act(act):
            norm_act(act, 10, 10, xT, None)
            norm_act(act, 11, None, h1T, norm_ready(10))
            act.wait_ge(s3["qk_done"], 4)
            attn_act(act, A3f)
            norm_act(act, 12, None, h1T, lambda e, i: e.wait_ge(s3["x2"], i + 1))
            softmax_act(act, E3, r3[1], r3[2])
            mlp_act(act, M3)

        def l3_ffn_dve(v):
            norm_dve(v, 10, 10, xT, h1T, None)
            norm_dve(v, 11, None, h1T, hT, col(C_LN1))
            rope_dve(v, s3["qk"], s3["qk_done"], [0.0, 0.0, 0.0, 0.0], s3["t"])
            v.wait_ge(s3["qk_done"], 4)
            values_dve(v, None, s3["v"], s3["v_done"], 4, HD)
            v.wait_ge(s3["v_done"], 2)
            clear_bank(v)
            attn_dve(v, A3f)
            for i in range(2):
                until(v, A3f.stored, 2 * B)
                nc.vector.tensor_tensor(h1T[:, half(i)], h1T[:, half(i)], att[:, half(i)], ALU.add).then_inc(s3["x2"], 1)
            norm_dve(v, 12, None, h1T, hT, col(C_LN2))
            softmax_dve(v, E3, r3[0], r3[1], r3[2])
            choose(v, lg, E3, 2)
            link(v, nc.vector.tensor_tensor(small[:, 3, :], top8[:, :, 0], top8[:, :, 1], ALU.add))
            link(v, nc.vector.reciprocal(small[:, 4, :], small[:, 3, :]))
            link(v, nc.vector.tensor_tensor(lg[:, :, 0:E3], lg[:, :, 0:E3],
                                            small[:, 4, :].unsqueeze(2).broadcast_to([P, NT, E3]), ALU.mult))
            nc.vector.tensor_tensor(comb[:, :, 0:E3], lg[:, :, 0:E3], oh[:, 2, :, 0:E3], ALU.mult).then_inc(r3[3], 1)
            mlp_dve(v, M3)
            v.wait_ge(M3.downed, M3.counted + len(M3.units))
            for i in range(2):
                link(v, nc.vector.tensor_tensor(h1T[:, half(i)], h1T[:, half(i)], ps[:, i, :], ALU.add))
                residual(v, 7, i, h1T[:, half(i)], 7, None, None)

        progs["pe"] += [l2_attn_pe, l2_ffn_pe, l3_attn_pe, l3_ffn_pe]
        progs["dve"] += [l2_attn_dve, l2_ffn_dve, l3_attn_dve, l3_ffn_dve]
        progs["act"] += [l2_attn_act, l2_ffn_act, l3_attn_act, l3_ffn_act]

        block = ctx.enter_context(nc.Block())

        @block.sync
        def _(sp):
            def load(*groups):
                for group in groups:
                    for dst, src in loads[group]:
                        sp.dma_start(dst, src).then_inc(ld[group], 16)

            load("c", "x", "w0", "m0", "w1", "w2", "e1a")
            if STAGES > 1:
                sp.wait_ge(x_done, 4)
                load("f2", "w3")
            if STAGES > 3:
                sp.wait_ge(x_done, 6)
                load("e1b")
            if STAGES > 5:
                sp.wait_ge(x_done, 8)
                load("r3")
            if STAGES > 6:
                l3_attn_sp(sp)
            if STAGES > 7:
                until(sp, A3x.scored, 32)
                load("m3")
            for i in range(2):
                sp.wait_ge(x_done, 2 * STAGES - 1 + i)
                sp.dma_start(out[:, half(i)], xT[:, half(i)]).then_inc(ld["out"], 16)
            sp.wait_ge(ld["out"], 32)

        @block.gpsimd
        def _(pool):
            if STAGES > 1:
                pool.wait_ge(ld["f2"], 32)
                nc.gpsimd.tensor_copy(up2[:, :, :].rearrange("p e n -> p (e n)"), mA[:, 0:E2 * HID2]).then_inc(narrowed, 1)
                nc.gpsimd.tensor_copy(dn2[:, :, :, :].rearrange("p e c n -> p (e c n)"),
                                      mA[:, E2 * HID2:E2 * HID2 + E2 * 2 * D]).then_inc(narrowed, 1)
        @block.tensor
        def _(pe):
            for f in progs["pe"][0:STAGES]:
                f(pe)

        @block.vector
        def _(v):
            for f in progs["dve"][0:STAGES]:
                f(v)

        @block.scalar
        def _(act):
            for f in progs["act"][0:STAGES]:
                f(act)


_TURN = [8 * (e // 8) + (e % 8 + 4) % 8 for e in range(D)]

_REL_ROWS = [int(np.clip(-(m - (S - 1)), -REL, REL)) + REL for m in range(2 * S - 1)]
_REL_IDS = np.clip(np.arange(S)[:, None] - np.arange(S)[None, :], -REL, REL).T.reshape(2, P, S) + REL


def constants():
    i = np.arange(P)
    inv = (1.0 / 10000.0 ** (np.arange(0, HD, 2, dtype=np.float32) / HD)).astype(np.float32)
    ang = np.arange(S, dtype=np.float32)[:, None] * inv[None, :]
    cos, sin = np.cos(ang), np.sin(ang)
    e = i % HD
    c = cos[:, e % 4].T
    s = sin[:, e % 4].T * np.where(e < 4, -1.0, 1.0)[:, None]
    scale = HD ** -0.5
    return {
        "ident": np.eye(P),
        "meaner": np.full((P, P), 1.0 / P),
        "before": (i[:, None] < i[None, :]),
        "causal": np.where(i[:, None] >= i[None, :], 0.0, NEG),
        "hmask": (i[:, None] % 32 // HD == np.arange(4)[None, :]),
        "smask": (np.array([0, 0, 0, 1, 1, 2, 3, 3])[i % 64 // HD][:, None] == np.arange(3)[None, :]),
        "rope": np.stack([c, s, c * scale, s * scale], 1),
        "iota": np.arange(SLOTS)[None],
        "slot_of": i[:, None] + CAP1 * np.arange(E1)[None, :],
    }


def kernel(**inputs):
    import concourse.bacc as _bacc
    from concourse.bass_utils import run_bass_kernel_spmd as _run

    w = {k: np.asarray(v) for k, v in inputs.items()}
    c = {k: np.ascontiguousarray(v, dtype=np.float32) for k, v in constants().items()}
    zero = np.zeros(D, np.float32)
    c["xT"] = w["x"].reshape(N, D).T
    c["ctxT"] = w["ctx_1024"].reshape(N, D).T
    c["gates"] = np.stack([w["g_xattn"], w["g_ffn"]], 1).reshape(1, 8)

    def quadrants(wo):
        parts = np.zeros((4, 4, 32, D), np.float32)
        parts[:, :, :HD] = wo.reshape(4, 4, HD, D)
        return list(parts.reshape(4, P, D))

    p = w["L0_xattn_Wq"], w["L0_xattn_Wk"]
    c["w0"] = np.stack([p[0].T, p[0][_TURN].T, p[1].T, p[1][_TURN].T, w["L0_xattn_Wv"].T]
                       + quadrants(w["L0_xattn_Wo"].T), 1)
    c["cols"] = np.stack([
        w["L0_xattn_bq"], w["L0_xattn_bq"][_TURN], w["L0_xattn_bk"], w["L0_xattn_bk"][_TURN], w["L0_xattn_bo"],
        w["L1_xattn_ptb_gamma"], w["L1_xattn_ca_gamma"], w["L1_xattn_ca_ctx_gamma"],
        w["L2_xattn_bq"], w["L2_xattn_bk"], w["L3_xattn_bq"], w["L3_xattn_bk"], w["L3_xattn_bo"],
        w["L3_ffn_ln1_w"], w["L3_ffn_ln2_w"]] + [zero] * 17, 1)
    c["bv"] = np.stack([w["L0_xattn_bv"], w["L2_xattn_bv"], w["L3_xattn_bv"]])[None]
    c["gw"] = np.concatenate([w["L0_ffn_gate_w"], w["L1_ffn_gate_w"], w["L2_ffn_gate_w"], w["L3_ffn_gate_w"]]).T
    c["ebias"] = w["L2_ffn_expert_bias"][None]

    def lhs(x):
        return x.transpose(2, 0, 1)

    m0 = [np.concatenate([w["L0_ffn_we_gate"], w["L0_ffn_ws_gate"].reshape(2, P, D)]),
          np.concatenate([w["L0_ffn_we_up"], w["L0_ffn_ws_up"].reshape(2, P, D)]),
          np.concatenate([w["L0_ffn_we_down"], w["L0_ffn_ws_down"].reshape(D, 2, P).transpose(1, 0, 2)])]
    c["m0"] = np.stack([lhs(m) for m in m0], 2).reshape(P, -1)
    fu, wq = w["L1_xattn_W_fused"], w["L1_xattn_W_q"]

    def attn1(q, kv, o):
        k, v = kv[:, :DH], kv[:, DH:]
        return [q, k, k, v, o.reshape(8, P, D).transpose(1, 0, 2).reshape(P, -1)]

    ff = fu[:, H * DH + 2 * DH:]
    c["w1"] = np.concatenate(
        attn1(fu[:, :H * DH], fu[:, H * DH:H * DH + 2 * DH], w["L1_xattn_W_attn_out"])
        + attn1(wq, w["L1_xattn_W_kv"], w["L1_xattn_W_out"]), 1)
    parts = [np.stack([ff[:, HALF + P * e:HALF + P * e + P], ff[:, P * e:P * e + P],
                       w["L1_xattn_W_ff_out"][P * e:P * e + P]], 1) for e in range(4)]
    c["m1"] = np.stack(parts, 1).reshape(P, -1)
    c["e1"] = np.concatenate([w["L1_ffn_w1"].transpose(1, 0, 2).reshape(P, -1),
                              w["L1_ffn_w2"].reshape(E1, 4, P, D).transpose(2, 0, 1, 3).reshape(P, -1)], 1)
    c["w2x"] = np.stack([w["L2_xattn_Wq"], w["L2_xattn_Wk"], w["L2_xattn_Wv"]], 1)
    c["up2"] = lhs(w["L2_ffn_w_up"])
    dn = np.zeros((E2, 2, P, D), np.float32)
    dn[:, 0] = w["L2_ffn_w_down"].transpose(0, 2, 1)[:, :P]
    dn[:, 1, :HID2B] = w["L2_ffn_w_down"].transpose(0, 2, 1)[:, P:]
    c["dn2"] = dn.transpose(2, 0, 1, 3)
    sd = np.zeros((2, P, D), np.float32)
    sd[0] = w["L2_ffn_shared_w_down"].T[:P]
    sd[1, :HID2B] = w["L2_ffn_shared_w_down"].T[P:]
    c["sh2"] = np.concatenate([w["L2_ffn_shared_w_up"].T, sd[0], sd[1]], 1)
    c["w3x"] = np.stack([w["L3_xattn_Wq"], w["L3_xattn_Wk"], w["L3_xattn_Wv"], w["L3_xattn_Wo"]]
                        + quadrants(w["L3_xattn_Wo"]), 1)


    c["relk"] = np.zeros((2, 64, 2 * S - 1), np.float32)
    c["relk"][:, :6 * HD] = np.tile(w["L3_xattn_rel_key_table"][_REL_ROWS].T, (6, 1))
    c["relk"] = c["relk"].reshape(P, -1)
    c["relv"] = w["L3_xattn_rel_value_table"][_REL_IDS].transpose(1, 0, 2, 3)
    f = w["L3_ffn_wqkv"]
    q, k, v = f[:D], f[D:D + 32], f[D + 32:]
    kx = k.reshape(4, 1, HD, D).repeat(4, 1).reshape(D, D)
    c["w3f"] = np.concatenate([q.T, q[_TURN].T, kx.T, kx[_TURN].T, v.T] + quadrants(w["L3_ffn_wo"].T), 1)
    w13, w2 = w["L3_ffn_w13"], w["L3_ffn_w2"]
    m3 = np.stack([np.stack([w13[:, P * j:P * j + P], w13[:, 256 + P * j:256 + P * j + P], w2[:, :, P * j:P * j + P]], 1)
                   for j in range(2)], 1)
    c["m3"] = m3.transpose(4, 0, 1, 2, 3).reshape(P, -1)

    nc = _bacc.Bacc("TRN2", target_bir_lowering=False, num_devices=1)
    arrays, args = {}, {}
    for name, x in c.items():
        x = np.ascontiguousarray(x)
        arrays[f"in_{name}"] = x
        args[name] = nc.dram_tensor(f"in_{name}", x.shape, mybir.dt.from_np(x.dtype), kind="ExternalInput").ap()
    out = nc.dram_tensor("out_0", (D, N), F32, kind="ExternalOutput").ap()
    qscratch = nc.dram_tensor("qscratch", (2, 3, 2, D, B * P // 2), BF16, kind="Internal").ap()
    build(nc, args, out, qscratch)
    r = _run(nc, [arrays], core_ids=[0])
    return np.ascontiguousarray(r.results[0]["out_0"].T).reshape(B, S, D)
```

```python
from contextlib import ExitStack

import numpy as np

import concourse.bass as bass
from concourse import mybir

F32 = mybir.dt.float32
BF16 = mybir.dt.bfloat16
U32 = mybir.dt.uint32
ALU = mybir.AluOpType
ACT = mybir.ActivationFunctionType
X = mybir.AxisListType.X

B, S, D = 4, 256, 128
N = B * S
P = 128
NT = N // P
HALF = 512
H = 16
HD = D // H
DH = 64
E0, E1, E2, E3 = 8, 16, 8, 8
EW = E0 + 2
CAP0, CAP1 = 320, 80
FF1 = 512
HID2 = 176
HID2B = HID2 - P
CONSTS = {"ident": P, "meaner": P, "cols": 32, "smask": 3, "rows3": EW, "slot_of": E1, "gw": E0 + E1 + E2 + E3, "rope": 4 * S}
REL = 128
EPS = 1e-5
SLOTS = E1 * CAP1
UNITS = 8
NEG = -3.0e38
SUBLAYERS = 8


def half(i):
    return slice(HALF * i, HALF * (i + 1))


def tile(t):
    return slice(P * t, P * (t + 1))


class Counted:

    def __init__(self, sem, past):
        self.sem, self.past = sem, past


def until(eng, counted, n):
    eng.wait_ge(counted.sem, n + counted.past)


class Attention:

    def __init__(self, sems, totals, width, causal, iters, units, staged_by, projected_by):
        self.width, self.causal, self.iters, self.units = width, causal, iters, units
        self.per_group = 4 if width == HD else 1
        self.groups = units // self.per_group
        self.staged_by = staged_by

        def counted(what, per_iteration):
            c = Counted(sems[what], totals.get(what, 0))
            totals[what] = c.past + per_iteration * iters
            return c

        self.staged = counted("staged", staged_by)
        self.projected = counted("projected", projected_by)
        self.scored = counted("scored", units)
        self.maxed = counted("maxed", units)
        self.exped = counted("exped", units)
        self.turned = [counted(f"turned{c}", self.count(c, units)) for c in range(2)]
        self.moved = [counted(f"moved{c}", self.count(c, units)) for c in range(2)]
        self.weighed = counted("weighed", units)
        self.inverted = counted("inverted", self.groups)
        self.widened = counted("widened", self.groups)
        self.spread = counted("spread", self.groups)
        self.spread_sb = counted("spread_sb", self.groups)
        self.normed = counted("normed", self.groups)
        outs = self.groups if width == HD else 0
        self.outed = counted("outed", outs)
        self.stored = counted("stored", outs)

    def qt(self, u):
        return u // 4 % 2

    def key_tiles(self, u):
        return 1 if self.causal and self.qt(u) == 0 else 2

    def count(self, c, u):
        return sum(1 for v in range(u) if c < self.key_tiles(v))

    def ends_group(self, u):
        return u >= 0 and (u + 1) % self.per_group == 0


def wait_count(eng, sem, per, it, n):
    if isinstance(it, int):
        if per * it + n > 0:
            until(eng, sem, per * it + n)
    elif n > 0:
        until(eng, sem, it * per + n)


def build(nc, a, out, qscratch, kscratch, qkscratch):
    ctx = ExitStack()
    with ctx:
        def sb(name, shape, dt=F32):
            return ctx.enter_context(nc.sbuf_tensor(name, shape, dt))

        def sem(name):
            return ctx.enter_context(nc.semaphore(name))

        ps = ctx.enter_context(nc.psum_tensor("ps", [P, 8, HALF], F32))

        xT = sb("xT", [P, N])
        ctxT = sb("ctxT", [P, N])
        hT = sb("hT", [P, N])
        h1T = sb("h1T", [P, N])
        sq = sb("sq", [P, N])
        xc = sb("xc", [P, N])
        consts = sb("consts", [P, sum(CONSTS.values())])
        at = {x: sum(list(CONSTS.values())[:i]) for i, x in enumerate(CONSTS)}
        ident, meaner, cols, smask, rows3, slot_of, gw, rope4 = (consts[:, at[x]:at[x] + n] for x, n in CONSTS.items())
        rope = rope4.rearrange("p (r s) -> p r s", r=4)
        identb = sb("identb", [P, P], BF16)
        beforeb = sb("beforeb", [P, P], BF16)
        ones = sb("ones", [P, 1])
        onesb = sb("onesb", [P, P], BF16)
        causalb = sb("causalb", [P, P], BF16)
        gates = sb("gates", [P, 8])
        iota = sb("iota", [P, SLOTS])
        iota_e = sb("iota_e", [P, E1])
        eps = sb("eps", [P, 1])
        std = sb("std", [P, NT])
        rstd = sb("rstd", [P, NT])

        w0 = sb("w0", [P, 9, D])
        bv = sb("bv", [P, 3, D])
        w2x = sb("w2x", [P, 3, D])
        w3x = sb("w3x", [P, 8, D])
        ebias = sb("ebias", [P, E2])
        mA = sb("mA", [P, 48 * D])
        w1 = sb("w1", [P, 8 * D + D + DH + 8 * D + 8 * D + D + DH + 8 * D])
        up2 = sb("up2", [P, E2, HID2], BF16)
        dn2 = sb("dn2", [P, E2, 2, D], BF16)
        arena = sb("arena", [P, 2 * E1 * FF1])
        q_all = sb("q_all", [P, N])
        k_all = sb("k_all", [P, N])
        q_st = sb("q_st", [P, 8, S])
        km = sb("km", [P, 4, S])
        v_all = sb("v_all", [P, NT, D])
        v_st = sb("v_st", [P, 2, D])
        prob = sb("prob", [P, 2, 4, S])
        probT = sb("probT", [P, 2, 2, HALF])
        negmax = sb("negmax", [P, 2, 4])
        rsum = sb("rsum", [P, 4, H])
        onorm = sb("onorm", [P, HALF])
        before, causal = onorm[:, 0:P], onorm[:, P:2 * P]
        sums = sb("sums", [P, 4, H])
        rspread = sq[:, :].rearrange("p (g q) -> p g q", g=2)
        big = arena[:, E1 * FF1:].rearrange("p (c t) -> p c t", c=8)
        att = xc
        lg = sb("lg", [P, NT, E1])
        lg2 = sb("lg2", [P, NT, E1])
        small = sb("small", [P, 8, NT])
        top8 = sb("top8", [P, NT, 8])
        idx8 = sb("idx8", [P, NT, 8], U32)
        idxf = sb("idxf", [P, NT, 2])
        oh = sb("oh", [P, 3, NT, E1])
        selb = sb("selb", [P, NT, E1], BF16)
        comb = sb("comb", [P, NT, EW])
        cparts = sb("cparts", [P, NT, 3, EW], BF16)
        crest = oh[:, 0, :, 0:EW]
        g_sb = prob[:, 0, :, :].rearrange("p j k -> p (j k)").rearrange("p (i n) -> p i n", i=2)
        a_sb = prob[:, 1, :, :].rearrange("p j k -> p (j k)").rearrange("p (i n) -> p i n", i=2)
        c_sb = probT[:, 0, :, :]
        d_sb = probT[:, 1, :, :]

        ld = {k: sem("ld_" + k) for k in ("c", "x", "w0", "m0", "w1", "e1", "w2", "f2", "w3", "m3", "r3", "out")}
        ld["e1a"] = ld["e1b"] = ld["e1"]
        narrowed = sem("narrowed")
        n_mean, n_cent, n_sq, n_var, n_std, n_rstd, n_wide, n_out = (
            sem(s) for s in ("n_mean", "n_cent", "n_sq", "n_var", "n_std", "n_rstd", "n_wide", "n_out"))
        x_done = sem("x_done")
        made = sem("made")
        gated = sem("gated")
        chain = sem("chain")
        links = [0]

        loads = {
            "c": [(consts[:, :], a["consts"]), (onorm[:, 0:2 * P], a["masks"]),
                  (gates[:, :], a["gates"].broadcast_to([P, 8])),
                  (iota[:, :], a["iota"].partition_broadcast(P)),
                  (bv[:, :, :], a["bv"].partition_broadcast(P)),
                  (ebias[:, :], a["ebias"].partition_broadcast(P))],
            "x": [(xT[:, :], a["xT"]), (ctxT[:, :], a["ctxT"])],
            "w0": [(w0[:, :, :], a["w0"])],
            "m0": [(mA[:, 0:30 * D], a["m0"])],
            "w1": [(w1[:, :], a["w1"]), (mA[:, 30 * D:42 * D], a["m1"])],
            "e1a": [(arena[:, 0:E1 * FF1], a["e1"][:, 0:E1 * FF1])],
            "e1b": [(arena[:, E1 * FF1:], a["e1"][:, E1 * FF1:])],
            "w2": [(w2x[:, :, :], a["w2x"]), (w3x[:, :, :], a["w3x"])],
            "f2": [(mA[:, 0:E2 * HID2], a["up2"].rearrange("p e n -> p (e n)")),
                   (mA[:, E2 * HID2:E2 * HID2 + E2 * 2 * D], a["dn2"].rearrange("p e c n -> p (e c n)"))],
            "m3": [(mA[:, :], a["m3"])],
            "w3": [(w0[:, :, :].rearrange("p w n -> p (w n)")[:, 0:8 * D + 32], a["w3f"])],
            "r3": [(w1[:, 0:2 * S * HD], a["relv"].rearrange("p c q d -> p (c q d)")),
                   (iota[:, 512:512 + HID2 + 2 * D], a["sh2"])]
                  + [(iota[:, 0:2 * S - 1], a["relk"])],
        }
        C_BQ0, C_BQR0, C_BK0, C_BKR0, C_BO0, C_PTB, C_CA, C_CTX, C_BQ2, C_BK2, C_BQ3, C_BK3, C_BO3, C_LN1, C_LN2 = range(15)

        def col(i):
            return cols[:, i:i + 1]

        def link(eng, ins):
            links[0] += 1
            ins.then_inc(chain, 1)
            eng.wait_ge(chain, links[0])

        def norm_pe(pe, k, km_, src, wait_src):
            for i in range(2):
                if km_ is not None:
                    wait_src(pe, i)
                    nc.tensor.matmul(ps[:, i, :], meaner[:, :], src[:, half(i)], start=True, stop=True).then_inc(n_mean, 1)
            for t in range(NT):
                pe.wait_ge(n_sq, 2 * k + t // 4 + 1)
                mm = nc.tensor.matmul(ps[:, 2, t:t + 1], sq[:, tile(t)], meaner[:, 0:1], start=True, stop=True)
            mm.then_inc(n_var, 1)
            pe.wait_ge(n_rstd, k + 1)
            for t in range(NT):
                mm = nc.tensor.matmul(ps[:, 2 + t // 4, tile(t % 4)], rstd[:, t:t + 1].broadcast_to([P, P]), ident[:, :],
                                      start=True, stop=True)
                if t % 4 == 3:
                    mm.then_inc(n_wide, 1)

        def norm_dve(v, k, km_, src, dst, gamma):
            if k:
                v.wait_ge(n_out, 2 * k)
            for i in range(2):
                if km_ is not None:
                    v.wait_ge(n_mean, 2 * km_ + i + 1)
                    nc.vector.tensor_tensor(xc[:, half(i)], src[:, half(i)], ps[:, i, :], ALU.subtract).then_inc(n_cent, 1)
            cen = xc if km_ is not None else src
            v.wait_ge(n_std, k + 1)
            nc.vector.reciprocal(rstd[:, :], std[:, :]).then_inc(n_rstd, 1)
            for i in range(2):
                v.wait_ge(n_wide, 2 * k + i + 1)
                if gamma is None:
                    nc.vector.tensor_tensor(dst[:, half(i)], cen[:, half(i)], ps[:, 2 + i, :], ALU.mult).then_inc(n_out, 1)
                else:
                    nc.vector.scalar_tensor_tensor(dst[:, half(i)], cen[:, half(i)], gamma, ps[:, 2 + i, :],
                                                   ALU.mult, ALU.mult).then_inc(n_out, 1)

        def norm_act(act, k, km_, src, wait_src):
            for i in range(2):
                if km_ is not None:
                    act.wait_ge(n_cent, 2 * km_ + i + 1)
                    nc.scalar.activation(sq[:, half(i)], xc[:, half(i)], ACT.Square).then_inc(n_sq, 1)
                else:
                    wait_src(act, i)
                    nc.scalar.activation(sq[:, half(i)], src[:, half(i)], ACT.Square).then_inc(n_sq, 1)
            act.wait_ge(n_var, k + 1)
            nc.scalar.activation(std[:, :], ps[:, 2, 0:NT], ACT.Sqrt, bias=eps[:, 0:1]).then_inc(n_std, 1)

        def x_ready(k):
            def wait(eng, i):
                if k == 0:
                    eng.wait_ge(ld["x"], 32)
                    eng.wait_ge(ld["c"], 16 * len(loads["c"]))
                    eng.wait_ge(made, 1)
                else:
                    eng.wait_ge(x_done, 2 * (k - 1) + i + 1)
            return wait

        def norm_ready(k):
            def wait(eng, i):
                eng.wait_ge(n_out, 2 * k + i + 1)
            return wait

        def sc_bank(u, j):
            return 2 * (u % 2) + j // 2

        def scores(pe, A, it, u):
            wait_count(pe, A.exped, A.units, it, max(0, u - 1))
            banks = [ps[:, sc_bank(u, 2 * jp), :].rearrange("p (j k) -> p j k", j=2) for jp in range(2)]
            A.score(it, u, banks, A.key_tiles(u) * P).then_inc(A.scored.sem, 1)

        def turn(pe, A, it, u):
            until(pe, A.exped, it * A.units + u + 1)
            for c in range(A.key_tiles(u)):
                wait_count(pe, A.moved[c], A.count(c, A.units), it, A.count(c, u))
                for j in range(4):
                    last = nc.tensor.transpose(ps[:, 4 + c, tile(j)], prob[:, u % 2, j, tile(c)], ident[:, :])
                last.then_inc(A.turned[c].sem, 1)

        def weigh(pe, A, it, u):
            for c in range(A.key_tiles(u)):
                until(pe, A.moved[c], it * A.count(c, A.units) + A.count(c, u) + 1)
            g = u // A.per_group
            last_c = A.key_tiles(u) - 1
            if A.width == HD:
                if u % 4 == 0:
                    until(pe, A.normed, it * A.groups + g)
                for j in range(4):
                    for c in range(last_c + 1):
                        last = nc.tensor.matmul(ps[32 * j:32 * j + HD, 6, tile(u % 4)], A.value(it, u, c, j),
                                                A.probT(it, u, c, j), start=(c == 0), stop=(c == last_c),
                                                skip_group_check=True)
            else:
                until(pe, A.normed, it * A.groups + max(0, g - 1))
                for c in range(last_c + 1):
                    for p in range(2):
                        last = nc.tensor.matmul(ps[DH * p:DH * p + DH, 6 + u % 2, 0:S], A.value(it, u, c, p),
                                                probT[:, u % 2, c, S * p:S * p + S], start=(c == 0), stop=(c == last_c),
                                                skip_group_check=True)
            last.then_inc(A.weighed.sem, 1)

        def spread(pe, A, it, g):
            until(pe, A.widened, it * A.groups + g + 1)
            if A.width == HD:
                until(pe, A.stored, it * A.groups + g)
                for i in range(4):
                    last = nc.tensor.matmul(ps[:, 7, tile(i)], A.inverse(g)[:, tile(i)], ident[:, :], start=True, stop=True)
            else:
                for i in range(2):
                    last = nc.tensor.matmul(ps[:, 6 + g % 2, S + P * i:S + P * i + P], A.inverse(g)[:, tile(i)], ident[:, :],
                                            start=True, stop=True, skip_group_check=True)
            last.then_inc(A.spread.sem, 1)

        def out_project(pe, A, it, g):
            until(pe, A.normed, it * A.groups + g + 1)
            for i in range(4):
                last = nc.tensor.matmul(ps[:, 7, 0:P], A.wo(i), onorm[:, tile(i)], start=(i == 0), stop=(i == 3))
            last.then_inc(A.outed.sem, 1)

        def batches(eng, A, prologue, iteration):
            prologue()
            with eng.Fori(0, A.iters - 1) as it:
                iteration(it, it + 1)
            iteration(A.iters - 1, None)

        def attn_pe(pe, A):
            def iteration(it, following):
                if A.staged_by:
                    until(pe, A.staged, it * A.staged_by + A.staged_by)
                for u in range(A.ahead):
                    scores(pe, A, it, u)
                for u in range(A.units + 3):
                    if u + A.ahead < A.units:
                        scores(pe, A, it, u + A.ahead)
                    if A.ahead == 2 and u < A.units:
                        turn(pe, A, it, u)
                    if 1 <= u <= A.units:
                        weigh(pe, A, it, u - 1)
                    if A.ahead == 1 and u < A.units:
                        turn(pe, A, it, u)
                    if following is not None and u in (A.units - 1, A.units):
                        A.project(pe, following, u - (A.units - 1))
                    if 1 <= u <= A.units:
                        if A.ends_group(u - 1):
                            spread(pe, A, it, (u - 1) // A.per_group)
                    if A.width == HD and u >= 3 and A.ends_group(u - 3):
                        out_project(pe, A, it, (u - 3) // A.per_group)

            if A.loop:
                def first():
                    A.project(pe, 0, 0)
                    A.project(pe, 0, 1)
                batches(pe, A, first, iteration)
            else:
                for it in range(A.iters):
                    A.before_pe(pe, it)
                    iteration(it, None)
                    A.after_pe(pe, it)
            until(pe, A.stored if A.width == HD else A.normed, A.iters * A.groups)

        def attn_dve(v, A):
            def maxima(it, u):
                until(v, A.scored, it * A.units + u + 1)
                b0 = sc_bank(u, 0)
                s = ps[:, b0:b0 + 2, :].rearrange("p b (j k) -> p (b j) k", j=2)[:, :, 0:A.key_tiles(u) * P]
                nc.vector.tensor_reduce(negmax[:, u % 2, :], s, X, ALU.max, negate=True).then_inc(A.maxed.sem, 1)

            def move(it, u):
                wait_count(v, A.weighed, A.units, it, max(0, u - 1))
                for c in range(A.key_tiles(u)):
                    until(v, A.turned[c], it * A.count(c, A.units) + A.count(c, u) + 1)
                    nc.vector.tensor_copy(A.moved_to(it, u, c), A.moved_from(c)).then_inc(A.moved[c].sem, 1)

            def invert(it, g):
                until(v, A.exped, it * A.units + (g + 1) * A.per_group)
                nh = 4 * A.per_group
                nc.vector.reciprocal(rsum[:, g % 4, 0:nh], sums[:, g % 4, 0:nh]).then_inc(A.inverted.sem, 1)

            def normalise(it, g):
                until(v, A.spread_sb, it * A.groups + g + 1)
                if A.width == HD:
                    wait_count(v, A.outed, A.groups, it, g)
                    until(v, A.weighed, it * A.units + (g + 1) * 4)
                    ins = nc.vector.tensor_tensor(onorm[:, :], ps[:, 6, :], rspread[:, g % 2, :], ALU.mult)
                else:
                    until(v, A.weighed, it * A.units + g + 1)
                    ins = nc.vector.tensor_tensor(A.output(it, g), ps[:, 6 + g % 2, 0:S].rearrange("p (c q) -> p c q", c=2),
                                                  rspread[:, g % 2, 0:S].rearrange("p (c q) -> p c q", c=2), ALU.mult)
                ins.then_inc(A.normed.sem, 1)

            def iteration(it, following):
                for u in range(A.units + 2):
                    if u < A.units:
                        maxima(it, u)
                    if 1 <= u <= A.units:
                        if A.ends_group(u - 1):
                            invert(it, (u - 1) // A.per_group)
                        move(it, u - 1)
                    if following is not None and u == A.units:
                        A.stage(v, following)
                    if A.ends_group(u - 2):
                        normalise(it, (u - 2) // A.per_group)
                if following is not None:
                    A.stage_values(v, following)

            if A.loop:
                def first():
                    A.stage(v, 0)
                    A.stage_values(v, 0)
                batches(v, A, first, iteration)
            else:
                for it in range(A.iters):
                    A.before_dve(v, it)
                    iteration(it, None)
                    A.after_dve(v, it)

        def attn_act(act, A):
            def exps(it, u):
                until(act, A.maxed, it * A.units + u + 1)
                for c in range(2):
                    wait_count(act, A.turned[c], A.count(c, A.units), it, A.count(c, max(0, u - 1)))
                n = A.key_tiles(u) * P
                g, at = u // A.per_group, 4 * (u % A.per_group)
                for j in range(4):
                    s = ps[:, sc_bank(u, j), :].rearrange("p (j k) -> p j k", j=2)[:, j % 2, 0:n]
                    h = at + A.head(j)
                    last = nc.scalar.activation(prob[:, u % 2, j, 0:n], s, ACT.Exp, bias=negmax[:, u % 2, j:j + 1],
                                                accum_out=sums[:, g % 4, h:h + 1])
                last.then_inc(A.exped.sem, 1)

            def widen(it, g):
                until(act, A.inverted, it * A.groups + g + 1)
                wait_count(act, A.spread, A.groups, it, max(0, g - 1))
                nh, w = (H, 32) if A.width == HD else (4, DH)
                nc.scalar.copy(A.inverse(g).rearrange("p (h w) -> p h w", w=w),
                               rsum[:, g % 4, 0:nh].unsqueeze(2).broadcast_to([P, nh, w])).then_inc(A.widened.sem, 1)

            def spread_move(it, g):
                until(act, A.spread, it * A.groups + g + 1)
                wait_count(act, A.normed, A.groups, it, max(0, g - 1))
                src, n = (ps[:, 7, :], HALF) if A.width == HD else (ps[:, 6 + g % 2, S:2 * S], S)
                nc.scalar.copy(rspread[:, g % 2, 0:n], src).then_inc(A.spread_sb.sem, 1)

            def store(it, g):
                until(act, A.outed, it * A.groups + g + 1)
                nc.scalar.copy(A.output(it, g), ps[:, 7, 0:P]).then_inc(A.stored.sem, 1)

            def iteration(it, following):
                for u in range(A.units + 4):
                    if u < A.units:
                        exps(it, u)
                    if 1 <= u <= A.units:
                        if A.ends_group(u - 1):
                            widen(it, (u - 1) // A.per_group)
                    if u < A.units + 2 and A.ends_group(u - 2):
                        spread_move(it, (u - 2) // A.per_group)
                    if following is not None and u == A.units:
                        A.stage_act(act, following)
                    if A.width == HD and A.ends_group(u - 4):
                        store(it, (u - 4) // A.per_group)
            if A.loop:
                batches(act, A, lambda: A.stage_act(act, 0), iteration)
            else:
                for it in range(A.iters):
                    A.before_act(act, it)
                    iteration(it, None)
                    A.after_act(act, it)

        def nothing(*_):
            pass

        attn_sems = {x: sem(f"attn_{x}") for x in ("staged", "projected", "scored", "maxed", "exped", "turned0", "turned1",
                                                   "moved0", "moved1", "weighed", "inverted", "widened", "spread", "spread_sb",
                                                   "normed", "outed", "stored")}
        attn_totals = {"normed": 1, "stored": 1}

        def attention(width, causal, iters, units, staged_by, projected_by, loop):
            A = Attention(attn_sems, attn_totals, width, causal, iters, units, staged_by, projected_by)
            A.loop = loop
            A.ahead = 1
            A.inverse = lambda g: km[:, 2 * (g % 2):2 * (g % 2) + 2, :].rearrange("p a s -> p (a s)")
            A.head = lambda j: j
            A.project = A.stage = A.stage_act = A.stage_values = nothing
            A.before_pe = A.after_pe = A.before_dve = A.after_dve = A.before_act = A.after_act = nothing
            A.probT = lambda it, u, c, j: probT[:, u % 2, c, tile(j)]
            A.moved_to = lambda it, u, c: probT[:, u % 2, c, :]
            A.moved_from = lambda c: ps[:, 4 + c, :]
            return A

        SLOT_PARTS = ((0, 3, 0), (3, 6, 1), (6, 8, 2))
        part = {x: sem(f"part_{x}") for x in ("cut", "rest", "done", "kept", "landed0", "landed1")}
        parts = arena[:, 0:3 * N].bitcast(BF16).rearrange("p (i x k n) -> p i x k n", i=2, x=2, k=3)
        qk6 = arena[:, E1 * FF1:].bitcast(BF16).rearrange("p (x h n) -> p x h n", x=2, h=8)
        q6_st = q_st[:, 0:4, :].rearrange("p c s -> p (c s)").bitcast(BF16).rearrange("p (h s) -> p h s", h=8)
        k6_st = km[:, :, :].rearrange("p j s -> p (j s)").bitcast(BF16).rearrange("p (h s) -> p h s", h=8)

        def part_act(act, layer, ready):
            for i in range(2):
                for x in range(2):
                    act.wait_ge(ready, 2 * i + x + 1)
                    nc.scalar.copy(parts[:, i, x, 0, :], (q_all, k_all)[x][:, half(i)]).then_inc(part["cut"], 1)
                for x in range(2):
                    act.wait_ge(part["rest"], 4 * layer + 2 * i + x + 1)
                    nc.scalar.copy(parts[:, i, x, 1, :], sq[:, half(x)]).then_inc(part["cut"], 1)

        def part_dve(v, layer, i):
            for x in range(2):
                v.wait_ge(part["cut"], 8 * layer + 4 * i + x + 1)
                nc.vector.tensor_tensor(sq[:, half(x)], (q_all, k_all)[x][:, half(i)], parts[:, i, x, 0, :],
                                        ALU.subtract).then_inc(part["rest"], 1)
            for x in range(2):
                v.wait_ge(part["cut"], 8 * layer + 4 * i + x + 3)
                nc.vector.tensor_tensor(parts[:, i, x, 2, :], sq[:, half(x)], parts[:, i, x, 1, :],
                                        ALU.subtract).then_inc(part["done"], 1)

        def part_sp(sp, layer):
            for i in range(2):
                for x in range(2):
                    sp.wait_ge(part["done"], 4 * layer + 2 * i + x + 1)
                    for s0, s1, k in SLOT_PARTS:
                        src = (parts[:, i, x, 0:s1 - s0, :] if x == 0 else
                               parts[:, i, x, k:k + 1, :].broadcast_to([P, s1 - s0, HALF]))
                        sp.dma_start(qkscratch[layer, i, x, s0:s1].rearrange("s f n -> f s n"), src).then_inc(part["kept"], 16)
                sp.wait_ge(part["kept"], 16 * 6 * (2 * layer + i + 1))
                for x in range(2):
                    rows = qkscratch[layer, i, x].rearrange("s (d g h) n -> g (s d) h n", d=HD, g=2)
                    for g in range(2):
                        sp.dma_start(qk6[64 * g:64 * g + 64, x, :, half(i)], rows[g]).then_inc(part[f"landed{i}"], 16)

        def narrow(layer, causal, value, wo):
            A = attention(HD, causal, B, UNITS, 3, 0, True)
            A.ahead = 2

            def score(it, u, banks, nk):
                r = slice(64 * (u % 4 // 2), 64 * (u % 4 // 2) + 64)
                for jp, o in enumerate(banks):
                    for s in range(2):
                        h = (4 * (u % 4) + 2 * jp + s) % 8
                        last = nc.tensor.matmul(o[:, s, 0:nk], q6_st[r, h, tile(A.qt(u))], k6_st[r, h, 0:nk],
                                                start=True, stop=True)
                        if causal:
                            last = nc.tensor.matmul(o[:, s, nk - P:nk], identb[:, :], causalb[:, :],
                                                    start=False, stop=True, skip_group_check=True)
                return last

            def parts_landed(eng, it):
                eng.wait_ge(part["landed0"], 16 * 4 * (layer + 1))
                if not (isinstance(it, int) and it == 0):
                    eng.wait_ge(part["landed1"], 16 * 4 * (layer + 1))

            def stage(v, it):
                parts_landed(v, it)
                for x, dst in enumerate((q6_st, k6_st)):
                    nc.vector.tensor_copy(dst, qk6[:, x, :, bass.ds(it * S, S)]).then_inc(A.staged.sem, 1)

            def stage_values(v, it):
                nc.vector.tensor_copy(v_st[:, :, :], v_all[:, bass.ds(it * 2, 2), :]).then_inc(A.staged.sem, 1)

            A.score, A.stage, A.stage_values, A.value, A.wo = score, stage, stage_values, value, wo
            A.inverse = lambda g: q_st[:, 4 + 2 * (g % 2):6 + 2 * (g % 2), :].rearrange("p a s -> p (a s)")
            A.output = lambda it, g: att[:, bass.ds(it * S + g * P, P)]
            return A

        def value_narrow(it, u, c, j):
            h = 4 * (u % 4) + j
            return v_st[:, c, h * HD:(h + 1) * HD]

        def value_grouped(it, u, c, j):
            h = u % 4
            return v_st[:, c, h * HD:(h + 1) * HD]

        A0 = narrow(0, False, value_narrow, lambda i: w0[:, 5 + i, :])

        def clear_bank(v):
            nc.vector.memset(ps[:, 6, :], 0.0)

        q0, k0, v0 = sem("L0_qk"), sem("L0_qk_done"), sem("L0_v")
        v0d, t0 = sem("L0_v_done"), sem("L0_t")

        def rope_pe(pe, wt, first, other, wait_h, done, qk_from_h):
            for w in range(4):
                src = hT if w < 2 or qk_from_h else other
                for i in range(2):
                    if w == 0:
                        wait_h(pe, i)
                    nc.tensor.matmul(ps[:, 2 * w + i, :], wt[:, w, :], src[:, half(i)], start=True, stop=True).then_inc(done, 1)

        def rope_dve(v, layer, done, rdy, biases, t):
            for i in range(2):
                for w, dst in ((0, q_all), (2, k_all)):
                    cs = 2 - w
                    v.wait_ge(done, 2 * (w + 1) + i + 1)
                    pair = (a_sb, g_sb) if w == 0 else (c_sb, d_sb)
                    for r, tmp in enumerate(pair):
                        nc.vector.scalar_tensor_tensor(
                            tmp[:, i, :].rearrange("p (b s) -> p b s", b=2),
                            ps[:, 2 * (w + r) + i, :].rearrange("p (b s) -> p b s", b=2),
                            biases[w + r], rope[:, cs + r, :].unsqueeze(1).broadcast_to([P, 2, S]),
                            ALU.add, ALU.mult).then_inc(t, 1)
                    v.wait_ge(t, 4 * i + 2 * (w // 2) + 2)
                    nc.vector.tensor_tensor(dst[:, half(i)], pair[0][:, i, :], pair[1][:, i, :], ALU.add).then_inc(rdy, 1)
                part_dve(v, layer, i)

        def l0_attn_pe(pe):
            norm_pe(pe, 0, 0, xT, x_ready(0))
            pe.wait_ge(ld["w0"], 16)
            rope_pe(pe, w0, 0, ctxT, norm_ready(0), q0, False)
            pe.wait_ge(k0, 4)
            for t in range(NT):
                mm = nc.tensor.matmul(ps[:, t // 4, tile(t % 4)], ctxT[:, tile(t)], w0[:, 4, :], start=True, stop=True)
            mm.then_inc(v0, 1)
            attn_pe(pe, A0)

        def values_dve(v, layer, done, vd, heads, width):
            v.wait_ge(done, 1)
            n = heads * width
            for i in range(2):
                o = v_all[:, 4 * i:4 * i + 4, 0:n]
                src = ps[:, i, :].rearrange("p (t n) -> p t n", t=4)[:, :, 0:n]
                if layer is None:
                    nc.vector.tensor_copy(o, src).then_inc(vd, 1)
                else:
                    nc.vector.tensor_tensor(o, src, bv[:, layer:layer + 1, 0:n].broadcast_to([P, 4, n]), ALU.add).then_inc(vd, 1)

        def residual(v, k, i, y, gate, bias, tmp):
            if bias is not None:
                link(v, nc.vector.tensor_scalar(tmp, y, bias, None, ALU.add))
                y = tmp
            nc.vector.scalar_tensor_tensor(xT[:, half(i)], y, gates[:, gate:gate + 1], xT[:, half(i)],
                                           ALU.mult, ALU.add).then_inc(x_done, 1)

        def l0_attn_dve(v):
            v.wait_ge(ld["c"], 16 * len(loads["c"]))
            v.sem_inc(attn_sems["normed"], 1)
            nc.vector.memset(eps[:, :], EPS)
            nc.vector.memset(ones[:, :], 1.0)
            nc.vector.memset(onesb[:, :], 1.0)
            nc.vector.tensor_copy(identb[:, :], ident[:, :])
            nc.vector.tensor_copy(iota_e[:, :], iota[:, 0:E1])
            nc.vector.tensor_copy(beforeb[:, :], before[:, :])
            nc.vector.tensor_copy(causalb[:, :], causal[:, :]).then_inc(made, 1)
            norm_dve(v, 0, 0, xT, hT, None)
            rope_dve(v, 0, q0, k0, [col(C_BQ0), col(C_BQR0), col(C_BK0), col(C_BKR0)], t0)
            v.wait_ge(k0, 4)
            values_dve(v, 0, v0, v0d, H, HD)
            v.wait_ge(v0d, 2)
            clear_bank(v)
            attn_dve(v, A0)
            v.wait_ge(gated, 1)
            for i in range(2):
                until(v, A0.stored, 2 * B)
                residual(v, 0, i, att[:, half(i)], 0, col(C_BO0), a_sb[:, i, :])

        def l0_attn_act(act):
            act.wait_ge(ld["c"], 16 * len(loads["c"]))
            act.sem_inc(attn_sems["stored"], 1)
            nc.scalar.activation(gates[:, :], gates[:, :], ACT.Tanh).then_inc(gated, 1)
            act.wait_ge(made, 1)
            norm_act(act, 0, 0, xT, x_ready(0))
            part_act(act, 0, k0)
            attn_act(act, A0)

        def by_tile(ap, e):
            return ap.rearrange("p (t e) -> p t e", e=e)

        def logits_pe(pe, k, first, e, done):
            for t in range(NT):
                pe.wait_ge(n_out, 2 * k + t // 4 + 1)
                mm = nc.tensor.matmul(ps[:, 4, t * e:(t + 1) * e], hT[:, tile(t)], gw[:, first:first + e], start=True, stop=True)
            mm.then_inc(done, 1)

        def softmax_dve(v, e, done, shifted, exped):
            v.wait_ge(done, 1)
            z = by_tile(ps[:, 4, 0:NT * e], e)
            link(v, nc.vector.tensor_reduce(small[:, 0, :], z, X, ALU.max))
            nc.vector.tensor_tensor(lg[:, :, 0:e], z, small[:, 0, :].unsqueeze(2).broadcast_to([P, NT, e]),
                                    ALU.subtract).then_inc(shifted, 1)
            v.wait_ge(exped, 1)
            link(v, nc.vector.tensor_reduce(small[:, 1, :], lg[:, :, 0:e], X, ALU.add))
            link(v, nc.vector.reciprocal(small[:, 2, :], small[:, 1, :]))
            link(v, nc.vector.tensor_tensor(lg[:, :, 0:e], lg[:, :, 0:e],
                                            small[:, 2, :].unsqueeze(2).broadcast_to([P, NT, e]), ALU.mult))

        def softmax_act(act, e, shifted, exped):
            act.wait_ge(shifted, 1)
            nc.scalar.activation(lg[:, :, 0:e], lg[:, :, 0:e], ACT.Exp).then_inc(exped, 1)

        def choose(v, src, e, ks):
            for t in range(NT):
                ins = nc.vector.max(top8[:, t, :], src[:, t, 0:e])
            link(v, ins)
            for t in range(NT):
                ins = nc.vector.max_index(idx8[:, t, :], top8[:, t, :], src[:, t, 0:e])
            link(v, ins)
            link(v, nc.vector.tensor_copy(idxf[:, :, :], idx8[:, :, 0:2]))
            for k in range(ks):
                ins = nc.vector.tensor_tensor(oh[:, k, :, 0:e], iota_e[:, 0:e].unsqueeze(1).broadcast_to([P, NT, e]),
                                              idxf[:, :, k:k + 1].broadcast_to([P, NT, e]), ALU.is_equal)
            link(v, ins)
            if ks == 2:
                link(v, nc.vector.tensor_tensor(oh[:, 2, :, 0:e], oh[:, 0, :, 0:e], oh[:, 1, :, 0:e], ALU.add))

        def ranks_pe(pe, e, sel_ready, done):
            pe.wait_ge(sel_ready, 1)
            flat = selb[:, :, 0:e]
            nc.tensor.matmul(by_tile(ps[:, 5, 0:NT * e], e), beforeb[:, :], flat, start=True, stop=False, skip_group_check=True)
            for t in range(NT - 1):
                mm = nc.tensor.matmul(by_tile(ps[:, 5, (t + 1) * e:NT * e], e), onesb[:, :],
                                      selb[:, t:t + 1, 0:e].broadcast_to([P, NT - 1 - t, e]),
                                      start=False, stop=(t == NT - 2), skip_group_check=True)
            mm.then_inc(done, 1)

        weigh3 = {x: sem(f"weights_{x}") for x in ("parts", "turned", "ready")}
        comb3 = q_st[:, 0:2, :].rearrange("p c s -> p (c s)").bitcast(BF16)[0:3 * EW, 0:N]
        pick3 = km[:, :, :].rearrange("p j s -> p (j s)").bitcast(BF16)[0:3 * EW, 0:EW * P].rearrange("p (e m) -> p e m", e=EW)

        def weights_dve(v):
            link(v, nc.vector.tensor_copy(cparts[:, :, 0, :], comb[:, :, :]))
            link(v, nc.vector.tensor_tensor(crest[:, :, :], comb[:, :, :], cparts[:, :, 0, :], ALU.subtract))
            link(v, nc.vector.tensor_copy(cparts[:, :, 1, :], crest[:, :, :]))
            nc.vector.tensor_tensor(cparts[:, :, 2, :], crest[:, :, :], cparts[:, :, 1, :], ALU.subtract).then_inc(weigh3["parts"], 1)
            nc.vector.tensor_copy(pick3, rows3[0:3 * EW, :].unsqueeze(2).broadcast_to([3 * EW, EW, P])).then_inc(weigh3["parts"], 1)

        def weights_pe(pe, k):
            pe.wait_ge(weigh3["parts"], 2 * k + 1)
            for t in range(NT):
                mm = nc.tensor.matmul(ps[0:3 * EW, 6 + t // 4, tile(t % 4)], cparts[:, t, :, :].rearrange("p k e -> p (k e)"),
                                      identb[:, :], start=True, stop=True)
            mm.then_inc(weigh3["turned"], 1)

        def weights_act(act, k):
            act.wait_ge(weigh3["turned"], k + 1)
            for i in range(2):
                nc.scalar.copy(comb3[:, half(i)], ps[0:3 * EW, 6 + i, :]).then_inc(weigh3["ready"], 1)

        def weights_ready(pe, k):
            pe.wait_ge(weigh3["ready"], 2 * (k + 1))
            pe.wait_ge(weigh3["parts"], 2 * (k + 1))

        def weights_spread(bank, e, i):
            return nc.tensor.matmul(ps[:, bank, :], pick3[:, e, :], comb3[:, half(i)], start=True, stop=True)

        class Mlp:

            upped, silued, mixed, acted, downed = (sem(f"mlp_{x}") for x in ("upped", "silued", "mixed", "acted", "downed"))

            def __init__(self, counted, base, experts, parts, weighed):
                self.counted = counted
                self.units = [(e, i, c) for e in range(experts) for i in range(2) for c in range(parts)]
                self.weights = lambda e, c, w: mA[:, base + ((e * parts + c) * 3 + w) * D:base + ((e * parts + c) * 3 + w + 1) * D]
                self.parts, self.weighed, self.last = parts, weighed, (experts - 1, parts - 1)

        def mlp_pe(pe, M, before_first):
            def up(n):
                e, i, c = M.units[n]
                if n >= 2:
                    pe.wait_ge(M.acted, M.counted + n - 1)
                nc.tensor.matmul(ps[:, 2 + n % 2, :], M.weights(e, c, 0), hT[:, half(i)], start=True, stop=True)
                mm = nc.tensor.matmul(ps[:, 4 + n % 2, :], M.weights(e, c, 1), hT[:, half(i)], start=True, stop=True)
                if M.weighed and c == 0:
                    mm = weights_spread(6 + n // M.parts % 2, e, i)
                mm.then_inc(M.upped, 1)

            def down(n):
                e, i, c = M.units[n]
                pe.wait_ge(M.acted, M.counted + n + 1)
                nc.tensor.matmul(ps[:, i, :], M.weights(e, c, 2), a_sb[:, n % 2, :], start=(e == 0 and c == 0),
                                 stop=((e, c) == M.last), skip_group_check=True).then_inc(M.downed, 1)

            before_first(pe)
            up(0)
            for n in range(len(M.units)):
                if n + 1 < len(M.units):
                    up(n + 1)
                down(n)

        def mlp_act(act, M):
            for n in range(len(M.units)):
                act.wait_ge(M.upped, M.counted + n + 1)
                if n >= 2:
                    act.wait_ge(M.mixed, M.counted + n - 1)
                nc.scalar.activation(g_sb[:, n % 2, :], ps[:, 2 + n % 2, :], ACT.Silu).then_inc(M.silued, 1)

        def mlp_dve(v, M):
            for n in range(len(M.units)):
                v.wait_ge(M.silued, M.counted + n + 1)
                if n >= 2:
                    v.wait_ge(M.downed, M.counted + n - 1)
                ins = nc.vector.tensor_tensor(a_sb[:, n % 2, :], g_sb[:, n % 2, :], ps[:, 4 + n % 2, :], ALU.mult)
                ins.then_inc(M.mixed, 1)
                if M.weighed:
                    v.wait_ge(M.mixed, M.counted + n + 1)
                    ins = nc.vector.tensor_tensor(a_sb[:, n % 2, :], a_sb[:, n % 2, :],
                                                  ps[:, 6 + n // M.parts % 2, :], ALU.mult).then_inc(M.acted, 1)
                else:
                    v.wait_ge(M.mixed, M.counted + n + 1)
                    v.sem_inc(M.acted, 1)

        r0 = [sem(f"R0_{x}") for x in ("logits", "shifted", "exped", "chosen", "ranked")]
        M0 = Mlp(0, 0, 10, 1, True)

        def l0_ffn_pe(pe):
            norm_pe(pe, 1, 1, xT, x_ready(1))
            logits_pe(pe, 1, 0, E0, r0[0])
            ranks_pe(pe, E0, r0[3], r0[4])

            weights_pe(pe, 0)

            def first(pe):
                pe.wait_ge(ld["m0"], 16)
                weights_ready(pe, 0)
            mlp_pe(pe, M0, first)

        def l0_ffn_act(act):
            norm_act(act, 1, 1, xT, x_ready(1))
            softmax_act(act, E0, r0[1], r0[2])
            weights_act(act, 0)
            mlp_act(act, M0)

        def l0_ffn_dve(v):
            norm_dve(v, 1, 1, xT, hT, None)
            softmax_dve(v, E0, r0[0], r0[1], r0[2])
            choose(v, lg, E0, 2)
            nc.vector.tensor_copy(selb[:, :, 0:E0], oh[:, 2, :, 0:E0]).then_inc(r0[3], 1)
            link(v, nc.vector.tensor_tensor(small[:, 3, :], top8[:, :, 0], top8[:, :, 1], ALU.add))
            link(v, nc.vector.tensor_scalar(small[:, 3, :], small[:, 3, :], 1e-20, None, ALU.add))
            link(v, nc.vector.reciprocal(small[:, 4, :], small[:, 3, :]))
            link(v, nc.vector.tensor_tensor(lg[:, :, 0:E0], lg[:, :, 0:E0],
                                            small[:, 4, :].unsqueeze(2).broadcast_to([P, NT, E0]), ALU.mult))
            link(v, nc.vector.tensor_tensor(lg[:, :, 0:E0], lg[:, :, 0:E0], oh[:, 2, :, 0:E0], ALU.mult))
            v.wait_ge(r0[4], 1)
            link(v, nc.vector.tensor_scalar(lg2[:, :, 0:E0], by_tile(ps[:, 5, 0:NT * E0], E0), float(CAP0), None, ALU.is_lt))
            nc.vector.memset(comb[:, :, E0:E0 + 2], 1.0)
            link(v, nc.vector.tensor_tensor(comb[:, :, 0:E0], lg[:, :, 0:E0], lg2[:, :, 0:E0], ALU.mult))
            weights_dve(v)
            mlp_dve(v, M0)
            for i in range(2):
                v.wait_ge(M0.downed, M0.counted + len(M0.units))
                residual(v, 1, i, ps[:, i, :], 1, None, None)

        WB = 8 * P + P + DH + 8 * P
        M1 = Mlp(20, 30 * D, 4, 1, False)
        cT = k_all

        def wide(causal, base, q_src, k_src):
            A = attention(DH, causal, B, UNITS, 6, 9, True)
            A.head = lambda j: j // 2 + 2 * (j % 2)

            def project(pe, it, part):
                cols_ = bass.ds(it * S, S)
                for c in (range(8), (8,))[part]:
                    src = q_src if c < 8 else k_src
                    nc.tensor.matmul(ps[:, c // 2, (c % 2) * S:(c % 2 + 1) * S], w1[:, base + P * c:base + P * c + P],
                                     src[:, cols_], start=True, stop=True).then_inc(A.projected.sem, 1)

            def stage(v, it):
                for c in range(0, 4, 2):
                    until(v, A.projected, it * 9 + c + 2)
                    nc.vector.tensor_copy(q_st[:, c:c + 2, :].rearrange("p c s -> p (c s)"),
                                          ps[:, c // 2, :]).then_inc(A.staged.sem, 1)
                until(v, A.projected, it * 9 + 9)
                nc.vector.tensor_scalar(km[:, 0, :], ps[:, 4, 0:S], DH ** -0.5, None, ALU.mult).then_inc(A.staged.sem, 1)

            def stage_values(v, it):
                nc.vector.tensor_copy(v_st[:, :, 0:DH], v_all[:, bass.ds(it * 2, 2), 0:DH]).then_inc(A.staged.sem, 1)

            def stage_act(act, it):
                for c in range(4, 8, 2):
                    until(act, A.projected, it * 9 + c + 2)
                    nc.scalar.copy(q_st[:, c:c + 2, :].rearrange("p c s -> p (c s)"),
                                   ps[:, c // 2, :]).then_inc(A.staged.sem, 1)

            def score(it, u, banks, nk):
                for s in range(2):
                    for jp, o in enumerate(banks):
                        r = slice(DH * jp, DH * jp + DH)
                        last = nc.tensor.matmul(o[:, s, 0:nk], q_st[r, 2 * (u % 4) + s, tile(A.qt(u))], km[r, 0, 0:nk],
                                                start=True, stop=True)
                    for o in banks:
                        if causal:
                            last = nc.tensor.matmul(o[:, s, nk - P:nk], identb[:, :], causalb[:, :],
                                                    start=False, stop=True, skip_group_check=True)
                return last

            A.project, A.stage, A.stage_values, A.stage_act, A.score = project, stage, stage_values, stage_act, score
            A.value = lambda it, u, c, p: v_st[:, c, 0:DH]
            A.inverse = lambda g: km[:, 1 + g % 2, :]
            A.output = lambda it, u: big[:, 2 * (u % 4):2 * (u % 4) + 2, bass.ds(it * S + A.qt(u) * P, P)]
            return A

        A1a = wide(True, 0, hT, hT)
        A1b = wide(False, WB, hT, cT)
        v1 = [[sem(f"L1{x}_v"), sem(f"L1{x}_v_done"), sem(f"L1{x}_o")] for x in "ab"]
        y1 = sem("L1_y")

        def wide_pe(pe, A, base, v_src, s):
            for t in range(NT):
                mm = nc.tensor.matmul(ps[:, t // 4, (t % 4) * P:(t % 4) * P + DH], v_src[:, tile(t)],
                                      w1[:, base + 9 * P:base + 9 * P + DH], start=True, stop=True)
            mm.then_inc(s[0], 1)
            pe.wait_ge(s[1], 2)
            attn_pe(pe, A)
            until(pe, A.normed, A.groups * B)
            for i in range(2):
                for c in range(8):
                    w = w1[:, base + 9 * P + DH + P * c:base + 9 * P + DH + P * c + P]
                    mm = nc.tensor.matmul(ps[:, i, :], w, big[:, c, half(i)], start=(c == 0), stop=(c == 7))
                mm.then_inc(s[2], 1)

        def l1_attn_pe(pe):
            norm_pe(pe, 2, 2, xT, x_ready(2))
            norm_pe(pe, 3, 3, h1T, norm_ready(2))
            norm_pe(pe, 4, 4, ctxT, norm_ready(3))

            def first(pe):
                pe.wait_ge(ld["w1"], 32)
                pe.wait_ge(n_out, 10)
            mlp_pe(pe, M1, first)
            pe.wait_ge(y1, 2)
            wide_pe(pe, A1a, 0, hT, v1[0])
            norm_pe(pe, 5, 5, h1T, lambda e, i: e.wait_ge(y1, 3 + i))
            pe.wait_ge(n_out, 12)
            wide_pe(pe, A1b, WB, cT, v1[1])

        def l1_attn_act(act):
            norm_act(act, 2, 2, xT, None)
            norm_act(act, 3, 3, h1T, None)
            norm_act(act, 4, 4, ctxT, None)
            mlp_act(act, M1)
            attn_act(act, A1a)
            norm_act(act, 5, 5, h1T, None)
            attn_act(act, A1b)

        def l1_attn_dve(v):
            norm_dve(v, 2, 2, xT, h1T, None)
            norm_dve(v, 3, 3, h1T, hT, col(C_PTB))
            norm_dve(v, 4, 4, ctxT, cT, col(C_CTX))
            mlp_dve(v, M1)
            v.wait_ge(M1.downed, M1.counted + len(M1.units))
            for i in range(2):
                nc.vector.tensor_tensor(h1T[:, half(i)], h1T[:, half(i)], ps[:, i, :], ALU.add).then_inc(y1, 1)
            values_dve(v, None, v1[0][0], v1[0][1], 1, DH)
            v.wait_ge(v1[0][1], 2)
            attn_dve(v, A1a)
            v.wait_ge(y1, 2)
            for i in range(2):
                v.wait_ge(v1[0][2], i + 1)
                nc.vector.tensor_tensor(h1T[:, half(i)], h1T[:, half(i)], ps[:, i, :], ALU.add).then_inc(y1, 1)
            norm_dve(v, 5, 5, h1T, hT, col(C_CA))
            values_dve(v, None, v1[1][0], v1[1][1], 1, DH)
            v.wait_ge(v1[1][1], 2)
            attn_dve(v, A1b)
            for i in range(2):
                v.wait_ge(v1[1][2], i + 1)
                residual(v, 2, i, ps[:, i, :], 2, None, None)

        r1 = [sem(f"R1_{x}") for x in ("logits", "shifted", "exped", "chosen", "ranked", "ready")]
        f1 = {x: sem(f"F1_{x}") for x in ("turned", "tokens", "spread", "spread_sb", "hot", "sent", "gathered",
                                          "up", "gelu", "down", "out", "pick", "y")}
        htok = q_st[:, :, :].rearrange("p c s -> p (c s)")[:, 0:N]
        xd = w1[:, 0:SLOTS]
        hot = w1[:, SLOTS:3 * SLOTS].rearrange("p (b s) -> p b s", b=2)
        eo = mA[:, 0:E1 * D]
        slotB, weightB = xc, h1T
        pick = prob[:, :, :, :].rearrange("p a j k -> p (a j k)")[:, 0:4 * HALF].rearrange("p (b n) -> p b n", b=4)
        hg = km[:, :, :].rearrange("p j s -> p (j s)")[:, 0:640].rearrange("p (b n) -> p b n", b=2)
        slot = small[:, 6, :]
        weight = small[:, 7, :]
        chunks = [(0, 512), (512, 1024), (1024, SLOTS)]

        def l1_ffn_pe(pe):
            norm_pe(pe, 6, 6, xT, x_ready(3))
            logits_pe(pe, 6, E0, E1, r1[0])
            for t in range(NT):
                mm = nc.tensor.transpose(ps[:, t // 4, tile(t % 4)], hT[:, tile(t)], ident[:, :])
            mm.then_inc(f1["turned"], 1)
            ranks_pe(pe, E1, r1[3], r1[4])
            pe.wait_ge(r1[5], 1)
            pe.wait_ge(f1["tokens"], 2)
            for w, src in enumerate((slot, weight)):
                for t in range(NT):
                    mm = nc.tensor.matmul(ps[:, (6, 0)[w] + t // 4, tile(t % 4)], src[:, t:t + 1].broadcast_to([P, P]),
                                          ident[:, :], start=True, stop=True)
                mm.then_inc(f1["spread"], 1)
            for t in range(NT):
                pe.wait_ge(f1["hot"], t + 1)
                for c, (lo, hi) in enumerate(chunks):
                    mm = nc.tensor.matmul(ps[:, 2 + c, 0:hi - lo], htok[:, tile(t)], hot[:, t % 2, lo:hi],
                                          start=(t == 0), stop=(t == NT - 1))
                mm.then_inc(f1["sent"], 1)
            pe.wait_ge(f1["gathered"], 3)
            pe.wait_ge(f1["spread_sb"], 4)
            pe.wait_ge(ld["e1"], 32)

            def up(e):
                if e >= 2:
                    pe.wait_ge(f1["gelu"], e - 1)
                for c in range(4):
                    mm = nc.tensor.matmul(ps[:, 6 + e % 2, CAP1 * c:CAP1 * c + CAP1], arena[:, FF1 * e + P * c:FF1 * e + P * c + P],
                                          xd[:, CAP1 * e:CAP1 * e + CAP1], start=True, stop=True)
                mm.then_inc(f1["up"], 1)

            up(0)
            for e in range(E1):
                if e + 1 < E1:
                    up(e + 1)
                pe.wait_ge(f1["gelu"], e + 1)
                if e >= 2:
                    pe.wait_ge(f1["out"], e - 1)
                for c in range(4):
                    w = E1 * FF1 + FF1 * e + P * c
                    mm = nc.tensor.matmul(ps[0:CAP1, e % 2, 0:D], hg[:, e % 2, CAP1 * c:CAP1 * c + CAP1],
                                          arena[:, w:w + P], start=(c == 0), stop=(c == 3))
                mm.then_inc(f1["down"], 1)
            for e in range(E1):
                pe.wait_ge(f1["out"], e + 1)
                for i in range(2):
                    n = 2 * e + i
                    pe.wait_ge(f1["pick"], n + 1)
                    nc.tensor.matmul(ps[:, 2 + i, :], eo[0:CAP1, tile(e)], pick[0:CAP1, n % 4, :],
                                     start=(e == 0), stop=(e == E1 - 1), skip_group_check=True).then_inc(f1["y"], 1)

        def l1_ffn_act(act):
            norm_act(act, 6, 6, xT, None)
            softmax_act(act, E1, r1[1], r1[2])
            act.wait_ge(f1["turned"], 1)
            for i in range(2):
                nc.scalar.copy(htok[:, half(i)], ps[:, i, :]).then_inc(f1["tokens"], 1)
            for w, dst in enumerate((slotB, weightB)):
                act.wait_ge(f1["spread"], w + 1)
                for i in range(2):
                    nc.scalar.copy(dst[:, half(i)], ps[:, (6, 0)[w] + i, :]).then_inc(f1["spread_sb"], 1)
            for e in range(E1):
                act.wait_ge(f1["up"], e + 1)
                if e >= 2:
                    act.wait_ge(f1["down"], e - 1)
                nc.scalar.activation(hg[:, e % 2, :], ps[:, 6 + e % 2, 0:4 * CAP1], ACT.Gelu_apprx_tanh).then_inc(f1["gelu"], 1)

        def l1_ffn_dve(v):
            norm_dve(v, 6, 6, xT, hT, None)
            softmax_dve(v, E1, r1[0], r1[1], r1[2])
            link(v, nc.vector.tensor_copy(lg2[:, :, :], by_tile(ps[:, 4, 0:NT * E1], E1)))
            choose(v, lg2, E1, 1)
            nc.vector.tensor_copy(selb[:, :, :], oh[:, 0, :, :]).then_inc(r1[3], 1)
            link(v, nc.vector.tensor_tensor(lg[:, :, :], lg[:, :, :], oh[:, 0, :, :], ALU.mult))
            link(v, nc.vector.tensor_reduce(weight, lg[:, :, :], X, ALU.add))
            v.wait_ge(r1[4], 1)
            link(v, nc.vector.tensor_tensor(lg2[:, :, :], by_tile(ps[:, 5, 0:NT * E1], E1), oh[:, 0, :, :], ALU.mult))
            link(v, nc.vector.tensor_reduce(small[:, 3, :], lg2[:, :, :], X, ALU.add))
            link(v, nc.vector.tensor_scalar(small[:, 4, :], small[:, 3, :], float(CAP1), 2.0 * SLOTS, ALU.is_ge, ALU.mult))
            link(v, nc.vector.tensor_tensor(small[:, 4, :], small[:, 4, :], small[:, 3, :], ALU.add))
            nc.vector.scalar_tensor_tensor(slot, idxf[:, :, 0], float(CAP1), small[:, 4, :], ALU.mult, ALU.add).then_inc(r1[5], 1)
            v.wait_ge(r1[5], 1)
            for t in range(NT):
                if t >= 2:
                    v.wait_ge(f1["sent"], t - 1)
                nc.vector.tensor_scalar(hot[:, t % 2, :], iota[:, :], slot[:, t:t + 1], None, ALU.is_equal).then_inc(f1["hot"], 1)
            v.wait_ge(f1["sent"], NT)
            for c, (lo, hi) in enumerate(chunks):
                nc.vector.tensor_copy(xd[:, lo:hi], ps[:, 2 + c, 0:hi - lo]).then_inc(f1["gathered"], 1)
            v.wait_ge(narrowed, 2)
            for e in range(E1):
                v.wait_ge(f1["down"], e + 1)
                nc.vector.tensor_copy(eo[0:CAP1, tile(e)], ps[0:CAP1, e % 2, 0:D]).then_inc(f1["out"], 1)
            v.wait_ge(f1["spread_sb"], 4)
            for e in range(E1):
                for i in range(2):
                    n = 2 * e + i
                    if n >= 4:
                        v.wait_ge(f1["y"], n - 3)
                    nc.vector.tensor_scalar(pick[0:CAP1, n % 4, :], slotB[0:CAP1, half(i)], slot_of[0:CAP1, e:e + 1], None,
                                            ALU.is_equal).then_inc(f1["pick"], 1)
            v.wait_ge(f1["y"], 2 * E1)
            for i in range(2):
                link(v, nc.vector.tensor_tensor(weightB[:, half(i)], ps[:, 2 + i, :], weightB[:, half(i)], ALU.mult))
                residual(v, 3, i, weightB[:, half(i)], 3, None, None)

        progs = {"pe": [l0_attn_pe, l0_ffn_pe, l1_attn_pe, l1_ffn_pe],
                 "dve": [l0_attn_dve, l0_ffn_dve, l1_attn_dve, l1_ffn_dve],
                 "act": [l0_attn_act, l0_ffn_act, l1_attn_act, l1_ffn_act]}

        a2 = {x: sem(f"A2_{x}") for x in ("proj", "q", "prod", "kext", "vals", "vtok", "vext", "scored", "maxed",
                                          "exped", "turned", "moved", "weighed", "mixed", "outturned")}
        prod = prob[:, 0, :, :].rearrange("p j k -> p (j k)")
        prob2 = prob[:, 1, :, :].rearrange("p j k -> p (j k)").rearrange("p (b n) -> p b n", b=2)
        pT2 = probT[:, :, 0, 0:S]
        v_tok = arena[:, 0:N].rearrange("p (t n) -> p t n", t=NT)
        v_ext = arena[:, N:2 * N].rearrange("p (t n) -> p t n", t=NT)

        def l2_attn_pe(pe):
            norm_pe(pe, 7, 7, xT, x_ready(4))
            pe.wait_ge(ld["w2"], 32)
            for w, src in enumerate((hT, hT, ctxT)):
                for i in range(2):
                    if w == 0:
                        pe.wait_ge(n_out, 15 + i)
                    nc.tensor.matmul(ps[:, 2 * w + i, :], w2x[:, min(w, 1), :], src[:, half(i)],
                                     start=True, stop=True).then_inc(a2["proj"], 1)
            for w, src in enumerate((hT, ctxT)):
                for i in range(2):
                    b = (6, 0)[w] + i
                    if w == 1 and i == 0:
                        pe.wait_ge(a2["q"], 2)
                    for t in range(4):
                        mm = nc.tensor.matmul(ps[:, b, tile(t)], src[:, tile(4 * i + t)], w2x[:, 2, :], start=True, stop=True)
                    mm.then_inc(a2["vals"], 1)
            pe.wait_ge(a2["prod"], 2)
            pe.wait_ge(a2["kext"], 2)
            pe.wait_ge(a2["vext"], 2)
            pe.wait_ge(a2["vtok"], 2)

            def scores(t):
                if t >= 2:
                    pe.wait_ge(a2["exped"], t - 1)
                nc.tensor.matmul(ps[:, t % 2, 0:S], q_all[:, tile(t)], k_all[:, S * (t // 2):S * (t // 2) + S],
                                 start=True, stop=True)
                nc.tensor.matmul(ps[:, t % 2, S:S + 1], prod[:, tile(t)], ones[:, 0:1], start=True, stop=True).then_inc(a2["scored"], 1)

            def out_turn(t):
                pe.wait_ge(a2["mixed"], t + 1)
                nc.tensor.transpose(ps[:, 6 + t // 4, tile(t % 4)], onorm[:, tile(t % 2)], ident[:, :]).then_inc(a2["outturned"], 1)

            scores(0)
            for t in range(NT):
                if t + 1 < NT:
                    scores(t + 1)
                pe.wait_ge(a2["exped"], t + 1)
                if t >= 2:
                    pe.wait_ge(a2["moved"], t - 1)
                for c in range(2):
                    mm = nc.tensor.transpose(ps[:, 2 + t % 2, tile(c)], prob2[:, t % 2, tile(c)], ident[:, :])
                mm.then_inc(a2["turned"], 1)
                if t >= 1:
                    out_turn(t - 1)
                pe.wait_ge(a2["moved"], t + 1)
                if t >= 2:
                    pe.wait_ge(a2["mixed"], t - 1)
                for c in range(2):
                    mm = nc.tensor.matmul(ps[:, 4 + t % 2, 0:D], pT2[:, t % 2, tile(c)], v_ext[:, 2 * (t // 2) + c, :],
                                          start=(c == 0), stop=(c == 1))
                mm.then_inc(a2["weighed"], 1)
            out_turn(NT - 1)

        def l2_attn_act(act):
            norm_act(act, 7, 7, xT, None)
            for i in range(2):
                act.wait_ge(a2["proj"], 5 + i)
                nc.scalar.activation(k_all[:, half(i)], ps[:, 4 + i, :], ACT.Identity, bias=col(C_BK2)).then_inc(a2["kext"], 1)
            for t in range(NT):
                act.wait_ge(a2["maxed"], t + 1)
                if t >= 2:
                    act.wait_ge(a2["mixed"], t - 1)
                nc.scalar.activation(prob2[:, t % 2, 0:S + 1], ps[:, t % 2, 0:S + 1], ACT.Exp, bias=negmax[:, t % 2, 0:1],
                                     accum_out=rsum[:, t % 2, 0:1]).then_inc(a2["exped"], 1)

        def l2_attn_dve(v):
            norm_dve(v, 7, 7, xT, hT, None)
            for i in range(2):
                v.wait_ge(a2["proj"], 1 + i)
                nc.vector.tensor_scalar(q_all[:, half(i)], ps[:, i, :], col(C_BQ2), None, ALU.add).then_inc(a2["q"], 1)
            for i in range(2):
                v.wait_ge(a2["proj"], 3 + i)
                v.wait_ge(a2["q"], 1 + i)
                nc.vector.scalar_tensor_tensor(prod[:, half(i)], ps[:, 2 + i, :], col(C_BK2), q_all[:, half(i)],
                                               ALU.add, ALU.mult).then_inc(a2["prod"], 1)
            for w, dst in enumerate((v_tok, v_ext)):
                for i in range(2):
                    v.wait_ge(a2["vals"], 2 * w + i + 1)
                    nc.vector.tensor_tensor(dst[:, 4 * i:4 * i + 4, :], ps[:, (6, 0)[w] + i, :].rearrange("p (t n) -> p t n", t=4),
                                            bv[:, 1:2, :].broadcast_to([P, 4, D]), ALU.add).then_inc(a2[("vtok", "vext")[w]], 1)
            v.wait_ge(a2["vtok"], 2)

            def mix(t):
                v.wait_ge(a2["weighed"], t + 1)
                if t >= 2:
                    v.wait_ge(a2["outturned"], t - 1)
                o = onorm[:, tile(t % 2)]
                link(v, nc.vector.reciprocal(rsum[:, t % 2, 1:2], rsum[:, t % 2, 0:1]))
                link(v, nc.vector.scalar_tensor_tensor(o, v_tok[:, t, :], prob2[:, t % 2, S:S + 1], ps[:, 4 + t % 2, 0:D],
                                                       ALU.mult, ALU.add))
                nc.vector.tensor_scalar(o, o, rsum[:, t % 2, 1:2], None, ALU.mult).then_inc(a2["mixed"], 1)

            for t in range(NT):
                v.wait_ge(a2["scored"], t + 1)
                nc.vector.tensor_reduce(negmax[:, t % 2, 0:1], ps[:, t % 2, 0:S + 1], X, ALU.max, negate=True).then_inc(a2["maxed"], 1)
                if t >= 1:
                    mix(t - 1)
                v.wait_ge(a2["turned"], t + 1)
                nc.vector.tensor_copy(pT2[:, t % 2, :], ps[:, 2 + t % 2, 0:S]).then_inc(a2["moved"], 1)
            mix(NT - 1)
            for i in range(2):
                v.wait_ge(a2["outturned"], 4 * (i + 1))
                residual(v, 4, i, ps[:, 6 + i, :], 4, None, None)

        r2 = [sem(f"R2_{x}") for x in ("logits", "exped")]
        f2 = {x: sem(f"F2_{x}") for x in ("up", "relu", "square", "scale", "down", "rounded", "summed",
                                          "sup", "srelu", "ssq", "y")}
        sh_up = iota[:, 512:512 + HID2]
        sh_dn = iota[:, 512 + HID2:512 + HID2 + 2 * D].rearrange("p (c n) -> p c n", c=2)
        bfv = big[:, 4:8, :].rearrange("p c t -> p (c t)").bitcast(BF16).rearrange("p (k n) -> p k n", n=HALF)
        xin = [bfv[:, b, :] for b in range(2)]
        hr = [[bfv[:, 2 + 2 * b + c, :] for c in range(2)] for b in range(2)]
        hq = [[bfv[:, 6 + 2 * b + c, :] for c in range(2)] for b in range(2)]
        yb = [bfv[:, 10 + b, :] for b in range(2)]
        sr = [big[:, 2 + c, 0:HALF] for c in range(2)]
        widths = (P, HID2B)
        n2 = 2 * E2

        def l2_ffn_pe(pe):
            norm_pe(pe, 8, 8, xT, x_ready(5))
            logits_pe(pe, 8, E0 + E1, E2, r2[0])
            weights_pe(pe, 1)
            pe.wait_ge(narrowed, 2)
            pe.wait_ge(ld["r3"], 16 * len(loads["r3"]))
            for i in range(2):
                if i:
                    pe.wait_ge(f2["ssq"], 2 * i)
                for c in range(2):
                    m = widths[c]
                    nc.tensor.matmul(ps[0:m, 2 + c, :], sh_up[:, P * c:P * c + m], hT[:, half(i)], start=True,
                                     stop=True).then_inc(f2["sup"], 1)
                for c in range(2):
                    m = widths[c]
                    pe.wait_ge(f2["ssq"], 2 * i + c + 1)
                    nc.tensor.matmul(ps[:, i, :], sh_dn[0:m, c, :], sr[c][0:m, :], start=(c == 0), stop=False,
                                     skip_group_check=True).then_inc(f2["y"], 1)

            def spread(n):
                e, i = n // 2, n % 2
                if n >= 2:
                    pe.wait_ge(f2["scale"], n - 1)
                mm = weights_spread(6 + n % 2, e, i)
                mm.then_inc(f2["up"], 1)

            def up(n):
                e = n // 2
                pe.wait_ge(f2["scale"], n + 1)
                if n >= 1:
                    pe.wait_ge(f2["relu"], 2 * n)
                for c in range(2):
                    m = widths[c]
                    mm = nc.tensor.matmul(ps[0:m, 2 + c, :], up2[:, e, P * c:P * c + m], xin[n % 2], start=True, stop=True)
                mm.then_inc(f2["sup"], 1)

            def down(n):
                e = n // 2
                pe.wait_ge(f2["square"], 2 * n + 2)
                if n >= 2:
                    pe.wait_ge(f2["rounded"], n - 1)
                for c in range(2):
                    m = widths[c]
                    mm = nc.tensor.matmul(ps[:, 4 + n % 2, :], dn2[0:m, e, c, :], hq[n % 2][c][0:m, :],
                                          start=(c == 0), stop=(c == 1))
                mm.then_inc(f2["down"], 1)

            def add(n):
                pe.wait_ge(f2["rounded"], n + 1)
                nc.tensor.matmul(ps[:, n % 2, :], identb[:, :], yb[n % 2], start=False, stop=(n >= n2 - 2),
                                 skip_group_check=True).then_inc(f2["summed"], 1)

            pe.wait_ge(f2["ssq"], 4)
            weights_ready(pe, 1)
            spread(0)
            for n in range(n2 + 2):
                if n + 1 < n2:
                    spread(n + 1)
                if n < n2:
                    up(n)
                if 1 <= n <= n2:
                    down(n - 1)
                if n >= 2:
                    add(n - 2)

        def l2_ffn_act(act):
            norm_act(act, 8, 8, xT, None)
            act.wait_ge(r2[0], 1)
            nc.scalar.activation(lg[:, :, 0:E2], by_tile(ps[:, 4, 0:NT * E2], E2), ACT.Exp, scale=-1.0).then_inc(r2[1], 1)
            weights_act(act, 1)
            for i in range(2):
                for c in range(2):
                    m = widths[c]
                    act.wait_ge(f2["sup"], 2 * i + c + 1)
                    if i:
                        act.wait_ge(f2["y"], c + 1)
                    nc.scalar.activation(sr[c][0:m, :], ps[0:m, 2 + c, :], ACT.Relu).then_inc(f2["srelu"], 1)
            for n in range(n2 + 1):
                if n < n2:
                    act.wait_ge(f2["sup"], 4 + n + 1)
                    if n >= 2:
                        act.wait_ge(f2["square"], 2 * (n - 1))
                    for c in range(2):
                        m = widths[c]
                        nc.scalar.activation(hr[n % 2][c][0:m, :], ps[0:m, 2 + c, :], ACT.Relu).then_inc(f2["relu"], 1)
                if n >= 1:
                    act.wait_ge(f2["down"], n)
                    if n >= 3:
                        act.wait_ge(f2["summed"], n - 2)
                    nc.scalar.copy(yb[(n - 1) % 2], ps[:, 4 + (n - 1) % 2, :]).then_inc(f2["rounded"], 1)

        def l2_ffn_dve(v):
            norm_dve(v, 8, 8, xT, hT, None)
            v.wait_ge(r2[1], 1)
            link(v, nc.vector.tensor_scalar(lg[:, :, 0:E2], lg[:, :, 0:E2], 1.0, None, ALU.add))
            link(v, nc.vector.reciprocal(lg[:, :, 0:E2], lg[:, :, 0:E2]))
            link(v, nc.vector.tensor_tensor(lg2[:, :, 0:E2], lg[:, :, 0:E2],
                                            ebias[:, :].unsqueeze(1).broadcast_to([P, NT, E2]), ALU.add))
            choose(v, lg2, E2, 2)
            link(v, nc.vector.tensor_tensor(comb[:, :, 0:E2], lg[:, :, 0:E2], oh[:, 2, :, 0:E2], ALU.mult))
            weights_dve(v)
            for i in range(2):
                for c in range(2):
                    m = widths[c]
                    v.wait_ge(f2["srelu"], 2 * i + c + 1)
                    nc.vector.tensor_tensor(sr[c][0:m, :], sr[c][0:m, :], sr[c][0:m, :], ALU.mult).then_inc(f2["ssq"], 1)

            def scale(n):
                v.wait_ge(f2["up"], n + 1)
                if n >= 2:
                    v.wait_ge(f2["sup"], 4 + n - 1)
                nc.vector.tensor_tensor(xin[n % 2], hT[:, half(n % 2)], ps[:, 6 + n % 2, :], ALU.mult).then_inc(f2["scale"], 1)

            scale(0)
            for n in range(n2):
                if n + 1 < n2:
                    scale(n + 1)
                if n >= 2:
                    v.wait_ge(f2["down"], n - 1)
                for c in range(2):
                    m = widths[c]
                    v.wait_ge(f2["relu"], 2 * n + c + 1)
                    nc.vector.tensor_tensor(hq[n % 2][c][0:m, :], hr[n % 2][c][0:m, :], hr[n % 2][c][0:m, :],
                                            ALU.mult).then_inc(f2["square"], 1)
            v.wait_ge(f2["summed"], n2)
            for i in range(2):
                residual(v, 5, i, ps[:, i, :], 5, None, None)

        a3 = {x: sem(f"A3_{x}") for x in ("proj", "q", "v", "v_done", "km", "spreadq", "rk", "rk_sb0", "rk_sb1", "split", "kept", "kept1", "kcut", "krest", "kdone",
                                          "kkept", "content", "rv", "rv_sb",
                                          "rt", "rn", "ro", "rf", "att", "o", "cleared")}
        rel = arena[:, :].rearrange("p (c h q) -> p c h q", c=2, h=B * H)
        QPART = (0, 1, 2, 0, 1, 0)
        SLOT_ROWS = HD * len(QPART)
        QH = P // 2
        qd = q_st[:, :, :].rearrange("p c s -> p (c s)").bitcast(BF16).rearrange("p (h b q) -> p h b q", h=H, b=B)
        qparts = mA[:, 4 * N:4 * N + 3 * N // 2].bitcast(BF16).rearrange("p (w k n) -> p w k n", w=2, k=3)
        q6 = mA[:, 4 * N:6 * N].bitcast(BF16).rearrange("p (h n) -> p h n", h=8)
        k6 = mA[:, 0:4 * N].bitcast(BF16).rearrange("p (h n) -> p h n", h=8)
        kparts = arena[:, 0:3 * N // 2].bitcast(BF16).rearrange("p (k n) -> p k n", k=3)
        relk32 = iota[:, 0:2 * S - 1]
        relk = iota[:, 1024:1024 + S].bitcast(BF16)[:, 0:2 * S - 1]
        relv = w1[:, 0:2 * S * HD].rearrange("p (c q d) -> p c q d", c=2, q=S)
        A3x = attention(HD, False, 2, 16, 0, 0, False)

        def score3(it, u, banks, nk):
            b, g = u // 4, u % 4
            r = slice(64 * (g // 2), 64 * (g // 2) + 64)
            for jp, o in enumerate(banks):
                for s in range(2):
                    h = 4 * g + 2 * jp + s
                    for c in range(2):
                        nc.tensor.transpose(o[:, s, tile(c)], rel[:, c, H * b + h, :], ident[:, :])
                        last = nc.tensor.matmul(o[:, s, tile(c)], q6[r, h % 8, tile(b)],
                                                k6[r, h % 8, S * b + P * c:S * b + P * c + P], start=False, stop=True,
                                                skip_group_check=True)
            return last

        def value3(it, u, c, j):
            h = 4 * (u % 4) + j
            return v_all[:, 2 * (u // 4) + c, h * HD:(h + 1) * HD]

        A3x.score, A3x.value, A3x.wo = score3, value3, lambda i: w3x[:, 4 + i, :]
        A3x.probT = lambda it, u, c, j: rel[:, c, 4 * u + j, :]
        A3x.moved_to = lambda it, u, c: rel[:, c, 4 * u:4 * u + 4, :]
        A3x.moved_from = lambda c: ps[:, 4 + c, :].rearrange("p (j q) -> p j q", j=4)
        A3x.output = lambda it, g: att[:, S * g + P * it:S * g + P * it + P]

        def rel_scores_pe(pe, it):
            pe.wait_ge(a3["spreadq"], 16 * 6 * (it + 1))
            pe.wait_ge(a3["split"], 3)
            for o in range(16):
                for c in range(2):
                    n = 32 * it + 2 * o + c
                    if n >= 8:
                        pe.wait_ge(a3[f"rk_sb{c}"], (n - 8) // 2 + 1)
                    for q8 in range(8):
                        q = 8 * o + q8
                        r = slice(64 * (q // QH), 64 * (q // QH) + SLOT_ROWS)
                        m = P * c - (P * it + q) + S - 1
                        mm = nc.tensor.matmul(ps[:, n % 8, q8:HALF:8], relk[r, m:m + P],
                                              qd[r, :, :, q % QH].rearrange("p h b -> p b h"), start=True, stop=True)
                    mm.then_inc(a3["rk"], 1)
            pe.wait_ge(a3["rk_sb0"], 16 * (it + 1))
            pe.wait_ge(a3["rk_sb1"], 16 * (it + 1))
            pe.wait_ge(a3["cleared"], it + 1)
            pe.wait_ge(a3["content"], 16 * (2 + 6 * (it + 1)))

        def rel_scores_move(eng, copy, it, c):
            eng.wait_ge(a3["kkept"], 16 * 3)
            for o in range(16):
                n = 32 * it + 2 * o + c
                eng.wait_ge(a3["rk"], n + 1)
                copy(rel[:, c, :, 8 * o:8 * o + 8],
                     ps[:, n % 8, :].rearrange("p (h q) -> p h q", q=8)).then_inc(a3[f"rk_sb{c}"], 1)

        def split_queries(v, w):
            src = q_all[:, :].rearrange("p (b w q) -> p w b q", b=B, w=2)[:, w, :, :]
            rest = a_sb[:, w, :].rearrange("p (b q) -> p b q", b=B)
            k0, k1, k2 = (qparts[:, w, k, :].rearrange("p (b q) -> p b q", b=B) for k in range(3))
            link(v, nc.vector.tensor_copy(k0, src))
            link(v, nc.vector.tensor_tensor(rest, src, k0, ALU.subtract))
            link(v, nc.vector.tensor_copy(k1, rest))
            nc.vector.tensor_tensor(k2, rest, k1, ALU.subtract).then_inc(a3["split"], 1)

        k_rest = prob[:, 0, :, :].rearrange("p j k -> p (j k)")

        def split_keys_dve(v):
            v.wait_ge(a3["kcut"], 1)
            nc.vector.tensor_tensor(k_rest, k_all[:, :], kparts[:, 0, :], ALU.subtract).then_inc(a3["krest"], 1)
            v.wait_ge(a3["kcut"], 2)
            nc.vector.tensor_tensor(kparts[:, 2, :], k_rest, kparts[:, 1, :], ALU.subtract).then_inc(a3["kdone"], 1)

        def split_keys_act(act):
            act.wait_ge(a3["km"], 2)
            nc.scalar.copy(kparts[:, 0, :], k_all[:, :]).then_inc(a3["kcut"], 1)
            act.wait_ge(a3["krest"], 1)
            nc.scalar.copy(kparts[:, 1, :], k_rest).then_inc(a3["kcut"], 1)

        def split_distances(v):
            n = 2 * S - 1
            k0, k1, k2 = (c_sb[:, 0, 256 * i:256 * i + 256].bitcast(BF16)[:, 0:n] if i < 2 else
                          c_sb[:, 1, 0:256].bitcast(BF16)[:, 0:n] for i in range(3))
            rest = d_sb[:, 0, 0:n]
            link(v, nc.vector.tensor_copy(k0, relk32))
            link(v, nc.vector.tensor_tensor(rest, relk32, k0, ALU.subtract))
            link(v, nc.vector.tensor_copy(k1, rest))
            link(v, nc.vector.tensor_tensor(k2, rest, k1, ALU.subtract))
            link(v, nc.vector.tensor_scalar(k0, k0, smask[:, 0:1], None, ALU.mult))
            link(v, nc.vector.scalar_tensor_tensor(k1, k1, smask[:, 1:2], k0, ALU.mult, ALU.add))
            nc.vector.scalar_tensor_tensor(relk, k2, smask[:, 2:3], k1, ALU.mult, ALU.add).then_inc(a3["split"], 1)

        def rel_values_pe(pe, it):
            until(pe, A3x.stored, 4 * (it + 1))
            for q in range(QH):
                for g in range(2):
                    for c in range(2):
                        mm = nc.tensor.matmul(ps[QH * g:QH * g + B * H, 0, HD * q:HD * q + HD], rel[:, c, :, QH * g + q],
                                              relv[:, c, P * it + QH * g + q, :], start=(c == 0), stop=(c == 1),
                                              skip_group_check=True)
            mm.then_inc(a3["rv"], 1)
            pe.wait_ge(a3["rv_sb"], it + 1)
            for d in range(HD):
                for g in range(2):
                    r = slice(QH * g, QH * g + QH)
                    mm = nc.tensor.matmul(ps[r, 2, 64 * d:64 * d + 64], rv_sb[r, d:HALF:HD], ident[r, r], start=True,
                                          stop=True, skip_group_check=True)
            mm.then_inc(a3["rt"], 1)
            pe.wait_ge(a3["rn"], it + 1)
            for b in range(B):
                mm = nc.tensor.transpose(ps[:, 3, tile(b)], rn_sb[:, tile(b)], ident[:, :])
            mm.then_inc(a3["ro"], 1)
            pe.wait_ge(a3["rf"], it + 1)
            nc.tensor.matmul(ps[:, 4, :], w3x[:, 3, :], rn_sb[:, :], start=True, stop=True).then_inc(a3["o"], 1)
            pe.wait_ge(a3["att"], it + 1)

        rv_sb = h1T
        rn_sb = sq[:, 0:HALF]

        def rel_values_dve(v, it):
            v.wait_ge(a3["rv"], it + 1)
            nc.vector.tensor_copy(rv_sb[:, 0:HALF], ps[:, 0, :]).then_inc(a3["rv_sb"], 1)
            v.wait_ge(a3["rt"], it + 1)
            until(v, A3x.inverted, 4 * (it + 1))
            for b in range(B):
                ins = nc.vector.tensor_tensor(
                    rn_sb[:, tile(b)].rearrange("p (h d) -> p h d", d=HD),
                    ps[:, 2, :].rearrange("p (d b h) -> p b h d", d=HD, b=B)[:, b, :, :],
                    rsum[:, b, :].unsqueeze(2).broadcast_to([P, H, HD]), ALU.mult)
            ins.then_inc(a3["rn"], 1)
            v.wait_ge(a3["ro"], it + 1)
            nc.vector.tensor_copy(rn_sb[:, :], ps[:, 3, :]).then_inc(a3["rf"], 1)
            v.wait_ge(a3["o"], it + 1)
            until(v, A3x.stored, 4 * (it + 1))
            o = att[:, :].rearrange("p (b s) -> p b s", b=B)[:, :, tile(it)]
            nc.vector.tensor_tensor(o, o, ps[:, 4, :].rearrange("p (b s) -> p b s", b=B), ALU.add).then_inc(a3["att"], 1)

        A3x.before_pe, A3x.after_pe = rel_scores_pe, rel_values_pe

        def before_dve3(v, it):
            rel_scores_move(v, nc.vector.tensor_copy, it, 0)
            v.wait_ge(a3["rk_sb0"], 16 * (it + 1))
            nc.vector.memset(ps[:, 6, :], 0.0).then_inc(a3["cleared"], 1)

        A3x.before_dve = before_dve3
        A3x.before_act = lambda act, it: rel_scores_move(act, nc.scalar.copy, it, 1)
        A3x.after_dve = rel_values_dve

        def l3_attn_pe(pe):
            norm_pe(pe, 9, 9, xT, x_ready(6))
            for w, src in enumerate((hT, ctxT)):
                for i in range(2):
                    if w == 0:
                        pe.wait_ge(n_out, 19 + i)
                    nc.tensor.matmul(ps[:, 2 * w + i, :], w3x[:, w, :], src[:, half(i)], start=True, stop=True).then_inc(a3["proj"], 1)
            pe.wait_ge(a3["q"], 2)
            for t in range(NT):
                mm = nc.tensor.matmul(ps[:, t // 4, tile(t % 4)], ctxT[:, tile(t)], w3x[:, 2, :], start=True, stop=True)
            mm.then_inc(a3["v"], 1)
            pe.wait_ge(a3["v_done"], 2)
            pe.wait_ge(a3["km"], 2)
            attn_pe(pe, A3x)

        def l3_attn_dve(v):
            norm_dve(v, 9, 9, xT, hT, None)
            for i in range(2):
                v.wait_ge(a3["proj"], 1 + i)
                nc.vector.tensor_scalar(q_all[:, half(i)], ps[:, i, :], col(C_BQ3), HD ** -0.5, ALU.add, ALU.mult).then_inc(a3["q"], 1)
            v.wait_ge(a3["q"], 2)
            split_queries(v, 0)
            for i in range(2):
                v.wait_ge(a3["proj"], 3 + i)
                nc.vector.tensor_scalar(k_all[:, half(i)], ps[:, 2 + i, :], col(C_BK3), None, ALU.add).then_inc(a3["km"], 1)
            split_queries(v, 1)
            values_dve(v, 2, a3["v"], a3["v_done"], H, HD)
            split_keys_dve(v)
            split_distances(v)
            attn_dve(v, A3x)
            v.wait_ge(a3["att"], 2)
            for i in range(2):
                residual(v, 6, i, att[:, half(i)], 6, col(C_BO3), a_sb[:, i, :])

        def l3_attn_act(act):
            norm_act(act, 9, 9, xT, None)
            split_keys_act(act)
            attn_act(act, A3x)

        def l3_attn_sp(sp):
            def relative(it):
                for g in range(2):
                    for s0, s1 in ((0, 3), (3, 5), (5, 6)):
                        rows = qscratch[it, 0:s1 - s0].rearrange("k (d h) (b g q) -> g (k d) (h b) q", d=HD, b=B, g=2)[g]
                        r = 64 * g + HD * s0
                        sp.dma_start(qd[r:r + HD * (s1 - s0), :, :, :].rearrange("p h b q -> p (h b) q"),
                                     rows).then_inc(a3["spreadq"], 16)

            def content(it):
                for g in range(2):
                    for s0, s1, _ in SLOT_PARTS:
                        rows = qscratch[it, 0:s1 - s0].rearrange("k (d g h) n -> g (k d) h n", d=HD, g=2)[g]
                        sp.dma_start(q6[64 * g + HD * s0:64 * g + HD * s1, :, :], rows).then_inc(a3["content"], 16)

            for w in range(2):
                sp.wait_ge(a3["split"], w + 1)
                sp.dma_start(qscratch[w].rearrange("k f n -> f k n"), qparts[:, w, :, :]).then_inc(a3[("kept", "kept1")[w]], 16)
            sp.wait_ge(a3["kept"], 16)
            relative(0)
            sp.wait_ge(a3["kdone"], 1)
            for s0, s1, k in SLOT_PARTS:
                sp.dma_start(kscratch[s0:s1].rearrange("s f n -> f s n"),
                             kparts[:, k:k + 1, :].broadcast_to([P, s1 - s0, N])).then_inc(a3["kkept"], 16)
            sp.wait_ge(a3["kkept"], 16 * 3)
            rows = kscratch.rearrange("s (d g h) n -> g (s d) h n", d=HD, g=2)
            for g in range(2):
                sp.dma_start(k6[64 * g:64 * g + 64, :, :], rows[g]).then_inc(a3["content"], 16)
            sp.wait_ge(a3["kept1"], 16)
            content(0)
            sp.wait_ge(a3["rk"], 32)
            relative(1)
            until(sp, A3x.scored, 16)
            content(1)

        w3f = w0[:, :, :].rearrange("p w n -> p (w n)")
        A3f = narrow(1, True, value_grouped, lambda i: w3f[:, 4 * D + 32 + i * D:5 * D + 32 + i * D])
        s3 = {x: sem(f"F3_{x}") for x in ("qk", "qk_done", "t", "v", "v_done", "x2")}
        r3 = [sem(f"R3_{x}") for x in ("logits", "shifted", "exped")]
        M3 = Mlp(28, 0, E3, 2, True)

        def l3_ffn_pe(pe):
            norm_pe(pe, 10, 10, xT, x_ready(7))
            norm_pe(pe, 11, None, h1T, None)
            pe.wait_ge(ld["w3"], 16)
            rope_pe(pe, w3f[:, 0:4 * D].rearrange("p (w n) -> p w n", w=4), 0, None, norm_ready(11), s3["qk"], True)
            pe.wait_ge(s3["qk_done"], 4)
            for t in range(NT):
                mm = nc.tensor.matmul(ps[:, t // 4, (t % 4) * P:(t % 4) * P + 32], hT[:, tile(t)], w3f[:, 4 * D:4 * D + 32],
                                      start=True, stop=True)
            mm.then_inc(s3["v"], 1)
            attn_pe(pe, A3f)
            norm_pe(pe, 12, None, h1T, None)
            logits_pe(pe, 12, E0 + E1 + E2, E3, r3[0])

            weights_pe(pe, 2)

            def first(pe):
                pe.wait_ge(ld["m3"], 16)
                weights_ready(pe, 2)
            mlp_pe(pe, M3, first)

        def l3_ffn_act(act):
            norm_act(act, 10, 10, xT, None)
            norm_act(act, 11, None, h1T, norm_ready(10))
            part_act(act, 1, s3["qk_done"])
            attn_act(act, A3f)
            norm_act(act, 12, None, h1T, lambda e, i: e.wait_ge(s3["x2"], i + 1))
            softmax_act(act, E3, r3[1], r3[2])
            weights_act(act, 2)
            mlp_act(act, M3)

        def l3_ffn_dve(v):
            norm_dve(v, 10, 10, xT, h1T, None)
            norm_dve(v, 11, None, h1T, hT, col(C_LN1))
            rope_dve(v, 1, s3["qk"], s3["qk_done"], [0.0, 0.0, 0.0, 0.0], s3["t"])
            v.wait_ge(s3["qk_done"], 4)
            values_dve(v, None, s3["v"], s3["v_done"], 4, HD)
            v.wait_ge(s3["v_done"], 2)
            clear_bank(v)
            attn_dve(v, A3f)
            for i in range(2):
                until(v, A3f.stored, 2 * B)
                nc.vector.tensor_tensor(h1T[:, half(i)], h1T[:, half(i)], att[:, half(i)], ALU.add).then_inc(s3["x2"], 1)
            norm_dve(v, 12, None, h1T, hT, col(C_LN2))
            softmax_dve(v, E3, r3[0], r3[1], r3[2])
            choose(v, lg, E3, 2)
            link(v, nc.vector.tensor_tensor(small[:, 3, :], top8[:, :, 0], top8[:, :, 1], ALU.add))
            link(v, nc.vector.reciprocal(small[:, 4, :], small[:, 3, :]))
            link(v, nc.vector.tensor_tensor(lg[:, :, 0:E3], lg[:, :, 0:E3],
                                            small[:, 4, :].unsqueeze(2).broadcast_to([P, NT, E3]), ALU.mult))
            link(v, nc.vector.tensor_tensor(comb[:, :, 0:E3], lg[:, :, 0:E3], oh[:, 2, :, 0:E3], ALU.mult))
            weights_dve(v)
            mlp_dve(v, M3)
            v.wait_ge(M3.downed, M3.counted + len(M3.units))
            for i in range(2):
                link(v, nc.vector.tensor_tensor(h1T[:, half(i)], h1T[:, half(i)], ps[:, i, :], ALU.add))
                residual(v, 7, i, h1T[:, half(i)], 7, None, None)

        progs["pe"] += [l2_attn_pe, l2_ffn_pe, l3_attn_pe, l3_ffn_pe]
        progs["dve"] += [l2_attn_dve, l2_ffn_dve, l3_attn_dve, l3_ffn_dve]
        progs["act"] += [l2_attn_act, l2_ffn_act, l3_attn_act, l3_ffn_act]

        block = ctx.enter_context(nc.Block())

        @block.sync
        def _(sp):
            def load(*groups):
                for group in groups:
                    for dst, src in loads[group]:
                        sp.dma_start(dst, src).then_inc(ld[group], 16)

            load("x", "c", "w0", "m0", "w1", "w2")
            part_sp(sp, 0)
            sp.wait_ge(x_done, 2)
            load("e1a")
            sp.wait_ge(x_done, 4)
            load("f2", "w3")
            sp.wait_ge(x_done, 6)
            load("e1b")
            sp.wait_ge(x_done, 8)
            load("r3")
            l3_attn_sp(sp)
            until(sp, A3x.scored, 32)
            load("m3")
            part_sp(sp, 1)
            for i in range(2):
                sp.wait_ge(x_done, 2 * SUBLAYERS - 1 + i)
                sp.dma_start(out[:, half(i)], xT[:, half(i)]).then_inc(ld["out"], 16)
            sp.wait_ge(ld["out"], 32)

        @block.gpsimd
        def _(pool):
            pool.wait_ge(ld["f2"], 32)
            nc.gpsimd.tensor_copy(up2[:, :, :].rearrange("p e n -> p (e n)"), mA[:, 0:E2 * HID2]).then_inc(narrowed, 1)
            nc.gpsimd.tensor_copy(dn2[:, :, :, :].rearrange("p e c n -> p (e c n)"),
                                  mA[:, E2 * HID2:E2 * HID2 + E2 * 2 * D]).then_inc(narrowed, 1)

        @block.tensor
        def _(pe):
            for f in progs["pe"]:
                f(pe)

        @block.vector
        def _(v):
            for f in progs["dve"]:
                f(v)

        @block.scalar
        def _(act):
            for f in progs["act"]:
                f(act)


_BY_DIM = [HD * (f % H) + f // H for f in range(D)]
_TURN = [8 * (e // 8) + (e % 8 + 4) % 8 for e in _BY_DIM]

_REL_ROWS = [int(np.clip(-(m - (S - 1)), -REL, REL)) + REL for m in range(2 * S - 1)]
_REL_IDS = np.clip(np.arange(S)[:, None] - np.arange(S)[None, :], -REL, REL).T.reshape(2, P, S) + REL


def constants():
    i = np.arange(P)
    inv = (1.0 / 10000.0 ** (np.arange(0, HD, 2, dtype=np.float32) / HD)).astype(np.float32)
    ang = np.arange(S, dtype=np.float32)[:, None] * inv[None, :]
    cos, sin = np.cos(ang), np.sin(ang)
    e = i // H
    c = cos[:, e % 4].T
    s = sin[:, e % 4].T * np.where(e < 4, -1.0, 1.0)[:, None]
    scale = HD ** -0.5
    return {
        "ident": np.eye(P),
        "meaner": np.full((P, P), 1.0 / P),
        "before": (i[:, None] < i[None, :]),
        "causal": np.where(i[:, None] >= i[None, :], 0.0, NEG),
        "rows3": (i[:, None] % EW == np.arange(EW)[None, :]),
        "smask": (np.array([0, 0, 0, 1, 1, 2, 3, 3])[i % 64 // HD][:, None] == np.arange(3)[None, :]),
        "rope": np.stack([c, s, c * scale, s * scale], 1),
        "iota": np.arange(SLOTS)[None],
        "slot_of": i[:, None] + CAP1 * np.arange(E1)[None, :],
    }


def kernel(**inputs):
    import concourse.bacc as _bacc
    from concourse.bass_utils import run_bass_kernel_spmd as _run

    w = {k: np.asarray(v) for k, v in inputs.items()}
    c = {k: np.ascontiguousarray(v, dtype=np.float32) for k, v in constants().items()}
    zero = np.zeros(D, np.float32)
    c["xT"] = w["x"].reshape(N, D).T
    c["ctxT"] = w["ctx_1024"].reshape(N, D).T
    c["gates"] = np.stack([w["g_xattn"], w["g_ffn"]], 1).reshape(1, 8)

    def quadrants(wo):
        parts = np.zeros((4, 4, 32, D), np.float32)
        parts[:, :, :HD] = wo.reshape(4, 4, HD, D)
        return list(parts.reshape(4, P, D))

    p = w["L0_xattn_Wq"], w["L0_xattn_Wk"]
    c["w0"] = np.stack([p[0][_BY_DIM].T, p[0][_TURN].T, p[1][_BY_DIM].T, p[1][_TURN].T, w["L0_xattn_Wv"].T]
                       + quadrants(w["L0_xattn_Wo"].T), 1)
    c["cols"] = np.stack([
        w["L0_xattn_bq"][_BY_DIM], w["L0_xattn_bq"][_TURN], w["L0_xattn_bk"][_BY_DIM], w["L0_xattn_bk"][_TURN], w["L0_xattn_bo"],
        w["L1_xattn_ptb_gamma"], w["L1_xattn_ca_gamma"], w["L1_xattn_ca_ctx_gamma"],
        w["L2_xattn_bq"], w["L2_xattn_bk"], w["L3_xattn_bq"][_BY_DIM], w["L3_xattn_bk"][_BY_DIM], w["L3_xattn_bo"],
        w["L3_ffn_ln1_w"], w["L3_ffn_ln2_w"]] + [zero] * 17, 1)
    c["bv"] = np.stack([w["L0_xattn_bv"], w["L2_xattn_bv"], w["L3_xattn_bv"]])[None]
    c["gw"] = np.concatenate([w["L0_ffn_gate_w"], w["L1_ffn_gate_w"], w["L2_ffn_gate_w"], w["L3_ffn_gate_w"]]).T
    c["ebias"] = w["L2_ffn_expert_bias"][None]

    c["consts"] = np.concatenate([c.pop(x).reshape(P, -1) for x in CONSTS], 1)
    c["masks"] = np.concatenate([c.pop("before"), c.pop("causal")], 1)

    def lhs(x):
        return x.transpose(2, 0, 1)

    m0 = [np.concatenate([w["L0_ffn_we_gate"], w["L0_ffn_ws_gate"].reshape(2, P, D)]),
          np.concatenate([w["L0_ffn_we_up"], w["L0_ffn_ws_up"].reshape(2, P, D)]),
          np.concatenate([w["L0_ffn_we_down"], w["L0_ffn_ws_down"].reshape(D, 2, P).transpose(1, 0, 2)])]
    c["m0"] = np.stack([lhs(m) for m in m0], 2).reshape(P, -1)
    fu, wq = w["L1_xattn_W_fused"], w["L1_xattn_W_q"]

    def attn1(q, kv, o):
        k, v = kv[:, :DH], kv[:, DH:]
        return [q, k, k, v, o.reshape(8, P, D).transpose(1, 0, 2).reshape(P, -1)]

    ff = fu[:, H * DH + 2 * DH:]
    c["w1"] = np.concatenate(
        attn1(fu[:, :H * DH], fu[:, H * DH:H * DH + 2 * DH], w["L1_xattn_W_attn_out"])
        + attn1(wq, w["L1_xattn_W_kv"], w["L1_xattn_W_out"]), 1)
    parts = [np.stack([ff[:, HALF + P * e:HALF + P * e + P], ff[:, P * e:P * e + P],
                       w["L1_xattn_W_ff_out"][P * e:P * e + P]], 1) for e in range(4)]
    c["m1"] = np.stack(parts, 1).reshape(P, -1)
    c["e1"] = np.concatenate([w["L1_ffn_w1"].transpose(1, 0, 2).reshape(P, -1),
                              w["L1_ffn_w2"].reshape(E1, 4, P, D).transpose(2, 0, 1, 3).reshape(P, -1)], 1)
    c["w2x"] = np.stack([w["L2_xattn_Wq"], w["L2_xattn_Wk"], w["L2_xattn_Wv"]], 1)
    c["up2"] = lhs(w["L2_ffn_w_up"])
    dn = np.zeros((E2, 2, P, D), np.float32)
    dn[:, 0] = w["L2_ffn_w_down"].transpose(0, 2, 1)[:, :P]
    dn[:, 1, :HID2B] = w["L2_ffn_w_down"].transpose(0, 2, 1)[:, P:]
    c["dn2"] = dn.transpose(2, 0, 1, 3)
    sd = np.zeros((2, P, D), np.float32)
    sd[0] = w["L2_ffn_shared_w_down"].T[:P]
    sd[1, :HID2B] = w["L2_ffn_shared_w_down"].T[P:]
    c["sh2"] = np.concatenate([w["L2_ffn_shared_w_up"].T, sd[0], sd[1]], 1)
    c["w3x"] = np.stack([w["L3_xattn_Wq"][:, _BY_DIM], w["L3_xattn_Wk"][:, _BY_DIM], w["L3_xattn_Wv"], w["L3_xattn_Wo"]]
                        + quadrants(w["L3_xattn_Wo"]), 1)


    c["relk"] = np.zeros((2, 64, 2 * S - 1), np.float32)
    c["relk"][:, :6 * HD] = np.tile(w["L3_xattn_rel_key_table"][_REL_ROWS].T, (6, 1))
    c["relk"] = c["relk"].reshape(P, -1)
    c["relv"] = w["L3_xattn_rel_value_table"][_REL_IDS].transpose(1, 0, 2, 3)
    f = w["L3_ffn_wqkv"]
    q, k, v = f[:D], f[D:D + 32], f[D + 32:]
    kx = k.reshape(4, 1, HD, D).repeat(4, 1).reshape(D, D)
    c["w3f"] = np.concatenate([q[_BY_DIM].T, q[_TURN].T, kx[_BY_DIM].T, kx[_TURN].T, v.T] + quadrants(w["L3_ffn_wo"].T), 1)
    w13, w2 = w["L3_ffn_w13"], w["L3_ffn_w2"]
    m3 = np.stack([np.stack([w13[:, P * j:P * j + P], w13[:, 256 + P * j:256 + P * j + P], w2[:, :, P * j:P * j + P]], 1)
                   for j in range(2)], 1)
    c["m3"] = m3.transpose(4, 0, 1, 2, 3).reshape(P, -1)

    nc = _bacc.Bacc("TRN2", target_bir_lowering=False, num_devices=1)
    arrays, args = {}, {}
    for name, x in c.items():
        x = np.ascontiguousarray(x)
        arrays[f"in_{name}"] = x
        args[name] = nc.dram_tensor(f"in_{name}", x.shape, mybir.dt.from_np(x.dtype), kind="ExternalInput").ap()
    out = nc.dram_tensor("out_0", (D, N), F32, kind="ExternalOutput").ap()
    qscratch = nc.dram_tensor("qscratch", (2, 3, D, HALF), BF16, kind="Internal").ap()
    kscratch = nc.dram_tensor("kscratch", (8, D, N), BF16, kind="Internal").ap()
    qkscratch = nc.dram_tensor("qkscratch", (2, 2, 2, 8, D, HALF), BF16, kind="Internal").ap()
    build(nc, args, out, qscratch, kscratch, qkscratch)
    r = _run(nc, [arrays], core_ids=[0])
    return np.ascontiguousarray(r.results[0]["out_0"].T).reshape(B, S, D)
```
